# Optimizing a Trainium2 kernel written in Bass

```python
import numpy as np
import jax
import jax.numpy as jnp

def _softmax(x, axis=-1):
    return jax.nn.softmax(x, axis=axis)

def _gelu(x):
    return jax.nn.gelu(x, approximate=True)

def _silu(x):
    return jax.nn.silu(x)

def _sigmoid(x):
    return jax.nn.sigmoid(x)

def _layernorm(x, axis=-1, eps=1e-05):
    m = jnp.mean(x, axis=axis, keepdims=True)
    v = jnp.var(x, axis=axis, keepdims=True)
    return (x - m) / jnp.sqrt(v + eps)

def _scatter_add(tgt, idx, src, axis=0):
    return tgt.at[idx].add(src)

def _segment_sum(src, seg, n):
    return jax.ops.segment_sum(src, seg, n)
kernel_name = 'mk_conv_preact_d4_conv_nchw32_r4_dac04b'

def setup_inputs(seed: int=0):
    np.random.seed(seed)
    _w = jnp.asarray

    def _rec_inputs():
        import jax
        import jax.numpy as jnp
        _gk = jax.random.key(seed)
        x = -0.000125 + 0.9999 * jax.random.normal(jax.random.fold_in(_gk, 1), (16, 32, 64, 64), jnp.float32)
        return x
    x = _rec_inputs()

    def _L0_conv_setup():
        import jax, jax.numpy as jnp
        import numpy as np
        from jax import lax
        STRIDE = (1, 1)
        PADDING = (1, 1)
        DILATION = (1, 1)
        GROUPS = 1
        key = jax.random.key(seed)
        k1, k2, k3 = jax.random.split(key, 3)
        x = jax.random.normal(k1, (16, 32, 64, 64), dtype=jnp.float32)
        weight = jax.random.normal(k2, (32, 32, 3, 3), dtype=jnp.float32)
        bias = jax.random.normal(k3, (32,), dtype=jnp.float32)
        return {'x': x, 'weight': weight, 'bias': bias}
    _L0_conv_all = _L0_conv_setup()
    _L0_conv_in = {k: v for k, v in _L0_conv_all.items() if k in ('weight', 'bias')}
    del _L0_conv_all

    def _L1_conv_setup():
        import jax, jax.numpy as jnp
        import numpy as np
        import math
        STATE_SIZE = 32

        def _cell(prev_col, cur_col, weight_ih, bias_ih, weight_hh, bias_hh):
            C = cur_col.shape[-1]
            pad = jnp.pad(prev_col, ((0, 0), (1, 1), (0, 0)))
            x = jnp.concatenate([pad[:, :-2], pad[:, 1:-1], pad[:, 2:]], axis=-1)
            i_vals = jnp.einsum('bhk,ok->bho', x, weight_ih) + bias_ih
            h_vals = jnp.einsum('bhc,oc->bho', cur_col, weight_hh) + bias_hh
            r_i, z_i, n_i = jnp.split(i_vals, 3, axis=-1)
            r_h, z_h, n_h = jnp.split(h_vals, 3, axis=-1)
            r = jax.nn.sigmoid(r_i + r_h)
            z = jax.nn.sigmoid(z_i + z_h)
            n = jnp.tanh(n_i + r * n_h)
            return n * z + cur_col * (1.0 - z)
        key = jax.random.key(seed)
        k1, k2, k3, k4, k5 = jax.random.split(key, 5)
        B, C, H, W = (8, STATE_SIZE, 128, 128)
        std = 1.0 / math.sqrt(C)
        states = jax.random.normal(k1, (B, C, H, W), dtype=jnp.float32)
        weight_ih = jax.random.uniform(k2, (3 * C, 3 * C), minval=-std, maxval=std, dtype=jnp.float32)
        bias_ih = jax.random.uniform(k3, (3 * C,), minval=-std, maxval=std, dtype=jnp.float32)
        weight_hh = jax.random.uniform(k4, (3 * C, C), minval=-std, maxval=std, dtype=jnp.float32)
        bias_hh = jax.random.uniform(k5, (3 * C,), minval=-std, maxval=std, dtype=jnp.float32)
        return {'states': states, 'weight_ih': weight_ih, 'bias_ih': bias_ih, 'weight_hh': weight_hh, 'bias_hh': bias_hh}
    _L1_conv_all = _L1_conv_setup()
    _L1_conv_in = {k: v for k, v in _L1_conv_all.items() if k in ('weight_ih', 'bias_ih', 'weight_hh', 'bias_hh')}
    del _L1_conv_all

    def _L2_conv_setup():
        import jax, jax.numpy as jnp
        import numpy as np
        IN_CH, OUT_CH = (32, 32)
        MODES1, MODES2 = (16, 16)
        SCALE = 1.0 / (IN_CH * OUT_CH)
        key = jax.random.key(seed)
        k1, k2, k3 = jax.random.split(key, 3)
        x = jax.random.normal(k1, (16, IN_CH, 64, 64), dtype=jnp.float32)
        w_real = SCALE * jax.random.uniform(k2, (IN_CH, OUT_CH, MODES1, MODES2), dtype=jnp.float32)
        w_imag = SCALE * jax.random.uniform(k3, (IN_CH, OUT_CH, MODES1, MODES2), dtype=jnp.float32)
        return {'x': x, 'w_real': w_real, 'w_imag': w_imag}
    _L2_conv_all = _L2_conv_setup()
    _L2_conv_in = {k: v for k, v in _L2_conv_all.items() if k in ('w_real', 'w_imag')}
    del _L2_conv_all

    def _L3_conv_setup():
        import jax, jax.numpy as jnp
        import numpy as np
        DIMS = (64, 64)
        key = jax.random.key(seed)
        k1, k2, k3, k4 = jax.random.split(key, 4)
        B, CIN, COUT = (8, 32, 32)
        H, W = DIMS
        WF = W // 2 + 1
        x = jax.random.normal(k1, (B, CIN, H, W), dtype=jnp.float32)
        kernel_re = jax.random.normal(k2, (COUT, CIN, H, WF), dtype=jnp.float32) * 0.05
        kernel_im = jax.random.normal(k3, (COUT, CIN, H, WF), dtype=jnp.float32) * 0.05
        bias = jax.random.normal(k4, (COUT, 1, 1), dtype=jnp.float32) * 0.01
        return {'x': x, 'kernel_re': kernel_re, 'kernel_im': kernel_im, 'bias': bias}
    _L3_conv_all = _L3_conv_setup()
    _L3_conv_in = {k: v for k, v in _L3_conv_all.items() if k in ('kernel_re', 'kernel_im', 'bias')}
    del _L3_conv_all
    return {'x': x, 'L0_conv_weight': _L0_conv_in['weight'], 'L0_conv_bias': _L0_conv_in['bias'], 'L1_conv_weight_ih': _L1_conv_in['weight_ih'], 'L1_conv_bias_ih': _L1_conv_in['bias_ih'], 'L1_conv_weight_hh': _L1_conv_in['weight_hh'], 'L1_conv_bias_hh': _L1_conv_in['bias_hh'], 'L2_conv_w_real': _L2_conv_in['w_real'], 'L2_conv_w_imag': _L2_conv_in['w_imag'], 'L3_conv_kernel_re': _L3_conv_in['kernel_re'], 'L3_conv_kernel_im': _L3_conv_in['kernel_im'], 'L3_conv_bias': _L3_conv_in['bias']}

def reference(x, L0_conv_weight, L0_conv_bias, L1_conv_weight_ih, L1_conv_bias_ih, L1_conv_weight_hh, L1_conv_bias_hh, L2_conv_w_real, L2_conv_w_imag, L3_conv_kernel_re, L3_conv_kernel_im, L3_conv_bias):
    import jax
    import jax.numpy as jnp

    def _L0_conv_ref(x, weight, bias):
        import jax, jax.numpy as jnp
        import numpy as np
        from jax import lax
        STRIDE = (1, 1)
        PADDING = (1, 1)
        DILATION = (1, 1)
        GROUPS = 1
        y = lax.conv_general_dilated(x, weight, window_strides=STRIDE, padding=[(PADDING[0], PADDING[0]), (PADDING[1], PADDING[1])], rhs_dilation=DILATION, dimension_numbers=('NCHW', 'OIHW', 'NCHW'), feature_group_count=GROUPS)
        return y + bias[None, :, None, None]

    def _L1_conv_ref(states, weight_ih, bias_ih, weight_hh, bias_hh):
        import jax, jax.numpy as jnp
        import numpy as np
        import math
        STATE_SIZE = 32

        def _cell(prev_col, cur_col, weight_ih, bias_ih, weight_hh, bias_hh):
            C = cur_col.shape[-1]
            pad = jnp.pad(prev_col, ((0, 0), (1, 1), (0, 0)))
            x = jnp.concatenate([pad[:, :-2], pad[:, 1:-1], pad[:, 2:]], axis=-1)
            i_vals = jnp.einsum('bhk,ok->bho', x, weight_ih) + bias_ih
            h_vals = jnp.einsum('bhc,oc->bho', cur_col, weight_hh) + bias_hh
            r_i, z_i, n_i = jnp.split(i_vals, 3, axis=-1)
            r_h, z_h, n_h = jnp.split(h_vals, 3, axis=-1)
            r = jax.nn.sigmoid(r_i + r_h)
            z = jax.nn.sigmoid(z_i + z_h)
            n = jnp.tanh(n_i + r * n_h)
            return n * z + cur_col * (1.0 - z)
        s = jnp.transpose(states, (3, 0, 2, 1))

        def step(carry, cur_col):
            new_col = _cell(carry, cur_col, weight_ih, bias_ih, weight_hh, bias_hh)
            return (new_col, new_col)
        col0 = s[0]
        _, cols = jax.lax.scan(step, col0, s[1:])
        out = jnp.concatenate([col0[None], cols], axis=0)
        return jnp.transpose(out, (1, 3, 2, 0))

    def _L2_conv_ref(x, w_real, w_imag):
        import jax, jax.numpy as jnp
        import numpy as np
        IN_CH, OUT_CH = (32, 32)
        MODES1, MODES2 = (16, 16)
        SCALE = 1.0 / (IN_CH * OUT_CH)
        B, Ci, H, W = x.shape
        Co, m1, m2 = (w_real.shape[1], w_real.shape[2], w_real.shape[3])
        weights = (w_real + 1j * w_imag).astype(jnp.complex64)
        x_hat = jnp.fft.rfft2(x)
        x_hat_m = x_hat[:, :, :m1, :m2]
        out_m = jnp.einsum('bikl,iokl->bokl', x_hat_m, weights)
        out_hat = jnp.zeros((B, Co, H, W // 2 + 1), dtype=jnp.complex64)
        out_hat = out_hat.at[:, :, :m1, :m2].set(out_m)
        return jnp.fft.irfft2(out_hat, s=(H, W))

    def _L3_conv_ref(x, kernel_re, kernel_im, bias):
        import jax, jax.numpy as jnp
        import numpy as np
        DIMS = (64, 64)
        kernel = kernel_re + 1j * kernel_im
        x_ = jnp.fft.rfftn(x, s=DIMS).astype(kernel.dtype)
        y_ = jnp.einsum('oihw,bihw->bohw', kernel, x_)
        y = jnp.fft.irfftn(y_, s=DIMS)
        return y + bias

    def _gn(v, G=16, eps=1e-05):
        B_, C_, H_, W_ = v.shape
        g = v.reshape(B_, G, C_ // G, H_, W_)
        m = jnp.mean(g, axis=(2, 3, 4), keepdims=True)
        s = jnp.var(g, axis=(2, 3, 4), keepdims=True)
        return ((g - m) / jnp.sqrt(s + eps)).reshape(v.shape)

    def _ln_c(v, eps=1e-06):
        m = jnp.mean(v, axis=1, keepdims=True)
        s = jnp.var(v, axis=1, keepdims=True)
        return (v - m) / jnp.sqrt(s + eps)

    def _ln_t(v, eps=1e-05):
        m = jnp.mean(v, axis=-1, keepdims=True)
        s = jnp.var(v, axis=-1, keepdims=True)
        return (v - m) / jnp.sqrt(s + eps)

    def _to_tokens(v):
        B_, C_, H_, W_ = v.shape
        return v.reshape(B_, C_, H_ * W_).transpose(0, 2, 1)

    def _from_tokens(t, like):
        B_, C_, H_, W_ = like.shape
        return t.transpose(0, 2, 1).reshape(B_, C_, H_, W_)
    x = x + _L0_conv_ref(_gn(x), L0_conv_weight, L0_conv_bias)
    x = x + _L1_conv_ref(_gn(x), L1_conv_weight_ih, L1_conv_bias_ih, L1_conv_weight_hh, L1_conv_bias_hh)
    x = x + _L2_conv_ref(_gn(x), L2_conv_w_real, L2_conv_w_imag)
    x = x + _L3_conv_ref(_gn(x), L3_conv_kernel_re, L3_conv_kernel_im, L3_conv_bias)
    return x

_drawn_inputs = setup_inputs


def setup_inputs(seed=0):
    import zlib

    import numpy as np

    out = dict(_drawn_inputs(seed))
    spreads = {}
    factors = {'L1_conv_weight_ih': 3.629,
     'L1_conv_bias_ih': 8.0,
     'L1_conv_weight_hh': 4.705,
     'L1_conv_bias_hh': 8.0,
     'L2_conv_w_real': 64.0,
     'L2_conv_w_imag': 64.0,
     'L3_conv_kernel_re': 3.511,
     'L3_conv_kernel_im': 3.521,
     'L3_conv_bias': 64.0}
    for name, (base, spread) in spreads.items():
        noise = np.random.default_rng([zlib.crc32(name.encode()), seed]).standard_normal(out[name].shape)
        drawn = base * np.exp(spread * noise) if base else spread * noise
        out[name] = jnp.asarray(drawn.astype(out[name].dtype))
    for name, factor in factors.items():
        out[name] = (out[name] * factor).astype(out[name].dtype)
    return out
```

```python
import numpy as np
import concourse.bass as bass
from concourse import mybir
from contextlib import ExitStack

F32 = mybir.dt.float32
ALU = mybir.AluOpType
ACT = mybir.ActivationFunctionType

B, C, H, W = 16, 32, 64, 64
HM = 4
H4 = H // HM
P = HM * C
ROWS = H4 * W
KW = W // 2
NYQ = W // 2 + 1
MODES = 16
GB = 4
NG = B // GB
TILE = 2 * HM * B
XT = 2 * B
CHUNK_T = 16
CHUNK = CHUNK_T * XT
NCHUNK = 2 * H * 4 // CHUNK_T
PLANES = 3 * HM * B
EPS = 1e-5


def constants():
    ang = 2 * np.pi * np.outer(np.arange(64), np.arange(64)) / 64
    cos, sin = np.cos(ang), np.sin(ang)
    cos[np.abs(cos) < 1e-12] = 0
    sin[np.abs(sin) < 1e-12] = 0
    two = np.eye(2)
    ident = np.eye(P)
    group = np.kron(np.ones((HM, HM)), np.kron(np.eye(C // 2), np.ones((2, 2)))) / (2 * HM)
    fw = np.zeros((2, W, 2, 2, NYQ))
    for b in range(2):
        fw[b, :, b, 0] = cos[:, :NYQ]
        fw[b, :, b, 1] = -sin[:, :NYQ]
    fhr = np.einsum("bd,rhk->bhdrk", two, np.stack([cos, -sin]))
    fhi = np.einsum("bd,rhk->bhdrk", two, np.stack([sin, cos]))
    ih = np.stack([np.stack([cos, sin], 1), np.stack([-sin, cos], 1)], 1).reshape(P, P)
    p = np.arange(KW)
    kw = 16 * (p // 16) + 4 * (p % 4) + (p // 4) % 4
    scale = np.where(kw == 0, 1.0, 2.0)[:, None] / (H * W)
    back_r = cos[kw] * scale
    back_i = -sin[kw] * scale
    back_i[0] = (-1.0) ** np.arange(W) / (H * W)
    iw = np.stack([np.kron(np.eye(4), back_r), np.kron(np.eye(4), back_i)], 1)
    parts = dict(ident=ident, fw=fw.reshape(P, -1), fhr=fhr.reshape(P, -1),
                 fhi=fhi.reshape(P, -1), ih=ih, iw=iw.reshape(P, -1))
    return group.astype(np.float32), {k: v.astype(np.float32) for k, v in parts.items()}


CONST_COLS = dict(ident=P, fw=4 * NYQ, fhr=4 * H, fhi=4 * H, ih=P, iw=8 * W)


def program(nc, x, conv_w, conv_b, scan_wi, scan_wh, scan_b, w2, w3, w9, out_b, group_d, const_d, out):
    ctx = ExitStack()
    with ctx:
        def sem(name):
            return ctx.enter_context(nc.semaphore(name))

        def sb(name, cols):
            return ctx.enter_context(nc.sbuf_tensor(name, [P, cols], F32))

        image = sb("image", B * ROWS)
        spec = sb("spec", 2 * H * 4 * XT)
        work = sb("work", B * ROWS + 128)
        ncol = sum(CONST_COLS.values())
        consts = sb("consts", ncol)
        conv_m = sb("conv_m", 5 * P)
        scan_m = sb("scan_m", 9 * P)
        group_m = sb("group_m", P)
        small = sb("small", 560)
        psum = ctx.enter_context(nc.psum_tensor("psum", [P, 8, 512], F32))

        cm, at = {}, 0
        for k, n in CONST_COLS.items():
            cm[k] = consts[:, at:at + n]
            at += n
        at = [0]

        def sm(n):
            at[0] += n
            return small[:, at[0] - n:at[0]]

        bn = sm(32 * 6)
        bn0, bn1 = bn[:, 0:48], bn[:, 48:96]
        mv0, gs0, mv1, gs1 = [bn[:, 96 + 8 * i:104 + 8 * i] for i in range(4)]
        carrier = bn[:, 152:153]
        sq0, var0, rstd_in0, sq1, var1, rstd_in1 = [bn[:, 128 + 4 * i:132 + 4 * i] for i in range(6)]
        mv = sm(32)
        gs = sm(32)
        sq = sm(16)
        mean, rstd, shift = sm(16), sm(16), sm(16)
        energy = sm(16)
        delta = sm(32)
        var, rstd_in = sm(16), sm(16)
        sc0, sh0, sc1, sh1 = sm(GB), sm(GB), sm(GB), sm(GB)
        bias_c, bias_o, eps_c = sm(1), sm(1), sm(1)
        bias_s = sm(6)
        bias_rz = sm(2)
        PADW = W + 2
        padded = [spec[:, i * H4 * PADW:(i + 1) * H4 * PADW] for i in range(2)]
        edges = [spec[:, (2 + i) * H4 * PADW:(3 + i) * H4 * PADW] for i in range(2)]
        HB = B * H4 // 2
        off = 4 * H4 * PADW

        def scan_buf():
            nonlocal off
            off += HB
            return spec[:, off - HB:off]

        state = [scan_buf() for _ in range(2)]
        sedge = [scan_buf() for _ in range(2)]
        gr, gz, gn, pre1, pre2, keep, mix = [[scan_buf() for _ in range(2)] for _ in range(7)]
        columns = work[:, 0:B * ROWS]
        stage = work[:, 0:4096]
        by_w = work[:, 4096:8192]
        by_h = work[:, 8192:8192 + C * 4 * NYQ]
        w2_m = work[:, 12416:16512]
        diag = [work[:, i * CHUNK_T * PLANES:(i + 1) * CHUNK_T * PLANES] for i in range(2)]
        w3_m = [work[:, 6144 + 1024 * i:7168 + 1024 * i] for i in range(4)]
        w9_m = work[:, 10240:11264]
        sq_before = work[:, 10240:12288]
        sq_after = work[:, 12416:14464]
        nyq_half = work[:, 11264:13312]
        t_sum = [work[:, 13312 + 1024 * i:14336 + 1024 * i] for i in range(3)]
        spec9 = conv_m[:, 0:16 * XT]
        ystage = work[:, 0:4096]
        by_kh = work[:, 4096:8192]
        by_kw = work[:, 8192:12288]

        x_first = [sem(f"x_first{u}") for u in range(GB)]
        x_in = [sem(f"x_in{j}") for j in range(NG)]
        conv_zeroed, scan_zeroed = sem("conv_zeroed"), sem("scan_zeroed")
        conv_w_in, scan_w_in, small_in, group_in, const_in = map(
            sem, ("conv_w_in", "scan_w_in", "small_in", "group_in", "const_in"))
        eps_set = sem("eps_set")
        pads_zeroed = sem("pads_zeroed")
        half0, half1 = sem("half0"), sem("half1")
        carried = sem("carried")
        stat0, stat1 = sem("stat0"), sem("stat1")
        sum0, sum1 = sem("sum0"), sem("sum1")
        dev0, dev1 = sem("dev0"), sem("dev1")
        padded_ready, edges_ready = sem("padded_ready"), sem("edges_ready")
        conv_done, conv_added = sem("conv_done"), sem("conv_added")
        columns_ready, last_columns = sem("columns_ready"), sem("last_columns")
        bias_ready = sem("bias_ready")
        state_ready = [sem(f"state_ready{h}") for h in range(2)]
        sedge_ready = [sem(f"sedge_ready{h}") for h in range(2)]
        r_sum, z_sum, n_sum = [[sem(f"{g}_sum{h}") for h in range(2)] for g in "rzn"]
        r_gate, z_gate, n_gate = [[sem(f"{g}_gate{h}") for h in range(2)] for g in "rzn"]
        reset_done = [sem(f"reset_done{h}") for h in range(2)]
        pre_ready = [sem(f"pre_ready{h}") for h in range(2)]
        keep_ready = [sem(f"keep_ready{h}") for h in range(2)]
        mix_ready = [sem(f"mix_ready{h}") for h in range(2)]
        added = [sem(f"added{h}") for h in range(2)]
        staged = [sem(f"staged{q}") for q in range(2)]
        t_done, t_act, t_dve = sem("t_done"), sem("t_act"), sem("t_dve")
        w_done, w_act, w_dve = sem("w_done"), sem("w_act"), sem("w_dve")
        h_done, h_act, h_dve = sem("h_done"), sem("h_act"), sem("h_dve")
        st2 = sem("st2")
        stat2, sum2, dev2 = sem("stat2"), sem("sum2"), sem("dev2")
        diag_zeroed = sem("diag_zeroed")
        w2_in = sem("w2_in")
        l2_pos, l2_neg, l2_done = sem("l2_pos"), sem("l2_neg"), sem("l2_done")
        sq1_done, sq2_done = sem("sq1_done"), sem("sq2_done")
        l2_added = sem("l2_added")
        stat3, sum3, dev3 = sem("stat3"), sem("sum3"), sem("dev3")
        w3_in = [sem(f"w3_in{i}") for i in range(4)]
        w9_in = sem("w9_in")
        pos_ready, neg_ready, mix_done, y_moved = map(sem, ("pos_ready", "neg_ready", "mix_done", "y_moved"))
        nyq_moved, sym = sem("nyq_moved"), sem("sym")
        ystaged = sem("ystaged")
        a_done, a_act, a_dve = sem("a_done"), sem("a_act"), sem("a_dve")
        b_done, b_act, b_dve = sem("b_done"), sem("b_act"), sem("b_dve")
        c_done, image_done = sem("c_done"), sem("image_done")
        stored = sem("stored")

        def steps_mean(n):
            return 1 + n + 2

        def steps_var(n):
            return steps_mean(n) + 3

        def steps_all(n):
            return steps_var(n) + 2

        KGN = steps_all(GB)
        EXTRA0 = steps_all(1) + steps_all(GB - 1) - KGN

        ds = bass.ds

        def images(j, n=GB):
            return image[:, ds(j * (GB * ROWS), n * ROWS)]

        def to_cols(op, j, u, cols, *func, **kw_):
            dst = columns.rearrange("p (w b h) -> p w b h", b=B, h=H4)[:, cols, ds(j * GB + u, 1), :] \
                .rearrange("p w o h -> p (o h) w")
            src = image[:, ds(j * (GB * ROWS) + u * ROWS, ROWS)].rearrange("p (h w) -> p h w", w=W)[:, :, cols]
            return op(dst, src, *func, **kw_)

        def to_stage(copy, j, q, *func):
            src = images(j)[:, q * 2 * ROWS:(q + 1) * 2 * ROWS].rearrange("p (b h w) -> p b h w", b=2, w=W)
            dst = stage[:, q * 2 * ROWS:(q + 1) * 2 * ROWS].rearrange("p (h b w) -> p b h w", b=2, w=W)
            return copy(dst, src, *func)

        def to_by_h(copy, n, *func):
            m = min(3, C - 3 * n)
            dst = by_h.rearrange("p (m c) -> p m c", c=C)[:, :, 3 * n:3 * n + m]
            src = psum[:, n % 8, 0:4 * NYQ * m].rearrange("p (c m) -> p m c", c=m)
            return copy(dst, src, *func)

        def to_spectrum(copy, j, n, *func):
            if n < 16:
                bp, g, t = n // 8, n % 8 // 4, n % 4
                src = psum[:, n % 8, 0:256].rearrange("p (q r k) -> p q r k", q=2, r=2)
                dst = spec[:, :].rearrange("p (g k t r j q b) -> p g k t r j q b", g=2, k=H, t=4, r=2, q=2, b=2)
                dst = dst[:, g, :, t, :, ds(j, 1), :, bp].rearrange("p k r o q -> p (o q) r k")
            else:
                bp = n - 16
                src = psum[:, bp, 0:64].rearrange("p (q r k) -> p q r k", q=2, r=2)
                dst = spec9.rearrange("p (k r j q b) -> p k r j q b", k=16, r=2, q=2, b=2)
                dst = dst[:, :, :, ds(j, 1), :, bp].rearrange("p k r o q -> p (o q) r k")
            return copy(dst, src, *func)

        def negative(activation, slot, m):
            d = diag[slot][C * m:C * m + C, :].rearrange("p (t k q b) -> p t k q b", k=3, q=HM, b=B)
            return activation(d[:, :, 0, m, :], d[:, :, 2, m, :], ACT.Copy, scale=-1.0)

        def to_kw(copy, n, *func):
            dst = by_kw.rearrange("p (m o) -> p m o", o=C)[:, :, 4 * n:4 * n + 4]
            return copy(dst, psum[:, n, :].rearrange("p (o m) -> p m o", o=4), *func)

        block = ctx.enter_context(nc.Block())

        @block.sync
        def _(sp):
            for u in range(GB):
                sp.dma_start(image[:, u * ROWS:(u + 1) * ROWS], x[:, u * ROWS:(u + 1) * ROWS]).then_inc(x_first[u], 16)
            sp.wait_ge(conv_w_in, 16 * 8)
            for j in range(1, NG):
                sp.dma_start(images(j), x[:, j * GB * ROWS:(j + 1) * GB * ROWS]).then_inc(x_in[j], 16)
            sp.wait_ge(scan_zeroed, 1)
            sv = scan_m[:, :].rearrange("p (k m) -> p k m", m=P)
            for hi in range(HM):
                lo, up = max(0, hi - 1), min(HM, hi + 2)
                sp.dma_start(sv[C * hi:C * hi + C, 0:3, C * lo:C * up],
                             scan_wi[:, :, C * (lo - hi + 1):C * (up - hi + 1)]).then_inc(scan_w_in, 16)
                sp.dma_start(sv[C * hi:C * hi + C, 6:9, C * hi:C * hi + C], scan_wh).then_inc(scan_w_in, 16)
            sp.dma_start(sv[0:C, 3:6, 0:C], scan_wi[:, :, 2 * C:3 * C]).then_inc(scan_w_in, 16)
            sp.dma_start(sv[C:2 * C, 3:6, P - C:P], scan_wi[:, :, 0:C]).then_inc(scan_w_in, 16)
            sp.dma_start(consts[:, :], const_d).then_inc(const_in, 16)
            sp.wait_ge(state_ready[0], W)
            sp.wait_ge(state_ready[1], W)
            sp.dma_start(w2_m, w2).then_inc(w2_in, 16)
            sp.wait_ge(h_done, 18 * NG)
            for i in range(4):
                sp.dma_start(w3_m[i], w3[:, i * 1024:(i + 1) * 1024]).then_inc(w3_in[i], 16)
            sp.wait_ge(stat3, 2)
            sp.dma_start(w9_m, w9).then_inc(w9_in, 16)
            with sp.Fori(1, NCHUNK // 4) as q:
                for i in range(4):
                    sp.wait_ge(mix_done, q * 4 + (i - 3))
                    sp.dma_start(w3_m[i], w3[:, ds(q * 4096 + i * 1024, 1024)]).then_inc(w3_in[i], 16)
            with sp.Fori(0, NG) as j:
                sp.wait_ge(image_done, j * 16 + 16)
                sp.dma_start(out[:, ds(j * (GB * ROWS), GB * ROWS)], images(j)).then_inc(stored, 16)
            sp.wait_ge(stored, 16 * NG)

        @block.gpsimd
        def _(pool):
            pool.dma_start(group_m[:, :], group_d).then_inc(group_in, 16)
            for hm in range(HM):
                q = slice(C * hm, C * hm + C)
                pool.dma_start(bias_c[q, :], conv_b).then_inc(small_in, 16)
                pool.dma_start(bias_o[q, :], out_b).then_inc(small_in, 16)
                pool.dma_start(bias_s[q, :], scan_b).then_inc(small_in, 16)
            nc.gpsimd.memset(scan_m[:, :], 0.0).then_inc(scan_zeroed, 1)
            with pool.Fori(0, W) as w:
                for h in range(2):
                    pool.wait_ge(state_ready[h], w + 1)
                    col = image[:, h * (B // 2 * ROWS):(h + 1) * (B // 2 * ROWS)] \
                        .rearrange("p (n w) -> p n w", w=W)[:, :, ds(w, 1)]
                    nc.gpsimd.tensor_tensor(col, col, state[h].unsqueeze(2), ALU.add).then_inc(added[h], 1)
            with pool.Fori(1, NG) as j:
                pool.wait_ge(t_done, j * 8)
                for q in range(2):
                    to_stage(nc.gpsimd.tensor_copy, j, q).then_inc(staged[q], 1)
            pool.wait_ge(w_done, 11 * NG)
            for i in range(2):
                nc.gpsimd.memset(diag[i], 0.0).then_inc(diag_zeroed, 1)
            with pool.Fori(1, NG) as j:
                pool.wait_ge(a_done, j * 8)
                nc.gpsimd.tensor_copy(ystage.rearrange("p (n b) -> p n b", b=GB),
                                      spec[:, :].rearrange("p (n b) -> p n b", b=B)[:, :, ds(j * GB, GB)]
                                      ).then_inc(ystaged, 1)

        @block.tensor
        def _(pe):
            mm = nc.tensor.matmul
            cv = conv_m[:, :].rearrange("p (k m) -> p k m", m=P)
            sv = scan_m[:, :].rearrange("p (k m) -> p k m", m=P)

            def sum0_of(lo, n, need):
                pe.wait_ge(stat0, need)
                mm(psum[:, 7, 2 * lo:2 * (lo + n)], group_m[:, :], mv0[:, 2 * lo:2 * (lo + n)],
                   start=True, stop=True).then_inc(sum0, 1)

            def sum1_of(lo, n, need):
                pe.wait_ge(stat1, need)
                mm(psum[:, 6, 2 * lo:2 * (lo + n)], group_m[:, :], mv1[:, 2 * lo:2 * (lo + n)],
                   start=True, stop=True).then_inc(sum1, 1)

            def conv_group(j, first, last):
                for u in range(GB):
                    if u == 1 and not first:
                        sum1_of(0, GB, (j - 1) * KGN + steps_mean(GB))
                    if u == 3 and not last:
                        sum0_of(0, GB, (j + 1) * KGN + (EXTRA0 + steps_mean(GB)))
                    xn = padded[u % 2].rearrange("p (h w) -> p h w", w=PADW)
                    en = edges[u % 2].rearrange("p (h w) -> p h w", w=PADW)
                    pe.wait_ge(padded_ready, j * GB + (u + 1))
                    for half in range(2):
                        n = 2 * u + half
                        if not (first and n < 4):
                            pe.wait_ge(conv_added, j * 8 + (n - 3))
                        for kx in range(3):
                            mm(psum[:, n % 4, :], cv[:, kx, :], xn[:, 8 * half:8 * half + 8, kx:kx + W],
                               start=kx == 0, stop=False)
                    if first and u == 0:
                        sum0_of(1, GB - 1, steps_all(1) + steps_mean(GB - 1))
                    pe.wait_ge(edges_ready, j * (4 * GB) + 4 * (u + 1))
                    for half in range(2):
                        n = 2 * u + half
                        mm(psum[:, n % 4, :], cv[:, 3, :], en[:, 8 * half:8 * half + 8, 0:W],
                           start=False, stop=False)
                        mm(psum[:, n % 4, :], cv[:, 4, :], en[:, 8 * half:8 * half + 8, 2:2 + W],
                           start=False, stop=True).then_inc(conv_done, 1)

            pe.wait_ge(group_in, 16)
            sum0_of(0, 1, steps_mean(1))
            pe.wait_ge(conv_w_in, 16 * 8)
            conv_group(0, True, False)
            with pe.Fori(1, NG - 1) as j:
                conv_group(j, False, False)
            conv_group(NG - 1, False, True)
            sum1_of(0, GB - 1, (NG - 1) * KGN + steps_mean(GB - 1))
            sum1_of(GB - 1, 1, (NG - 1) * KGN + steps_all(GB - 1) + steps_mean(1))

            def from_column(h, w):
                for g, bank in ((0, 0), (1, 1), (2, 3)):
                    mm(psum[:, 4 * h + bank, 0:HB], sv[:, 6 + g, :], columns[:, ds(w * (2 * HB) + h * HB, HB)],
                       start=True, stop=bank == 3)

            def banks_free(h, w):
                pe.wait_ge(r_gate[h], w - 1)
                pe.wait_ge(z_gate[h], w - 1)
                pe.wait_ge(reset_done[h], w - 1)

            def from_state(h, w):
                pe.wait_ge(state_ready[h], w)
                for g in (0, 2, 1):
                    mm(psum[:, 4 * h + g, 0:HB], sv[:, g, :], state[h], start=g == 2, stop=False)
                pe.wait_ge(sedge_ready[h], w * 2)
                for g, s in ((0, r_sum), (2, n_sum), (1, z_sum)):
                    mm(psum[:, 4 * h + g, 0:HB], sv[:, 3 + g, :], sedge[h], start=False, stop=True).then_inc(s[h], 1)

            pe.wait_ge(scan_w_in, 16 * 10)
            pe.wait_ge(columns_ready, B // 2)
            pe.wait_ge(conv_added, 2 * B)
            from_column(0, 1)
            from_state(0, 1)
            pe.wait_ge(columns_ready, B)
            pe.wait_ge(last_columns, 1)
            pe.wait_ge(stat1, (NG - 1) * KGN + steps_all(GB - 1) + steps_all(1))
            from_column(1, 1)
            from_state(1, 1)
            banks_free(0, 2)
            from_column(0, 2)
            with pe.Fori(2, W - 1) as w:
                from_state(0, w)
                banks_free(1, w)
                from_column(1, w)
                from_state(1, w)
                banks_free(0, w + 1)
                from_column(0, w + 1)
            from_state(0, W - 1)
            banks_free(1, W - 1)
            from_column(1, W - 1)
            from_state(1, W - 1)

            bw = by_w.rearrange("p (q h c) -> p q h c", q=2, c=C)
            bh = by_h.rearrange("p (b r k c) -> p b r k c", c=C, b=2, r=2)
            sg = stage.rearrange("p (q h b w) -> p q h b w", q=2, b=2, w=W)
            pe.wait_ge(const_in, 16)
            for h in range(2):
                pe.wait_ge(z_gate[h], W - 1)
                pe.wait_ge(pre_ready[h], W - 1)

            def forward(j, first):
                if not first:
                    pe.wait_ge(h_act, j * 9)
                    pe.wait_ge(h_dve, j * 9)
                for n in range(8):
                    if n % 4 == 0:
                        pe.wait_ge(staged[n // 4], j + 1)
                    for i in range(4):
                        h4 = 4 * (n % 4) + i
                        last = nc.tensor.transpose(psum[:, n, P * i:P * i + P], sg[:, n // 4, h4, :, :], cm["ident"])
                    last.then_inc(t_done, 1)
                pe.wait_ge(t_act, j * 4 + 4)
                pe.wait_ge(t_dve, j * 4 + 4)
                for n in range(11):
                    if n >= 8:
                        pe.wait_ge(*((w_act, j * 6 + (n - 8) // 2 + 1) if n % 2 == 0 else (w_dve, j * 5 + (n - 8) // 2 + 1)))
                    for i in range(min(3, C - 3 * n)):
                        last = mm(psum[:, n % 8, 132 * i:132 * i + 132], bw[:, :, :, 3 * n + i], cm["fw"],
                                  start=True, stop=True)
                    last.then_inc(w_done, 1)
                pe.wait_ge(w_act, j * 6 + 6)
                pe.wait_ge(w_dve, j * 5 + 5)
                for n in range(16):
                    bp, kwg = n // 8, n % 8
                    if n >= 8:
                        pe.wait_ge(*((h_act, j * 9 + (n - 8) // 2 + 1) if n % 2 == 0 else (h_dve, j * 9 + (n - 8) // 2 + 1)))
                    for ri, f in ((0, "fhr"), (1, "fhi")):
                        lhs = bh[:, bp, ri, 4 * kwg:4 * kwg + 4, :]
                        last = mm(psum[:, n % 8, 0:256], lhs, cm[f], start=ri == 0, stop=ri == 1)
                    last.then_inc(h_done, 1)
                for bp in range(2):
                    pe.wait_ge(*((h_act, j * 9 + 5) if bp == 0 else (h_dve, j * 9 + 5)))
                    rhs = cm["fhr"].rearrange("p (b r k) -> p b r k", b=2, r=2)
                    for q in range(4):
                        last = mm(psum[C * q:C * q + C, bp, 0:64], bh[:, bp, 0, KW, :],
                                  rhs[:, :, :, 16 * q:16 * q + 16], start=True, stop=True)
                    last.then_inc(h_done, 1)

            forward(0, True)
            with pe.Fori(1, NG) as j:
                forward(j, False)

            pe.wait_ge(h_act, 9 * NG)
            pe.wait_ge(h_dve, 9 * NG)
            pe.wait_ge(stat2, B + 2)
            mm(psum[:, 7, 0:2 * B], group_m[:, :], mv, start=True, stop=True).then_inc(sum2, 1)

            def tiles(weights, planes, bank, done, nyquist=False, starts=True):
                wt = weights.rearrange("p (t r o) -> p t r o", r=2, o=C)
                pl = planes.rearrange("p (t m) -> p t m", m=PLANES)
                for t in range(CHUNK_T):
                    k, q = (t % 4, 0) if nyquist else (t // 4, t % 4)
                    o = psum[C * q:C * q + C, bank + (t // 4 if nyquist else 0), TILE * k:TILE * k + TILE]
                    mm(o, wt[:, t, 0, :], pl[:, t, 64:192], start=starts and k == 0, stop=False,
                       skip_group_check=True)
                    last = mm(o, wt[:, t, 1, :], pl[:, t, 0:128], start=False, stop=True, skip_group_check=True)
                last.then_inc(done, 1)

            pe.wait_ge(w2_in, 16)
            for c in range(4):
                pe.wait_ge(l2_pos, 4 * (c + 1))
                pe.wait_ge(l2_neg, 4 * (c + 1))
                tiles(w2_m[:, 1024 * c:1024 * c + 1024], diag[c % 2], c, l2_done)
            pe.wait_ge(stat3, 3)
            mm(psum[:, 7, 0:2 * B], group_m[:, :], delta, start=True, stop=True).then_inc(sum3, 1)

            def mix_four(q, first):
                for i in range(4):
                    pe.wait_ge(w3_in[i], q * 16 + 16)
                    pe.wait_ge(pos_ready, q * 16 + 4 * (i + 1))
                    pe.wait_ge(neg_ready, q * 16 + 4 * (i + 1))
                    if not first:
                        pe.wait_ge(y_moved, q * 4 + (i - 3))
                    tiles(w3_m[i], diag[i % 2], i, mix_done, starts=not first)

            mix_four(0, True)
            with pe.Fori(1, NCHUNK // 4) as q:
                mix_four(q, False)
            pe.wait_ge(w9_in, 16)
            pe.wait_ge(pos_ready, 4 * (NCHUNK + 1))
            pe.wait_ge(neg_ready, 4 * (NCHUNK + 1))
            tiles(w9_m, diag[0], 4, mix_done, nyquist=True)

            ys = ystage.rearrange("p (g k r q b) -> p g k r q b", g=2, k=H, r=2, q=4)
            kh = by_kh.rearrange("p (b k o) -> p b k o", b=GB, k=KW)
            kwv = by_kw.rearrange("p (r h m) -> p r h m", r=2, m=P)

            def back(j, first):
                pe.wait_ge(ystaged, j + (2 if first else 2))
                if first:
                    pe.wait_ge(y_moved, NCHUNK)
                    pe.wait_ge(nyq_moved, 2)
                else:
                    pe.wait_ge(image_done, j * 16)
                for n in range(8):
                    b, g = n // 2, n % 2
                    for i in range(4):
                        last = nc.tensor.transpose(psum[:, n, P * i:P * i + P], ys[:, g, :, :, i, b], cm["ident"])
                    last.then_inc(a_done, 1)
                pe.wait_ge(a_act, j * 4 + 4)
                pe.wait_ge(a_dve, j * 4 + 4)
                for n in range(8):
                    for i in range(4):
                        last = mm(psum[:, n, P * i:P * i + P], kh[:, :, :, 4 * n + i], cm["ih"],
                                  start=True, stop=True)
                    last.then_inc(b_done, 1)
                pe.wait_ge(b_act, j * 4 + 4)
                pe.wait_ge(b_dve, j * 4 + 4)
                iw = cm["iw"].rearrange("p (r n) -> p r n", r=2)
                for n in range(8):
                    for i in range(2):
                        for ri in range(2):
                            last = mm(psum[:, n, 256 * i:256 * i + 256], kwv[:, ri, 2 * n + i, :], iw[:, ri, :],
                                      start=ri == 0, stop=ri == 1)
                    last.then_inc(c_done, 1)

            back(0, True)
            with pe.Fori(1, NG) as j:
                back(j, False)

        @block.scalar
        def _(act):
            a = nc.scalar.activation

            def deviation(d, v_, lo, n, stat_sem, need, dev_sem):
                act.wait_ge(stat_sem, need)
                a(d[:, lo:lo + n], v_[:, lo:lo + n], ACT.Sqrt, bias=eps_c).then_inc(dev_sem, 1)

            def edge_rows(j, u):
                act.wait_ge(padded_ready, j * GB + (u + 1))
                xn = padded[u % 2].rearrange("p (h w) -> p h w", w=PADW)
                en = edges[u % 2].rearrange("p (h w) -> p h w", w=PADW)
                a(en[0:C, 1:H4, :], xn[P - C:P, 0:H4 - 1, :], ACT.Copy).then_inc(edges_ready, 1)
                a(en[C:2 * C, 0:H4 - 1, :], xn[0:C, 1:H4, :], ACT.Copy).then_inc(edges_ready, 1)
                a(en[2 * C:3 * C, 1:H4, 0:PADW - 1], xn[P - C:P, 0:H4 - 1, 1:PADW], ACT.Copy).then_inc(edges_ready, 1)
                a(en[3 * C:4 * C, 0:H4 - 1, 0:PADW - 1], xn[0:C, 1:H4, 1:PADW], ACT.Copy).then_inc(edges_ready, 1)

            def to_columns(j, images_):
                for u in images_:
                    to_cols(a, j, u, slice(0, W), ACT.Identity, scale=sc1[:, u:u + 1],
                            bias=sh1[:, u:u + 1]).then_inc(columns_ready, 1)

            def conv_group(j, first, last):
                for u in range(GB):
                    if u < GB - 1:
                        edge_rows(j, u + 1)
                    elif not last:
                        deviation(rstd_in0, var0, 0, GB, stat0, (j + 1) * KGN + (EXTRA0 + steps_var(GB)), dev0)
                        edge_rows(j + 1, 0)
                    if u == 1 and not first:
                        deviation(rstd_in1, var1, 0, GB, stat1, (j - 1) * KGN + steps_var(GB), dev1)
                    if u >= 2 and not first:
                        act.wait_ge(stat1, (j - 1) * KGN + KGN)
                        to_columns(j - 1, (2 * u - 4, 2 * u - 3))

            act.wait_ge(conv_zeroed, 1)
            cv = conv_m[:, :].rearrange("p (k m) -> p k m", m=P)
            for hi in range(HM):
                lo, up = max(0, hi - 1), min(HM, hi + 2)
                act.dma_start(cv[C * hi:C * hi + C, 0:3, C * lo:C * up],
                              conv_w[:, :, C * (lo - hi + 1):C * (up - hi + 1)]).then_inc(conv_w_in, 16)
            for quad in range(4):
                taps, rows_ = slice(0, C), slice(P - C, P)
                if quad % 2 == 0:
                    taps, rows_ = slice(2 * C, 3 * C), slice(0, C)
                kx = slice(0, 3, 2) if quad < 2 else slice(1, 2)
                act.dma_start(cv[C * quad:C * quad + C, slice(3, 5 if quad < 2 else 4), rows_],
                              conv_w[:, kx, taps]).then_inc(conv_w_in, 16)
            act.wait_ge(eps_set, 1)
            deviation(rstd_in0, var0, 0, 1, stat0, steps_var(1), dev0)
            edge_rows(0, 0)
            deviation(rstd_in0, var0, 1, GB - 1, stat0, steps_all(1) + steps_var(GB - 1), dev0)
            conv_group(0, True, False)
            with act.Fori(1, NG - 1) as j:
                conv_group(j, False, False)
            conv_group(NG - 1, False, True)
            before = (NG - 1) * KGN
            deviation(rstd_in1, var1, 0, GB - 1, stat1, before + steps_var(GB - 1), dev1)
            act.wait_ge(stat1, before + steps_all(GB - 1))
            to_columns(NG - 1, (0, 1))
            before += steps_all(GB - 1)
            deviation(rstd_in1, var1, GB - 1, 1, stat1, before + steps_var(1), dev1)
            to_columns(NG - 1, (2,))
            act.wait_ge(stat1, before + steps_all(1))
            to_cols(a, NG - 1, GB - 1, slice(0, W // 2), ACT.Identity, scale=sc1[:, GB - 1:GB],
                    bias=sh1[:, GB - 1:GB]).then_inc(columns_ready, 1)

            def state_edges(h, w):
                act.wait_ge(state_ready[h], w + 1)
                s = state[h].rearrange("p (b h) -> p b h", h=H4)
                e = sedge[h].rearrange("p (b h) -> p b h", h=H4)
                a(e[0:C, :, 1:H4], s[P - C:P, :, 0:H4 - 1], ACT.Copy).then_inc(sedge_ready[h], 1)
                a(e[C:2 * C, :, 0:H4 - 1], s[0:C, :, 1:H4], ACT.Copy).then_inc(sedge_ready[h], 1)

            def gates(h, w):
                act.wait_ge(r_sum[h], w)
                a(gr[h], psum[:, 4 * h, 0:HB], ACT.Sigmoid, bias=bias_rz[:, 0:1]).then_inc(r_gate[h], 1)
                act.wait_ge(z_sum[h], w)
                a(gz[h], psum[:, 4 * h + 1, 0:HB], ACT.Sigmoid, bias=bias_rz[:, 1:2]).then_inc(z_gate[h], 1)

            def candidate(h, w):
                act.wait_ge(pre_ready[h], w)
                a(gn[h], pre2[h], ACT.Tanh, bias=bias_s[:, 2:3]).then_inc(n_gate[h], 1)

            act.wait_ge(bias_ready, 1)

            def scan_step(w):
                gates(0, w)
                state_edges(1, w - 1)
                candidate(0, w)
                gates(1, w)
                state_edges(0, w)
                candidate(1, w)

            state_edges(0, 0)
            scan_step(1)
            with act.Fori(2, W) as w:
                scan_step(w)

            act.wait_ge(added[0], W)
            to_stage(a, 0, 1, ACT.Copy).then_inc(staged[1], 1)
            act.wait_ge(added[1], W)
            sp6 = spec[:, :].rearrange("p (g k t r b) -> p g k t r b", g=2, k=H, t=4, r=2)
            s9 = spec9.rearrange("p (k r b) -> p k r b", r=2, b=B)

            def forward(j):
                for n in range(0, 8, 2):
                    act.wait_ge(t_done, j * 8 + (n + 1))
                    a(by_w[:, 512 * n:512 * n + 512], psum[:, n, :], ACT.Copy).then_inc(t_act, 1)
                for n in range(0, 11, 2):
                    act.wait_ge(w_done, j * 11 + (n + 1))
                    to_by_h(a, n, ACT.Copy).then_inc(w_act, 1)
                for n in range(0, 17, 2):
                    act.wait_ge(h_done, j * 18 + (n + 1))
                    to_spectrum(a, j, n, ACT.Copy).then_inc(h_act, 1)

            with act.Fori(0, NG) as j:
                forward(j)

            act.wait_ge(stat2, B + 5)
            a(rstd_in[:, 0:B], var[:, 0:B], ACT.Sqrt, bias=eps_c).then_inc(dev2, 1)
            act.wait_ge(h_dve, 9 * NG)
            act.wait_ge(stat2, B + 8)
            for c in range(4):
                act.wait_ge(l2_pos, 4 * (c + 1))
                if c >= 2:
                    act.wait_ge(l2_done, c - 1)
                for m in range(HM):
                    negative(a, c % 2, m).then_inc(l2_neg, 1)
            a(sq_before, spec[:, 0:2048], ACT.Square).then_inc(sq1_done, 1)
            act.wait_ge(l2_added, 24)
            act.wait_ge(l2_done, 4)
            a(sq_after, spec[:, 0:2048], ACT.Square).then_inc(sq2_done, 1)
            act.wait_ge(stat3, 7)
            a(rstd_in[:, 0:B], var[:, 0:B], ACT.Sqrt, bias=eps_c).then_inc(dev3, 1)

            def move_y(q, i):
                act.wait_ge(mix_done, q * 4 + (i + 1))
                a(spec[:, ds(q * 2048 + i * CHUNK, CHUNK)], psum[:, i, :], ACT.Copy).then_inc(y_moved, 1)

            def full(q, first):
                for i in range(4):
                    act.wait_ge(pos_ready, q * 16 + 4 * (i + 1))
                    for m in range(HM):
                        negative(a, i % 2, m).then_inc(neg_ready, 1)
                    if i == 0 and not first:
                        move_y(q - 1, 3)
                    if i > 0:
                        move_y(q, i - 1)

            full(0, True)
            with act.Fori(1, NCHUNK // 4) as q:
                full(q, False)
            act.wait_ge(pos_ready, 4 * (NCHUNK + 1))
            for m in range(HM):
                negative(a, 0, m).then_inc(neg_ready, 1)
            move_y(NCHUNK // 4 - 1, 3)
            act.wait_ge(mix_done, NCHUNK + 1)
            src = psum[0:C, 4:8, :].rearrange("p n (k r m) -> p (n k) r m", k=4, r=2)
            nyq = nyq_half[0:C, :].rearrange("p (r q k b) -> p r q k b", r=2, q=4, b=B)
            for ri in range(2):
                a(nyq[:, ri].rearrange("p q k b -> p k q b"),
                  src[:, :, ri, :].rearrange("p k (q b) -> p k q b", b=B), ACT.Copy, scale=0.5).then_inc(nyq_moved, 1)
            act.wait_ge(sym, 8)
            yv = ystage.rearrange("p (n b) -> p n b", b=GB)
            sv_ = spec[:, :].rearrange("p (n b) -> p n b", b=B)
            a(yv[:, 0:512, :], sv_[:, 0:512, 0:GB], ACT.Copy).then_inc(ystaged, 1)

            def back(j):
                for n in range(0, 8, 2):
                    act.wait_ge(a_done, j * 8 + (n + 1))
                    a(by_kh[:, 512 * n:512 * n + 512], psum[:, n, :], ACT.Copy).then_inc(a_act, 1)
                for n in range(0, 8, 2):
                    act.wait_ge(b_done, j * 8 + (n + 1))
                    to_kw(a, n, ACT.Copy).then_inc(b_act, 1)

            with act.Fori(0, NG) as j:
                back(j)

        @block.vector
        def _(dve):
            v = nc.vector

            def chain(norm, lo, n, base):
                half_sem, stat_sem, sum_sem, dev_sem, bnv, mv_, gs_, sq_, var_, dev_in, bank, scale, shifted = norm
                cols = slice(lo, lo + n)
                m = mv_.rearrange("p (u k) -> p u k", k=2)[:, cols]
                g = gs_.rearrange("p (u k) -> p u k", k=2)[:, cols]
                q = sq_[:, cols]
                count = [0]

                def step(ins):
                    count[0] += 1
                    ins.then_inc(stat_sem, 1)

                def settle():
                    dve.wait_ge(stat_sem, base + count[0])

                def to_mean(halves):
                    dve.wait_ge(half_sem, halves)
                    step(v.memset(q, 0.0))
                    for u in range(lo, lo + n):
                        step(v.bn_aggr(mv_[:, 2 * u:2 * u + 2], bnv[:, 12 * u:12 * u + 12]))
                    settle()
                    step(v.tensor_tensor(q, m[:, :, 0], m[:, :, 0], ALU.mult))
                    settle()
                    step(v.tensor_tensor(m[:, :, 1], m[:, :, 1], q, ALU.add))
                    assert count[0] == steps_mean(n)

                def to_var(sums):
                    dve.wait_ge(sum_sem, sums)
                    step(v.tensor_copy(gs_[:, 2 * lo:2 * (lo + n)], psum[:, bank, 2 * lo:2 * (lo + n)]))
                    settle()
                    step(v.tensor_tensor(q, g[:, :, 0], g[:, :, 0], ALU.mult))
                    settle()
                    step(v.tensor_tensor(var_[:, cols], g[:, :, 1], q, ALU.subtract))
                    assert count[0] == steps_var(n)

                def to_scale(devs):
                    dve.wait_ge(dev_sem, devs)
                    step(v.reciprocal(scale[:, cols], dev_in[:, cols]))
                    settle()
                    step(v.scalar_tensor_tensor(out=shifted[:, cols], in0=g[:, :, 0], scalar=-1.0, in1=scale[:, cols],
                                                op0=ALU.mult, op1=ALU.mult))
                    settle()
                    assert count[0] == steps_all(n)

                return to_mean, to_var, to_scale

            norm0 = (half0, stat0, sum0, dev0, bn0, mv0, gs0, sq0, var0, rstd_in0, 7, sc0, sh0)
            norm1 = (half1, stat1, sum1, dev1, bn1, mv1, gs1, sq1, var1, rstd_in1, 6, sc1, sh1)

            def half_stats(bnv, half_sem, j, u):
                for k in (2 * u, 2 * u + 1):
                    at_ = 6 * (k % 8)
                    v.bn_stats(bnv[:, at_:at_ + 6],
                               image[:, ds(j * (GB * ROWS) + 512 * k, 512)]).then_inc(half_sem, 1)

            def normalise(j, u, first):
                if not (first and u < 2):
                    dve.wait_ge(conv_done, j * 8 + 2 * (u - 1))
                xn = padded[u % 2].rearrange("p (h w) -> p h w", w=PADW)
                v.tensor_scalar(xn[:, :, 1:1 + W],
                                image[:, ds(j * (GB * ROWS) + u * ROWS, ROWS)].rearrange("p (h w) -> p h w", w=W),
                                sc0[:, u:u + 1], sh0[:, u:u + 1], ALU.mult, ALU.add).then_inc(padded_ready, 1)

            def add_conv(j, u):
                for half in range(2):
                    dve.wait_ge(conv_done, j * 8 + (2 * u + half + 1))
                    part = image[:, ds(j * (GB * ROWS) + (2 * u + half) * 512, 512)]
                    v.scalar_tensor_tensor(out=part, in0=psum[:, (2 * u + half) % 4, :], scalar=bias_c[:, 0:1],
                                           in1=part, op0=ALU.add, op1=ALU.add).then_inc(conv_added, 1)

            def conv_group(j, first, last):
                before1 = chain(norm1, 0, GB, (j - 1) * KGN) if not first else None
                next0 = chain(norm0, 0, GB, (j + 1) * KGN + EXTRA0) if not last else None
                for u in range(GB):
                    if u < GB - 1:
                        normalise(j, u + 1, first)
                    elif not last:
                        next0[1](j + 3)
                    if u == 1 and not first:
                        before1[1](j)
                    if not (first and u == 0):
                        add_conv(j, u - 1)
                        if not (first and u == 1):
                            dve.wait_ge(carried, j * GB + (u - 1))
                        dve.wait_ge(conv_added, j * 8 + 2 * u)
                        v.memset(carrier, 0.0).then_inc(carried, 1)
                        half_stats(bn1, half1, *((j - 1, GB - 1) if u == 0 else (j, u - 1)))
                    if u < GB - 1 and not last:
                        for i in ((0,), (1, 2), (3,))[u]:
                            half_stats(bn0, half0, j + 1, i)
                    if u == 0 and not first:
                        before1[0](j * 8)
                    if u == 1 and not first:
                        if not last:
                            dve.wait_ge(columns_ready, j * GB - GB)
                        else:
                            dve.wait_ge(columns_ready, (NG - 2) * GB)
                        before1[2](j)
                    if u == 2 and not last:
                        next0[0](j * 8 + 16)
                    if u == GB - 1 and not last:
                        next0[2](j + 3)
                        normalise(j + 1, 0, False)

            v.memset(conv_m[:, :], 0.0).then_inc(conv_zeroed, 1)
            v.memset(eps_c, EPS).then_inc(eps_set, 1)
            for i in range(2):
                xn = padded[i].rearrange("p (h w) -> p h w", w=PADW)
                v.memset(xn[:, :, 0:1], 0.0).then_inc(pads_zeroed, 1)
                v.memset(xn[:, :, PADW - 1:PADW], 0.0).then_inc(pads_zeroed, 1)
                v.memset(edges[i], 0.0).then_inc(pads_zeroed, 1)
                v.memset(sedge[i], 0.0).then_inc(pads_zeroed, 1)
            dve.wait_ge(x_first[0], 16)
            half_stats(bn0, half0, 0, 0)
            one, rest = chain(norm0, 0, 1, 0), chain(norm0, 1, GB - 1, steps_all(1))
            one[0](2)
            dve.wait_ge(x_first[1], 16)
            half_stats(bn0, half0, 0, 1)
            one[1](1)
            dve.wait_ge(pads_zeroed, 8)
            one[2](1)
            normalise(0, 0, True)
            for u in range(2, GB):
                dve.wait_ge(x_first[u], 16)
                half_stats(bn0, half0, 0, u)
            rest[0](8)
            rest[1](2)
            rest[2](2)
            dve.wait_ge(small_in, 16 * 12)
            v.tensor_tensor(bias_rz, bias_s[:, 0:2], bias_s[:, 3:5], ALU.add).then_inc(bias_ready, 1)
            dve.wait_ge(x_in[1], 16)
            conv_group(0, True, False)
            for j in range(2, NG):
                dve.wait_ge(x_in[j], 16)
            with dve.Fori(1, NG - 1) as j:
                conv_group(j, False, False)
            conv_group(NG - 1, False, True)
            three, one = chain(norm1, 0, GB - 1, (NG - 1) * KGN), chain(norm1, GB - 1, 1, (NG - 1) * KGN + steps_all(GB - 1))
            three[0](8 * NG - 2)
            add_conv(NG - 1, GB - 1)
            dve.wait_ge(conv_added, 2 * B)
            half_stats(bn1, half1, NG - 1, GB - 1)
            three[1](NG)
            dve.wait_ge(columns_ready, B - GB)
            three[2](NG)
            one[0](8 * NG)
            one[1](NG + 1)
            one[2](NG + 1)
            to_cols(v.tensor_scalar, NG - 1, GB - 1, slice(W // 2, W), sc1[:, GB - 1:GB], sh1[:, GB - 1:GB],
                    ALU.mult, ALU.add).then_inc(last_columns, 1)

            for h in range(2):
                if h == 1:
                    dve.wait_ge(columns_ready, B)
                v.tensor_copy(state[h], columns[:, h * HB:h * HB + HB]).then_inc(state_ready[h], 1)

            def new_state(h, w):
                dve.wait_ge(r_gate[h], w)
                v.scalar_tensor_tensor(out=pre1[h], in0=psum[:, 4 * h + 3, 0:HB], scalar=bias_s[:, 5:6], in1=gr[h],
                                       op0=ALU.add, op1=ALU.mult).then_inc(reset_done[h], 1)
                dve.wait_ge(n_sum[h], w)
                dve.wait_ge(reset_done[h], w)
                v.tensor_tensor(pre2[h], pre1[h], psum[:, 4 * h + 2, 0:HB], ALU.add).then_inc(pre_ready[h], 1)
                dve.wait_ge(z_gate[h], w)
                v.scalar_tensor_tensor(out=keep[h], in0=gz[h], scalar=1.0, in1=columns[:, ds(w * (2 * HB) + h * HB, HB)],
                                       op0=ALU.subtract, op1=ALU.mult).then_inc(keep_ready[h], 1)
                dve.wait_ge(n_gate[h], w)
                v.tensor_tensor(mix[h], gn[h], gz[h], ALU.mult).then_inc(mix_ready[h], 1)
                dve.wait_ge(mix_ready[h], w)
                dve.wait_ge(keep_ready[h], w)
                dve.wait_ge(added[h], w)
                dve.wait_ge(sedge_ready[h], w * 2)
                v.tensor_tensor(state[h], mix[h], keep[h], ALU.subtract).then_inc(state_ready[h], 1)

            with dve.Fori(1, W) as w:
                for h in range(2):
                    new_state(h, w)

            dve.wait_ge(added[0], W)
            to_stage(v.tensor_copy, 0, 0).then_inc(staged[0], 1)
            dve.wait_ge(added[1], W)

            with dve.Fori(0, NG) as j:
                for n in range(1, 8, 2):
                    dve.wait_ge(t_done, j * 8 + (n + 1))
                    v.tensor_copy(by_w[:, 512 * n:512 * n + 512], psum[:, n, :]).then_inc(t_dve, 1)
                for n in range(1, 11, 2):
                    dve.wait_ge(w_done, j * 11 + (n + 1))
                    to_by_h(v.tensor_copy, n).then_inc(w_dve, 1)
                for k in range(8):
                    v.bn_stats(bn[:, ds(j * 48 + 6 * k, 6)],
                               image[:, ds(j * (GB * ROWS) + 512 * k, 512)]).then_inc(st2, 1)
                for n in range(1, 18, 2):
                    dve.wait_ge(h_done, j * 18 + (n + 1))
                    to_spectrum(v.tensor_copy, j, n).then_inc(h_dve, 1)

            n2 = [0]

            def step2(ins):
                n2[0] += 1
                ins.then_inc(stat2, 1)

            def settle2():
                dve.wait_ge(stat2, n2[0])

            m16 = mv.rearrange("p (b k) -> p b k", k=2)
            g16 = gs.rearrange("p (b k) -> p b k", k=2)
            dve.wait_ge(st2, 32)
            for b in range(B):
                step2(v.bn_aggr(mv[:, 2 * b:2 * b + 2], bn[:, 12 * b:12 * b + 12]))
            settle2()
            step2(v.tensor_tensor(sq, m16[:, :, 0], m16[:, :, 0], ALU.mult))
            settle2()
            step2(v.tensor_tensor(m16[:, :, 1], m16[:, :, 1], sq, ALU.add))
            dve.wait_ge(sum2, 1)
            step2(v.tensor_copy(gs, psum[:, 7, 0:2 * B]))
            settle2()
            step2(v.tensor_tensor(sq, g16[:, :, 0], g16[:, :, 0], ALU.mult))
            settle2()
            step2(v.tensor_tensor(var, g16[:, :, 1], sq, ALU.subtract))
            dve.wait_ge(dev2, 1)
            step2(v.reciprocal(rstd, rstd_in))
            dve.wait_ge(h_act, 9 * NG)
            dve.wait_ge(h_dve, 9 * NG)
            step2(v.tensor_scalar(shift, g16[:, :, 0], float(H * W), None, ALU.mult))
            settle2()
            dc = spec[0:C, 0:B]
            step2(v.tensor_tensor(dc, dc, shift[0:C, :], ALU.subtract))
            settle2()

            dve.wait_ge(diag_zeroed, 2)

            def positive(c_cols, slot, m, source=None):
                src = (source if source is not None else spec[:, c_cols])[C * m:C * m + C, :] \
                    .rearrange("p (t r b) -> p t r b", r=2, b=B)
                dst = diag[slot][C * m:C * m + C, :].rearrange("p (t k q b) -> p t k q b", k=3, q=4, b=B)[:, :, 1:3, m, :]
                scale = rstd[C * m:C * m + C, :].unsqueeze(1).unsqueeze(1).broadcast_to([C, CHUNK_T, 2, B])
                return v.tensor_tensor(dst, src, scale, ALU.mult)

            for c in range(4):
                if c >= 2:
                    dve.wait_ge(l2_done, c - 1)
                for m in range(HM):
                    positive(slice(c * CHUNK, c * CHUNK + CHUNK), c % 2, m).then_inc(l2_pos, 1)
            dve.wait_ge(l2_done, 4)
            dve.wait_ge(sq1_done, 1)
            dve.wait_ge(l2_neg, 16)
            dve.wait_ge(l2_pos, 16)
            res = psum[:, 0:4, :].rearrange("p n (k r q b) -> p (n k) r q b", k=4, r=2, q=4)
            low = spec[:, 0:2048].rearrange("p (k t r b) -> p k t r b", t=4, r=2, b=B)
            col0 = spec[0:C, 0:H * 4 * XT].rearrange("p (k t r b) -> p k t r b", t=4, r=2, b=B)[:, :, 0]
            n_add = 0
            for t in range(4):
                for m in range(HM):
                    o = res[C * t:C * t + C, :, :, m, :]
                    if t == 0 and m == 0:
                        continue
                    x_ = low[C * m:C * m + C, :, t]
                    v.tensor_tensor(x_, x_, o, ALU.add).then_inc(l2_added, 1)
                    n_add += 1
            o = res[0:C, :, :, 0, :]
            v.scalar_tensor_tensor(out=sq[0:C, :], in0=o[:, 0, 0, :], scalar=1.0, in1=shift[0:C, :],
                                   op0=ALU.mult, op1=ALU.add).then_inc(l2_added, 1)
            dve.wait_ge(l2_added, n_add + 1)
            v.tensor_tensor(dc, dc, sq[0:C, :], ALU.add).then_inc(l2_added, 1)
            half = col0[:, 1:MODES]
            for sign, ri, dst in ((0.5, None, half), (0.5, 0, col0[:, H - 1:H - MODES:-1, 0, :]),
                                  (-0.5, 1, col0[:, H - 1:H - MODES:-1, 1, :])):
                s_ = o[:, 1:MODES] if ri is None else o[:, 1:MODES, ri, :]
                if ri is None:
                    for r in range(2):
                        v.scalar_tensor_tensor(out=dst[:, :, r, :], in0=s_[:, :, r, :], scalar=sign, in1=dst[:, :, r, :],
                                               op0=ALU.mult, op1=ALU.add).then_inc(l2_added, 1)
                else:
                    v.scalar_tensor_tensor(out=dst, in0=s_, scalar=sign, in1=dst,
                                           op0=ALU.mult, op1=ALU.add).then_inc(l2_added, 1)
            v.tensor_copy(energy, var).then_inc(l2_added, 1)
            v.memset(delta, 0.0).then_inc(l2_added, 1)
            v.tensor_copy(mean, g16[:, :, 0]).then_inc(l2_added, 1)
            assert n_add + 2 + 4 + 3 == 24
            dve.wait_ge(l2_added, 24)
            dve.wait_ge(sq2_done, 1)
            v.tensor_tensor(sq_after, sq_after, sq_before, ALU.subtract).then_inc(stat3, 1)
            dve.wait_ge(stat3, 1)
            v.tensor_reduce(delta[:, 0:B], sq_after.rearrange("p (n b) -> p b n", b=B),
                            mybir.AxisListType.X, ALU.add).then_inc(stat3, 1)
            dve.wait_ge(stat3, 2)
            v.scalar_tensor_tensor(out=delta[0:C, 0:B], in0=sq_after[0:C, 0:B], scalar=-0.5, in1=delta[0:C, 0:B],
                                   op0=ALU.mult, op1=ALU.add).then_inc(l2_added, 1)
            dve.wait_ge(l2_added, 25)
            v.tensor_copy(delta[0:C, B:2 * B], dc).then_inc(stat3, 1)
            dve.wait_ge(sum3, 1)
            v.tensor_scalar(mean, psum[:, 7, B:2 * B], 8.0 / (2 * H * W), None, ALU.mult).then_inc(stat3, 1)
            v.scalar_tensor_tensor(out=energy, in0=psum[:, 7, 0:B], scalar=2.0 * 8 / (2.0 * (H * W) ** 2), in1=energy,
                                   op0=ALU.mult, op1=ALU.add).then_inc(stat3, 1)
            dve.wait_ge(stat3, 5)
            v.tensor_tensor(sq, mean, mean, ALU.mult).then_inc(stat3, 1)
            dve.wait_ge(stat3, 6)
            v.tensor_tensor(var, energy, sq, ALU.subtract).then_inc(stat3, 1)
            dve.wait_ge(dev3, 1)
            v.reciprocal(rstd, rstd_in).then_inc(stat3, 1)
            v.scalar_tensor_tensor(out=dc, in0=mean[0:C, :], scalar=-float(H * W), in1=dc,
                                   op0=ALU.mult, op1=ALU.add).then_inc(stat3, 1)
            dve.wait_ge(stat3, 9)

            def full(q, first):
                for i in range(4):
                    if not (first and i < 2):
                        dve.wait_ge(mix_done, q * 4 + (i - 1))
                    for m in range(HM):
                        positive(ds(q * 2048 + i * CHUNK, CHUNK), i % 2, m).then_inc(pos_ready, 1)

            full(0, True)
            with dve.Fori(1, NCHUNK // 4) as q:
                full(q, False)
            dve.wait_ge(mix_done, NCHUNK - 1)
            for m in range(HM):
                positive(None, 0, m, source=spec9).then_inc(pos_ready, 1)

            dve.wait_ge(nyq_moved, 2)
            dve.wait_ge(y_moved, NCHUNK)
            y0 = spec[0:C, 0:H * 4 * XT].rearrange("p (k r q b) -> p k r q b", r=2, q=4, b=B)[:, :, :, 0, :]
            n32 = nyq_half[0:C, :].rearrange("p (r k b) -> p r k b", r=2, b=B)
            ts = [t[0:C, :].rearrange("p (k b) -> p k b", b=B) for t in t_sum]
            k = 0
            for ri, op_same, op_mirror in ((0, ALU.subtract, ALU.add), (1, ALU.add, ALU.subtract)):
                other = n32[:, 1 - ri]
                v.scalar_tensor_tensor(out=ts[ri], in0=y0[:, :, ri, :], scalar=0.5, in1=other,
                                       op0=ALU.mult, op1=op_same).then_inc(sym, 1)
                v.scalar_tensor_tensor(out=ts[2], in0=y0[:, :, ri, :], scalar=0.5 if ri == 0 else -0.5, in1=other,
                                       op0=ALU.mult, op1=ALU.add).then_inc(sym, 1)
                k += 2
                dve.wait_ge(sym, k)
                v.tensor_tensor(y0[:, 1:H, ri, :], ts[ri][:, 1:H, :], ts[2][:, H - 1:0:-1, :], ALU.add).then_inc(sym, 1)
                v.tensor_tensor(y0[:, 0, ri, :], ts[ri][:, 0, :], ts[2][:, 0, :], ALU.add).then_inc(sym, 1)
                k += 2
                dve.wait_ge(sym, k)
            yv = ystage.rearrange("p (n b) -> p n b", b=GB)
            sv_ = spec[:, :].rearrange("p (n b) -> p n b", b=B)
            v.tensor_copy(yv[:, 512:1024, :], sv_[:, 512:1024, 0:GB]).then_inc(ystaged, 1)
            with dve.Fori(0, NG) as j:
                for n in range(1, 8, 2):
                    dve.wait_ge(a_done, j * 8 + (n + 1))
                    v.tensor_copy(by_kh[:, 512 * n:512 * n + 512], psum[:, n, :]).then_inc(a_dve, 1)
                for n in range(1, 8, 2):
                    dve.wait_ge(b_done, j * 8 + (n + 1))
                    to_kw(v.tensor_copy, n).then_inc(b_dve, 1)
                for n in range(8):
                    dve.wait_ge(c_done, j * 8 + (n + 1))
                    for i in range(2):
                        part = images(j).rearrange("p (b h w) -> p h b w", b=GB, w=W)[:, 2 * n + i]
                        res = psum[:, n, 256 * i:256 * i + 256].rearrange("p (b w) -> p b w", b=GB)
                        v.scalar_tensor_tensor(out=part, in0=res, scalar=bias_o[:, 0:1], in1=part,
                                               op0=ALU.add, op1=ALU.add).then_inc(image_done, 1)



def kernel(x, L0_conv_weight, L0_conv_bias, L1_conv_weight_ih, L1_conv_bias_ih, L1_conv_weight_hh,
           L1_conv_bias_hh, L2_conv_w_real, L2_conv_w_imag, L3_conv_kernel_re, L3_conv_kernel_im, L3_conv_bias):
    import concourse.bacc as bacc
    from concourse.bass_utils import run_bass_kernel_spmd

    def rows(a, n=P):
        return np.ascontiguousarray(a).reshape(n, -1)

    x_l = rows(np.asarray(x).reshape(B, C, H4, HM, W).transpose(3, 1, 0, 2, 4))
    conv_w = np.ascontiguousarray(np.asarray(L0_conv_weight)[:, :, ::-1].transpose(1, 3, 2, 0)).reshape(C, 3, 3 * C)
    wi = np.ascontiguousarray(np.asarray(L1_conv_weight_ih).reshape(3, C, 3, C)[:, :, ::-1].transpose(3, 0, 2, 1)).reshape(C, 3, 3 * C)
    wh = np.ascontiguousarray(np.asarray(L1_conv_weight_hh).reshape(3, C, C).transpose(2, 0, 1))
    sb_ = np.ascontiguousarray(np.concatenate([np.asarray(L1_conv_bias_ih).reshape(3, C),
                                               np.asarray(L1_conv_bias_hh).reshape(3, C)]).T)
    w2 = np.stack([np.asarray(L2_conv_w_real), np.asarray(L2_conv_w_imag)])
    w2 = rows(w2.reshape(2, C, C, MODES, 4, 4).transpose(5, 1, 3, 4, 0, 2))
    k = np.stack([np.asarray(L3_conv_kernel_re), np.asarray(L3_conv_kernel_im)])
    w3 = rows(k[..., :KW].reshape(2, C, C, H, 2, 4, 4).transpose(6, 2, 4, 3, 5, 0, 1))
    w9 = rows(k[..., KW].reshape(2, C, C, 4, 16).transpose(3, 2, 4, 0, 1))
    group, parts = constants()
    const = np.ascontiguousarray(np.concatenate([parts[n] for n in CONST_COLS], 1))
    arrays = dict(x=x_l, conv_w=conv_w, conv_b=np.asarray(L0_conv_bias).reshape(C, 1), scan_wi=wi, scan_wh=wh,
                  scan_b=sb_, w2=w2, w3=w3, w9=w9, out_b=np.asarray(L3_conv_bias).reshape(C, 1),
                  group=group, const=const)
    nc = bacc.Bacc("TRN2", target_bir_lowering=False, num_devices=1)
    args = [nc.dram_tensor(f"{n}_dram", a.shape, F32, kind="ExternalInput").ap() for n, a in arrays.items()]
    args.append(nc.dram_tensor("out_dram", [P, B * ROWS], F32, kind="ExternalOutput").ap())
    program(nc, *args)
    r = run_bass_kernel_spmd(nc, [{f"{n}_dram": a for n, a in arrays.items()}], core_ids=[0])
    y = r.results[0]["out_dram"].reshape(HM, C, B, H4, W)
    return np.ascontiguousarray(y.transpose(2, 1, 3, 0, 4)).reshape(B, C, H, W)
```

```python
import numpy as np
import concourse.bass as bass
from concourse import mybir
from contextlib import ExitStack

F32 = mybir.dt.float32
ALU = mybir.AluOpType
ACT = mybir.ActivationFunctionType

B, C, H, W = 16, 32, 64, 64
HM = 4
H4 = H // HM
P = HM * C
ROWS = H4 * W
KW = W // 2
NYQ = W // 2 + 1
MODES = 16
GB = 4
NG = B // GB
TILE = 2 * HM * B
XT = 2 * B
CHUNK_T = 16
CHUNK = CHUNK_T * XT
NCHUNK = 2 * H * 4 // CHUNK_T
PLANES = 3 * HM * B
EPS = 1e-5


def constants():
    ang = 2 * np.pi * np.outer(np.arange(64), np.arange(64)) / 64
    cos, sin = np.cos(ang), np.sin(ang)
    cos[np.abs(cos) < 1e-12] = 0
    sin[np.abs(sin) < 1e-12] = 0
    ident = np.eye(P)
    group = np.kron(np.ones((HM, HM)), np.kron(np.eye(C // 2), np.ones((2, 2)))) / (2 * HM)
    fw = np.zeros((2, W, 2, 2, NYQ))
    for b in range(2):
        fw[b, :, 0, b] = cos[:, :NYQ]
        fw[b, :, 1, b] = -sin[:, :NYQ]
    fh = np.stack([np.stack([cos, -sin], 1), np.stack([sin, cos], 1)])
    ih = np.stack([np.stack([cos, sin], 1), np.stack([-sin, cos], 1)], 1).reshape(P, P)
    p = np.arange(KW)
    kw = 16 * (p // 16) + 4 * (p % 4) + (p // 4) % 4
    scale = np.where(kw == 0, 0.5, 2.0)[:, None] / (H * W)
    back_r = cos[kw] * scale
    back_i = -sin[kw] * scale
    back_i[0] = 0.5 * (-1.0) ** np.arange(W) / (H * W)
    iw = np.concatenate([np.kron(np.eye(2), back_r), np.kron(np.eye(2), back_i)])
    parts = dict(ident=ident, fw=fw.reshape(P, -1), fh=fh.reshape(P, -1), ih=ih, iw=iw)
    return group.astype(np.float32), {k: v.astype(np.float32) for k, v in parts.items()}


KEPT_COLS = dict(ident=P, ih=P, iw=2 * W)
FORWARD_COLS = dict(fw=4 * NYQ, fh=2 * H)


def program(nc, x, conv_w, conv_b, scan_wi, scan_wh, scan_b, w2, w3, w9, out_b, group_d, const_d, out):
    ctx = ExitStack()
    with ctx:
        def sem(name):
            return ctx.enter_context(nc.semaphore(name))

        def sb(name, cols):
            return ctx.enter_context(nc.sbuf_tensor(name, [P, cols], F32))

        image = sb("image", B * ROWS)
        spec = sb("spec", 2 * H * 4 * XT)
        work = sb("work", B * ROWS + 128)
        kept = sb("kept", sum(KEPT_COLS.values()))
        nf = sum(FORWARD_COLS.values())
        matrices = sb("matrices", 2 * H * B + H * B // 2)
        forward_m = matrices[:, 0:nf]
        conv_m = matrices[:, nf:nf + 5 * P]
        scan_m = matrices[:, nf + 5 * P:nf + 14 * P]
        group_m = matrices[:, nf + 14 * P:nf + 15 * P]
        small = sb("small", 560)
        psum = ctx.enter_context(nc.psum_tensor("psum", [P, 8, 512], F32))

        cm = {}
        for buf, widths in ((kept, KEPT_COLS), (forward_m, FORWARD_COLS)):
            at = 0
            for k, n in widths.items():
                cm[k] = buf[:, at:at + n]
                at += n
        at = [0]

        def sm(n):
            at[0] += n
            return small[:, at[0] - n:at[0]]

        bn = sm(32 * 6)
        bn0, bn1 = bn[:, 0:48], bn[:, 48:96]
        mv0, gs0, mv1, gs1 = [bn[:, 96 + 8 * i:104 + 8 * i] for i in range(4)]
        carrier = bn[:, 152:153]
        sq0, var0, rstd_in0, sq1, var1, rstd_in1 = [bn[:, 128 + 4 * i:132 + 4 * i] for i in range(6)]
        mv = sm(32)
        gs = sm(32)
        sq = sm(16)
        mean, rstd, shift = sm(16), sm(16), sm(16)
        energy = sm(16)
        delta = sm(16)
        var, rstd_in = sm(16), sm(16)
        sc0, sh0, sc1, sh1 = sm(GB), sm(GB), sm(GB), sm(GB)
        bias_c, bias_o, eps_c = sm(1), sm(1), sm(1)
        bias_s = sm(6)
        bias_rz = sm(2)
        PADW = W + 2
        padded = [spec[:, i * H4 * PADW:(i + 1) * H4 * PADW] for i in range(2)]
        edges = [spec[:, (2 + i) * H4 * PADW:(3 + i) * H4 * PADW] for i in range(2)]
        HB = B * H4 // 2
        off = 4 * H4 * PADW

        def scan_buf():
            nonlocal off
            off += HB
            return spec[:, off - HB:off]

        state = [scan_buf() for _ in range(2)]
        sedge = [scan_buf() for _ in range(2)]
        gr, gz, gn, pre1, pre2, keep, mix = [[scan_buf() for _ in range(2)] for _ in range(7)]
        columns = work[:, 0:B * ROWS]
        stage = work[:, 0:4096]
        by_w = work[:, 4096:8192]
        by_h = work[:, 8192:8192 + C * 4 * NYQ]
        w2_m = work[:, 12416:16512]
        diag = [work[:, i * CHUNK_T * PLANES:(i + 1) * CHUNK_T * PLANES] for i in range(4)]
        w3_m = [w2_m[:, 1024 * i:1024 + 1024 * i] for i in range(4)]
        spec9 = conv_m[:, 0:16 * XT]
        squares = [scan_m[:, CHUNK * i:CHUNK + CHUNK * i] for i in range(2)]
        l2_copy = diag[3][:, 0:CHUNK]
        nyq = matrices[:, 0:2 * H * B]
        t_sum = matrices[:, 2 * H * B:2 * H * B + H * B // 2]
        ystage = work[:, 0:4096]
        by_kh = work[:, 4096:8192]
        by_kw = work[:, 8192:12288]

        x_first = [sem(f"x_first{u}") for u in range(GB)]
        x_in = [sem(f"x_in{j}") for j in range(NG)]
        conv_zeroed, scan_zeroed = sem("conv_zeroed"), sem("scan_zeroed")
        conv_b_in = sem("conv_b_in")
        conv_w_in, scan_w_in, small_in, group_in, const_in = map(
            sem, ("conv_w_in", "scan_w_in", "small_in", "group_in", "const_in"))
        eps_set = sem("eps_set")
        pads_zeroed = sem("pads_zeroed")
        half0, half1 = sem("half0"), sem("half1")
        carried = sem("carried")
        stat0, stat1 = sem("stat0"), sem("stat1")
        sum0, sum1 = sem("sum0"), sem("sum1")
        dev0, dev1 = sem("dev0"), sem("dev1")
        padded_ready, edges_ready = sem("padded_ready"), sem("edges_ready")
        conv_done, conv_added = sem("conv_done"), sem("conv_added")
        columns_ready, last_columns = sem("columns_ready"), sem("last_columns")
        bias_ready = sem("bias_ready")
        state_ready = [sem(f"state_ready{h}") for h in range(2)]
        sedge_ready = [sem(f"sedge_ready{h}") for h in range(2)]
        r_sum, z_sum, n_sum = [[sem(f"{g}_sum{h}") for h in range(2)] for g in "rzn"]
        r_gate, z_gate, n_gate = [[sem(f"{g}_gate{h}") for h in range(2)] for g in "rzn"]
        reset_done = [sem(f"reset_done{h}") for h in range(2)]
        pre_ready = [sem(f"pre_ready{h}") for h in range(2)]
        keep_ready = [sem(f"keep_ready{h}") for h in range(2)]
        mix_ready = [sem(f"mix_ready{h}") for h in range(2)]
        added = [sem(f"added{h}") for h in range(2)]
        staged = [sem(f"staged{q}") for q in range(2)]
        t_done, t_act, t_dve = sem("t_done"), sem("t_act"), sem("t_dve")
        w_done, w_act, w_dve = sem("w_done"), sem("w_act"), sem("w_dve")
        h_done, h_act, h_dve = sem("h_done"), sem("h_act"), sem("h_dve")
        st2 = sem("st2")
        stat2, sum2, dev2 = sem("stat2"), sem("sum2"), sem("dev2")
        diag_zeroed = sem("diag_zeroed")
        w2_in = sem("w2_in")
        l2_pos, l2_neg, l2_done = sem("l2_pos"), sem("l2_neg"), sem("l2_done")
        l2_added, l2_pool_added = sem("l2_added"), sem("l2_pool_added")
        l2_pool, l2_moved = sem("l2_pool"), sem("l2_moved")
        sq_done, sq_summed = sem("sq_done"), sem("sq_summed")
        stat3, sum3, dev3 = sem("stat3"), sem("sum3"), sem("dev3")
        w3_in = [sem(f"w3_in{i}") for i in range(4)]
        pos_pool = sem("pos_pool")
        pos_ready, neg_ready, mix_done, y_moved = map(sem, ("pos_ready", "neg_ready", "mix_done", "y_moved"))
        nyq_moved, sym = sem("nyq_moved"), sem("sym")
        ystaged = sem("ystaged")
        a_done, a_act, a_dve = sem("a_done"), sem("a_act"), sem("a_dve")
        b_done, b_act, b_dve = sem("b_done"), sem("b_act"), sem("b_dve")
        c_done, image_done = sem("c_done"), sem("image_done")
        stored = sem("stored")

        def steps_mean(n):
            return 1 + n + 2

        def steps_var(n):
            return steps_mean(n) + 3

        def steps_all(n):
            return steps_var(n) + 2

        KGN = steps_all(GB)
        EXTRA0 = steps_all(1) + steps_all(GB - 1) - KGN

        L2_ADDED = 3 + 4 + 15 - 4
        STAT3 = 10
        ENERGY = 8.0 / (H * W) ** 2
        ds = bass.ds

        def images(j, n=GB):
            return image[:, ds(j * (GB * ROWS), n * ROWS)]

        def to_cols(op, j, u, cols, *func, **kw_):
            dst = columns.rearrange("p (w b h) -> p w b h", b=B, h=H4)[:, cols, ds(j * GB + u, 1), :] \
                .rearrange("p w o h -> p (o h) w")
            src = image[:, ds(j * (GB * ROWS) + u * ROWS, ROWS)].rearrange("p (h w) -> p h w", w=W)[:, :, cols]
            return op(dst, src, *func, **kw_)

        def to_stage(copy, j, q, *func):
            src = images(j)[:, q * 2 * ROWS:(q + 1) * 2 * ROWS].rearrange("p (b h w) -> p b h w", b=2, w=W)
            dst = stage[:, q * 2 * ROWS:(q + 1) * 2 * ROWS].rearrange("p (h b w) -> p b h w", b=2, w=W)
            return copy(dst, src, *func)

        def to_by_h(copy, k, q, ri, *func):
            banks, chans = (2, 3) if k < 5 else (1, 2)
            at_ = (2 * k + 4) % 8
            src = psum[H * q:H * q + H, at_:at_ + banks, 0:4 * NYQ * chans] \
                .rearrange("p n (c r m) -> p n c r m", c=chans, r=2)[:, :, :, ri]
            dst = by_h[H * ri:H * ri + H, :].rearrange("p (q m c) -> p q m c", q=2, c=C)[:, q, :, 6 * k:6 * k + banks * chans] \
                .rearrange("p m (n c) -> p n c m", n=banks)
            return copy(dst, src, *func)

        def to_spectrum(copy, j, n, *func):
            if n < 8:
                g, t = n // 4, n % 4
                src = psum[:, n, :].rearrange("p (b r k) -> p b r k", b=GB, r=2)
                dst = spec[:, :].rearrange("p (g k t r b) -> p g t b r k", g=2, k=H, t=4, r=2)
                dst = dst[:, g, t, ds(j * GB, GB)]
            else:
                src = psum[:, 0, 0:2 * 16 * GB].rearrange("p (b r k) -> p b r k", b=GB, r=2)
                dst = spec9.rearrange("p (k r b) -> p b r k", k=16, r=2)[:, ds(j * GB, GB)]
            return copy(dst, src, *func)

        def positive(multiply, slot, m, columns_):
            src = columns_[C * m:C * m + C, :].rearrange("p (t r b) -> p t r b", r=2, b=B)
            dst = diag[slot][C * m:C * m + C, :].rearrange("p (t k q b) -> p t k q b", k=3, q=4, b=B)[:, :, 1:3, m, :]
            scale = rstd[C * m:C * m + C, :].unsqueeze(1).unsqueeze(1).broadcast_to([C, CHUNK_T, 2, B])
            return multiply(dst, src, scale, ALU.mult)

        def negative(activation, slot, m):
            d = diag[slot][C * m:C * m + C, :].rearrange("p (t k q b) -> p t k q b", k=3, q=HM, b=B)
            return activation(d[:, :, 0, m, :], d[:, :, 2, m, :], ACT.Copy, scale=-1.0)

        def chunk(c):
            return spec[:, ds(c * CHUNK, CHUNK)]

        def low_result(t, m):
            return psum[C * t:C * t + C, 0:4, :].rearrange("p n (k r q b) -> p (n k) r q b", k=4, r=2, q=4)[:, :, :, m, :]

        def add_low(add, t, m):
            if t == 3:
                res = l2_copy[C * m:C * m + C, :].rearrange("p (k r b) -> p k r b", r=2, b=B)
            else:
                res = low_result(t, m)
            low = spec[C * m:C * m + C, 0:4 * CHUNK].rearrange("p (k t r b) -> p k t r b", t=4, r=2, b=B)[:, :, t]
            return add(low, low, res, ALU.add)

        ON_POOL = [(3, m) for m in range(HM)]

        BY_ACT, BY_DVE = (0, 1, 3, 4, 6, 7), (2, 5)
        T_ORDER = (4, 6, 0, 2, 5, 7, 1, 3)

        def to_kw(copy, k, x_, ri, *func):
            src = psum[H * x_:H * x_ + H, 2 * k:2 * k + 2, :].rearrange("p n (o r h) -> p (n o) r h", o=4, r=2)[:, :, ri]
            dst = by_kw[H * ri:H * ri + H, :].rearrange("p (x h o) -> p x o h", x=2, o=C)[:, x_, 8 * k:8 * k + 8]
            return copy(dst, src, *func)

        block = ctx.enter_context(nc.Block())

        @block.sync
        def _(sp):
            for u in range(GB):
                sp.dma_start(image[:, u * ROWS:(u + 1) * ROWS], x[:, u * ROWS:(u + 1) * ROWS]).then_inc(x_first[u], 16)
            sp.wait_ge(conv_w_in, 16 * 8)
            for j in range(1, NG):
                sp.dma_start(images(j), x[:, j * GB * ROWS:(j + 1) * GB * ROWS]).then_inc(x_in[j], 16)
            sp.wait_ge(scan_zeroed, 1)
            sv = scan_m[:, :].rearrange("p (k m) -> p k m", m=P)
            for hi in range(HM):
                lo, up = max(0, hi - 1), min(HM, hi + 2)
                sp.dma_start(sv[C * hi:C * hi + C, 0:3, C * lo:C * up],
                             scan_wi[:, :, C * (lo - hi + 1):C * (up - hi + 1)]).then_inc(scan_w_in, 16)
                sp.dma_start(sv[C * hi:C * hi + C, 6:9, C * hi:C * hi + C], scan_wh).then_inc(scan_w_in, 16)
            sp.dma_start(sv[0:C, 3:6, 0:C], scan_wi[:, :, 2 * C:3 * C]).then_inc(scan_w_in, 16)
            sp.dma_start(sv[C:2 * C, 3:6, P - C:P], scan_wi[:, :, 0:C]).then_inc(scan_w_in, 16)
            sp.dma_start(kept[:, :], const_d[:, 0:sum(KEPT_COLS.values())]).then_inc(const_in, 16)
            sp.dma_start(forward_m, const_d[:, sum(KEPT_COLS.values()):]).then_inc(const_in, 16)
            sp.wait_ge(state_ready[0], W)
            sp.wait_ge(state_ready[1], W)
            sp.dma_start(w2_m, w2).then_inc(w2_in, 16)
            for i in range(4):
                sp.wait_ge(l2_done, i + 1)
                sp.dma_start(w3_m[i], w3[:, i * 1024:(i + 1) * 1024]).then_inc(w3_in[i], 16)
            sp.wait_ge(mix_done, 1)
            sp.dma_start(w3_m[0], w9).then_inc(w3_in[0], 16)
            with sp.Fori(1, NCHUNK // 4) as q:
                for i in range(4):
                    sp.wait_ge(mix_done, q * 4 + (i - 2))
                    slot = (i + 1) % 4
                    sp.dma_start(w3_m[slot], w3[:, ds(q * 4096 + i * 1024, 1024)]).then_inc(w3_in[slot], 16)
            with sp.Fori(0, NG) as j:
                sp.wait_ge(image_done, j * 16 + 16)
                sp.dma_start(out[:, ds(j * (GB * ROWS), GB * ROWS)], images(j)).then_inc(stored, 16)
            sp.wait_ge(stored, 16 * NG)

        @block.gpsimd
        def _(pool):
            pool.dma_start(group_m[:, :], group_d).then_inc(group_in, 16)
            for hm in range(HM):
                q = slice(C * hm, C * hm + C)
                pool.dma_start(bias_c[q, :], conv_b).then_inc(conv_b_in, 16)
            for hm in range(HM):
                q = slice(C * hm, C * hm + C)
                pool.dma_start(bias_o[q, :], out_b).then_inc(small_in, 16)
                pool.dma_start(bias_s[q, :], scan_b).then_inc(small_in, 16)
            nc.gpsimd.memset(scan_m[:, :], 0.0).then_inc(scan_zeroed, 1)
            with pool.Fori(0, W) as w:
                for h in range(2):
                    pool.wait_ge(state_ready[h], w + 1)
                    col = image[:, h * (B // 2 * ROWS):(h + 1) * (B // 2 * ROWS)] \
                        .rearrange("p (n w) -> p n w", w=W)[:, :, ds(w, 1)]
                    nc.gpsimd.tensor_tensor(col, col, state[h].unsqueeze(2), ALU.add).then_inc(added[h], 1)
            pool.wait_ge(t_done, 8)
            to_stage(nc.gpsimd.tensor_copy, 1, 0).then_inc(staged[0], 1)
            with pool.Fori(2, NG) as j:
                pool.wait_ge(t_done, j * 8)
                for q in range(2):
                    to_stage(nc.gpsimd.tensor_copy, j, q).then_inc(staged[q], 1)
            pool.wait_ge(w_done, 6 * NG)
            for i in range(2):
                nc.gpsimd.memset(diag[i], 0.0).then_inc(diag_zeroed, 1)
            pool.wait_ge(diag_zeroed, 2)
            pool.wait_ge(h_act, 6 * NG)
            pool.wait_ge(h_dve, 3 * NG)
            pool.wait_ge(stat2, B + 8)
            for c in range(4):
                if c >= 2:
                    pool.wait_ge(l2_done, c - 1)
                positive(nc.gpsimd.tensor_tensor, c % 2, 3, chunk(c)).then_inc(l2_pool, 1)
            pool.wait_ge(h_done, 9 * NG)
            pool.wait_ge(l2_pool, 4)
            nc.gpsimd.memset(diag[2], 0.0).then_inc(diag_zeroed, 1)
            pool.wait_ge(l2_moved, HM)
            pool.wait_ge(sq_done, 5)
            pool.wait_ge(diag_zeroed, 3)
            for i, (t, m) in enumerate(ON_POOL):
                if i > 0:
                    pool.wait_ge(l2_pool_added, i)
                add_low(nc.gpsimd.tensor_tensor, t, m).then_inc(l2_pool_added, 1)
            pool.wait_ge(l2_pool_added, len(ON_POOL))
            nc.gpsimd.memset(diag[3], 0.0).then_inc(diag_zeroed, 1)
            pool.wait_ge(diag_zeroed, 4)
            pool.wait_ge(l2_added, L2_ADDED)
            pool.wait_ge(stat3, STAT3)
            for s_ in range(5):
                if s_ == 4:
                    pool.wait_ge(mix_done, 1)
                positive(nc.gpsimd.tensor_tensor, s_ % 4, 3, spec9 if s_ == 4 else chunk(s_)).then_inc(pos_pool, 1)
            with pool.Fori(1, NCHUNK // 4) as q:
                for i in range(4):
                    pool.wait_ge(mix_done, q * 4 + (i - 2))
                    positive(nc.gpsimd.tensor_tensor, (i + 1) % 4, 3, chunk(q * 4 + i)).then_inc(pos_pool, 1)
            pool.wait_ge(y_moved, NCHUNK)
            pool.wait_ge(sym, 20)
            pool.wait_ge(pos_pool, NCHUNK + 1)
            with pool.Fori(2, NG) as j:
                pool.wait_ge(a_done, j * 8)
                nc.gpsimd.tensor_copy(ystage.rearrange("p (n b) -> p n b", b=GB),
                                      spec[:, :].rearrange("p (n b) -> p n b", b=B)[:, :, ds(j * GB, GB)]
                                      ).then_inc(ystaged, 1)

        @block.tensor
        def _(pe):
            mm = nc.tensor.matmul
            cv = conv_m[:, :].rearrange("p (k m) -> p k m", m=P)
            sv = scan_m[:, :].rearrange("p (k m) -> p k m", m=P)

            def sum0_of(lo, n, need):
                pe.wait_ge(stat0, need)
                mm(psum[:, 7, 2 * lo:2 * (lo + n)], group_m[:, :], mv0[:, 2 * lo:2 * (lo + n)],
                   start=True, stop=True).then_inc(sum0, 1)

            def sum1_of(lo, n, need):
                pe.wait_ge(stat1, need)
                mm(psum[:, 6, 2 * lo:2 * (lo + n)], group_m[:, :], mv1[:, 2 * lo:2 * (lo + n)],
                   start=True, stop=True).then_inc(sum1, 1)

            def conv_group(j, first, last):
                for u in range(GB):
                    if u == 1 and not first:
                        sum1_of(0, GB, (j - 1) * KGN + steps_mean(GB))
                    if u == 3 and not last:
                        sum0_of(0, GB, (j + 1) * KGN + (EXTRA0 + steps_mean(GB)))
                    xn = padded[u % 2].rearrange("p (h w) -> p h w", w=PADW)
                    en = edges[u % 2].rearrange("p (h w) -> p h w", w=PADW)
                    pe.wait_ge(padded_ready, j * GB + (u + 1))
                    for half in range(2):
                        n = 2 * u + half
                        if not (first and n < 4):
                            pe.wait_ge(conv_added, j * 8 + (n - 3))
                        for kx in range(3):
                            mm(psum[:, n % 4, :], cv[:, kx, :], xn[:, 8 * half:8 * half + 8, kx:kx + W],
                               start=kx == 0, stop=False)
                    if first and u == 0:
                        sum0_of(1, GB - 1, steps_all(1) + steps_mean(GB - 1))
                    pe.wait_ge(edges_ready, j * (4 * GB) + 4 * (u + 1))
                    for half in range(2):
                        n = 2 * u + half
                        mm(psum[:, n % 4, :], cv[:, 3, :], en[:, 8 * half:8 * half + 8, 0:W],
                           start=False, stop=False)
                        mm(psum[:, n % 4, :], cv[:, 4, :], en[:, 8 * half:8 * half + 8, 2:2 + W],
                           start=False, stop=True).then_inc(conv_done, 1)

            pe.wait_ge(group_in, 16)
            sum0_of(0, 1, steps_mean(1))
            pe.wait_ge(conv_w_in, 16 * 8)
            conv_group(0, True, False)
            with pe.Fori(1, NG - 1) as j:
                conv_group(j, False, False)
            conv_group(NG - 1, False, True)
            sum1_of(0, GB - 1, (NG - 1) * KGN + steps_mean(GB - 1))
            sum1_of(GB - 1, 1, (NG - 1) * KGN + steps_all(GB - 1) + steps_mean(1))

            def from_column(h, w):
                for g, bank in ((0, 0), (1, 1), (2, 3)):
                    mm(psum[:, 4 * h + bank, 0:HB], sv[:, 6 + g, :], columns[:, ds(w * (2 * HB) + h * HB, HB)],
                       start=True, stop=bank == 3)

            def banks_free(h, w):
                pe.wait_ge(r_gate[h], w - 1)
                pe.wait_ge(z_gate[h], w - 1)
                pe.wait_ge(reset_done[h], w - 1)

            def from_state(h, w):
                pe.wait_ge(state_ready[h], w)
                for g in (0, 2, 1):
                    mm(psum[:, 4 * h + g, 0:HB], sv[:, g, :], state[h], start=g == 2, stop=False)
                pe.wait_ge(sedge_ready[h], w * 2)
                for g, s in ((0, r_sum), (2, n_sum), (1, z_sum)):
                    mm(psum[:, 4 * h + g, 0:HB], sv[:, 3 + g, :], sedge[h], start=False, stop=True).then_inc(s[h], 1)

            pe.wait_ge(scan_w_in, 16 * 10)
            pe.wait_ge(columns_ready, B // 2)
            pe.wait_ge(conv_added, 2 * B)
            from_column(0, 1)
            from_state(0, 1)
            pe.wait_ge(columns_ready, B)
            pe.wait_ge(last_columns, 1)
            pe.wait_ge(stat1, (NG - 1) * KGN + steps_all(GB - 1) + steps_all(1))
            from_column(1, 1)
            from_state(1, 1)
            banks_free(0, 2)
            from_column(0, 2)
            with pe.Fori(2, W - 1) as w:
                from_state(0, w)
                banks_free(1, w)
                from_column(1, w)
                from_state(1, w)
                banks_free(0, w + 1)
                from_column(0, w + 1)
            from_state(0, W - 1)
            banks_free(1, W - 1)
            from_column(1, W - 1)
            from_state(1, W - 1)

            bw = by_w.rearrange("p (q h c) -> p q h c", q=2, c=C)
            bh = by_h.rearrange("p (b k c) -> p b k c", b=GB, c=C)
            sg = stage.rearrange("p (q h b w) -> p q h b w", q=2, b=2, w=W)
            pe.wait_ge(const_in, 32)
            for h in range(2):
                pe.wait_ge(z_gate[h], W - 1)
                pe.wait_ge(pre_ready[h], W - 1)

            def transposes(j, first=False):
                for n in range(8):
                    if n % 4 == 0:
                        pe.wait_ge(staged[n // 4], j + 1)
                    if not first and n % 2 == 0:
                        pe.wait_ge(w_act, j * 12 + (n - 6))
                        pe.wait_ge(w_dve, j * 12 + (n - 6))
                    for i in range(4):
                        h4 = 4 * (n % 4) + i
                        last = nc.tensor.transpose(psum[:, n, P * i:P * i + P], sg[:, n // 4, h4, :, :], cm["ident"])
                    last.then_inc(t_done, 1)

            def over_w(j, first):
                pe.wait_ge(t_act, j * 6 + 6)
                pe.wait_ge(t_dve, j * 2 + 2)
                for k in range(6):
                    if not first and k < 3:
                        pe.wait_ge(h_act, j * 6 + (k - 2))
                        if k < 2:
                            pe.wait_ge(h_dve, j * 3 + (k - 1))
                    if k >= 4:
                        pe.wait_ge(w_act, j * 12 + 2 * (k - 3))
                        pe.wait_ge(w_dve, j * 12 + 2 * (k - 3))
                    for c in range(6 * k, min(6 * k + 6, C)):
                        last = mm(psum[:, (c // 3 + 4) % 8, 132 * (c % 3):132 * (c % 3) + 132], bw[:, :, :, c], cm["fw"],
                                  start=True, stop=True)
                    last.then_inc(w_done, 1)

            def over_h(j, last_group=False):
                pe.wait_ge(w_act, j * 12 + 12)
                pe.wait_ge(w_dve, j * 12 + 12)
                for n in range(8):
                    if not last_group:
                        if n in BY_DVE:
                            pe.wait_ge(t_dve, j * 2 + (3 + BY_DVE.index(n)))
                        else:
                            pe.wait_ge(t_act, j * 6 + (7 + BY_ACT.index(n)))
                    for b in range(GB):
                        last = mm(psum[:, n, 2 * H * b:2 * H * b + 2 * H], bh[:, b, 4 * n:4 * n + 4, :], cm["fh"],
                                  start=True, stop=True)
                    last.then_inc(h_done, 1)
                pe.wait_ge(h_act, j * 6 + 1)
                fh = cm["fh"].rearrange("p (r k) -> p r k", r=2)
                for b in range(GB):
                    for q in range(4):
                        last = mm(psum[C * q:C * q + C, 0, 32 * b:32 * b + 32], bh[:, b, KW, :],
                                  fh[:, :, 16 * q:16 * q + 16], start=True, stop=True)
                last.then_inc(h_done, 1)
                if last_group:
                    pe.wait_ge(h_act, j * 6 + 2)
                    pe.wait_ge(stat2, B + 2)
                    mm(psum[:, 1, 0:2 * B], group_m, mv, start=True, stop=True).then_inc(sum2, 1)

            transposes(0, True)
            over_w(0, True)
            transposes(1)
            over_h(0)
            with pe.Fori(1, NG - 1) as j:
                over_w(j, False)
                transposes(j + 1)
                over_h(j)
            over_w(NG - 1, False)
            over_h(NG - 1, True)


            def tiles(weights, planes, bank, done, nyquist=False, starts=True):
                wt = weights.rearrange("p (t r o) -> p t r o", r=2, o=C)
                pl = planes.rearrange("p (t m) -> p t m", m=PLANES)
                for t in range(CHUNK_T):
                    k, q = (t % 4, 0) if nyquist else (t // 4, t % 4)
                    o = psum[C * q:C * q + C, bank + (t // 4 if nyquist else 0), TILE * k:TILE * k + TILE]
                    mm(o, wt[:, t, 0, :], pl[:, t, 64:192], start=starts and k == 0, stop=False,
                       skip_group_check=True)
                    last = mm(o, wt[:, t, 1, :], pl[:, t, 0:128], start=False, stop=True, skip_group_check=True)
                last.then_inc(done, 1)

            def sum_squares(s_):
                pe.wait_ge(sq_done, s_ + 2 + s_ // 4)
                mm(psum[:, 6 + s_ // 4, :], group_m, squares[s_ % 2], start=s_ % 4 == 0, stop=s_ % 4 == 3
                   ).then_inc(sq_summed, 1)

            pe.wait_ge(w2_in, 16)
            for c in range(4):
                pe.wait_ge(l2_pos, 3 * (c + 1))
                pe.wait_ge(l2_pool, c + 1)
                pe.wait_ge(l2_neg, 4 * (c + 1))
                tiles(w2_m[:, 1024 * c:1024 * c + 1024], diag[c % 2], c, l2_done)
                sum_squares(c)
            pe.wait_ge(stat3, 1)
            mm(psum[:, 5, 0:B], group_m, delta, start=True, stop=True).then_inc(sum3, 1)
            for s_ in range(4, 8):
                sum_squares(s_)

            def mix(s_, slot, bank, weights_in, y_needed, nyquist=False, starts=True):
                pe.wait_ge(w3_in[slot], weights_in)
                pe.wait_ge(pos_ready, s_ * 3 + 3)
                pe.wait_ge(pos_pool, s_ + 1)
                pe.wait_ge(neg_ready, s_ * 4 + 4)
                if y_needed is not None:
                    pe.wait_ge(y_moved, y_needed)
                tiles(w3_m[slot], diag[slot], bank, mix_done, nyquist, starts)

            for i in range(4):
                mix(i, i, i, 16, None, starts=False)
            pe.wait_ge(stat3, STAT3)
            mix(4, 0, 4, 32, None, nyquist=True)
            with pe.Fori(1, NCHUNK // 4) as q:
                for i in range(4):
                    mix(q * 4 + (i + 1), (i + 1) % 4, i, q * 16 + (16 if i < 3 else 32), q * 4 + (i - 3))

            ys = ystage.rearrange("p (g k r q b) -> p g k r q b", g=2, k=H, r=2, q=4)
            kh = by_kh.rearrange("p (b k o) -> p b k o", b=GB, k=KW)
            kwv = by_kw.rearrange("p (x h m) -> p x h m", x=2, m=P)

            def back_transposes(j, first):
                if first:
                    src = spec[:, :].rearrange("p (g k r q b) -> p g k r q b", g=2, k=H, r=2, q=4)
                    pe.wait_ge(nyq_moved, 2)
                    pe.wait_ge(sym, 20)
                else:
                    src = ys
                    pe.wait_ge(ystaged, j + 1)
                for i_, n in enumerate(T_ORDER if first else range(8)):
                    if first and i_ == 2:
                        pe.wait_ge(y_moved, NCHUNK)
                    if not first and n % 2 == 0:
                        pe.wait_ge(b_act, j * 8 + (n - 6))
                        pe.wait_ge(b_dve, j * 8 + (n - 6))
                    b, g = n // 2, n % 2
                    for i in range(4):
                        last = nc.tensor.transpose(psum[:, n, P * i:P * i + P], src[:, g, :, :, i, b], cm["ident"])
                    last.then_inc(a_done, 1)

            def back(j, first, last_group=False):
                pe.wait_ge(a_act, j * 6 + 6)
                pe.wait_ge(a_dve, j * 2 + 2)
                for n in range(8):
                    if not first:
                        pe.wait_ge(image_done, j * 16 + (2 * n - 14))
                    for i in range(4):
                        last = mm(psum[:, n, P * i:P * i + P], kh[:, :, :, 4 * n + i], cm["ih"],
                                  start=True, stop=True)
                    last.then_inc(b_done, 1)
                if not last_group:
                    back_transposes(j + 1, False)
                pe.wait_ge(b_act, j * 8 + 8)
                pe.wait_ge(b_dve, j * 8 + 8)
                for n in range(8):
                    if not last_group:
                        if n in BY_DVE:
                            pe.wait_ge(a_dve, j * 2 + (3 + BY_DVE.index(n)))
                        else:
                            pe.wait_ge(a_act, j * 6 + (7 + BY_ACT.index(n)))
                    for i in range(2):
                        for x_ in range(2):
                            at_ = 256 * i + 128 * x_
                            last = mm(psum[:, n, at_:at_ + 128], kwv[:, x_, 2 * n + i, :], cm["iw"], start=True, stop=True)
                    last.then_inc(c_done, 1)

            back_transposes(0, True)
            back(0, True)
            with pe.Fori(1, NG - 1) as j:
                back(j, False)
            back(NG - 1, False, True)

        @block.scalar
        def _(act):
            a = nc.scalar.activation

            def deviation(d, v_, lo, n, stat_sem, need, dev_sem):
                act.wait_ge(stat_sem, need)
                a(d[:, lo:lo + n], v_[:, lo:lo + n], ACT.Sqrt, bias=eps_c).then_inc(dev_sem, 1)

            def edge_rows(j, u):
                act.wait_ge(padded_ready, j * GB + (u + 1))
                xn = padded[u % 2].rearrange("p (h w) -> p h w", w=PADW)
                en = edges[u % 2].rearrange("p (h w) -> p h w", w=PADW)
                a(en[0:C, 1:H4, :], xn[P - C:P, 0:H4 - 1, :], ACT.Copy).then_inc(edges_ready, 1)
                a(en[C:2 * C, 0:H4 - 1, :], xn[0:C, 1:H4, :], ACT.Copy).then_inc(edges_ready, 1)
                a(en[2 * C:3 * C, 1:H4, 0:PADW - 1], xn[P - C:P, 0:H4 - 1, 1:PADW], ACT.Copy).then_inc(edges_ready, 1)
                a(en[3 * C:4 * C, 0:H4 - 1, 0:PADW - 1], xn[0:C, 1:H4, 1:PADW], ACT.Copy).then_inc(edges_ready, 1)

            def to_columns(j, images_):
                for u in images_:
                    to_cols(a, j, u, slice(0, W), ACT.Identity, scale=sc1[:, u:u + 1],
                            bias=sh1[:, u:u + 1]).then_inc(columns_ready, 1)

            def conv_group(j, first, last):
                for u in range(GB):
                    if u < GB - 1:
                        edge_rows(j, u + 1)
                    elif not last:
                        deviation(rstd_in0, var0, 0, GB, stat0, (j + 1) * KGN + (EXTRA0 + steps_var(GB)), dev0)
                        edge_rows(j + 1, 0)
                    if u == 1 and not first:
                        deviation(rstd_in1, var1, 0, GB, stat1, (j - 1) * KGN + steps_var(GB), dev1)
                    if u >= 2 and not first:
                        act.wait_ge(stat1, (j - 1) * KGN + KGN)
                        to_columns(j - 1, (2 * u - 4, 2 * u - 3))

            act.wait_ge(conv_zeroed, 1)
            cv = conv_m[:, :].rearrange("p (k m) -> p k m", m=P)
            for hi in range(HM):
                lo, up = max(0, hi - 1), min(HM, hi + 2)
                act.dma_start(cv[C * hi:C * hi + C, 0:3, C * lo:C * up],
                              conv_w[:, :, C * (lo - hi + 1):C * (up - hi + 1)]).then_inc(conv_w_in, 16)
            for quad in range(4):
                taps, rows_ = slice(0, C), slice(P - C, P)
                if quad % 2 == 0:
                    taps, rows_ = slice(2 * C, 3 * C), slice(0, C)
                kx = slice(0, 3, 2) if quad < 2 else slice(1, 2)
                act.dma_start(cv[C * quad:C * quad + C, slice(3, 5 if quad < 2 else 4), rows_],
                              conv_w[:, kx, taps]).then_inc(conv_w_in, 16)
            act.wait_ge(eps_set, 1)
            deviation(rstd_in0, var0, 0, 1, stat0, steps_var(1), dev0)
            edge_rows(0, 0)
            deviation(rstd_in0, var0, 1, GB - 1, stat0, steps_all(1) + steps_var(GB - 1), dev0)
            conv_group(0, True, False)
            with act.Fori(1, NG - 1) as j:
                conv_group(j, False, False)
            conv_group(NG - 1, False, True)
            before = (NG - 1) * KGN
            deviation(rstd_in1, var1, 0, GB - 1, stat1, before + steps_var(GB - 1), dev1)
            act.wait_ge(stat1, before + steps_all(GB - 1))
            to_columns(NG - 1, (0, 1))
            before += steps_all(GB - 1)
            deviation(rstd_in1, var1, GB - 1, 1, stat1, before + steps_var(1), dev1)
            to_columns(NG - 1, (2,))
            act.wait_ge(stat1, before + steps_all(1))
            to_cols(a, NG - 1, GB - 1, slice(0, W // 2), ACT.Identity, scale=sc1[:, GB - 1:GB],
                    bias=sh1[:, GB - 1:GB]).then_inc(columns_ready, 1)

            def state_edges(h, w):
                act.wait_ge(state_ready[h], w + 1)
                s = state[h].rearrange("p (b h) -> p b h", h=H4)
                e = sedge[h].rearrange("p (b h) -> p b h", h=H4)
                a(e[0:C, :, 1:H4], s[P - C:P, :, 0:H4 - 1], ACT.Copy).then_inc(sedge_ready[h], 1)
                a(e[C:2 * C, :, 0:H4 - 1], s[0:C, :, 1:H4], ACT.Copy).then_inc(sedge_ready[h], 1)

            def gates(h, w):
                act.wait_ge(r_sum[h], w)
                a(gr[h], psum[:, 4 * h, 0:HB], ACT.Sigmoid, bias=bias_rz[:, 0:1]).then_inc(r_gate[h], 1)
                act.wait_ge(z_sum[h], w)
                a(gz[h], psum[:, 4 * h + 1, 0:HB], ACT.Sigmoid, bias=bias_rz[:, 1:2]).then_inc(z_gate[h], 1)

            def candidate(h, w):
                act.wait_ge(pre_ready[h], w)
                a(gn[h], pre2[h], ACT.Tanh, bias=bias_s[:, 2:3]).then_inc(n_gate[h], 1)

            act.wait_ge(bias_ready, 1)

            def scan_step(w):
                gates(0, w)
                state_edges(1, w - 1)
                candidate(0, w)
                gates(1, w)
                state_edges(0, w)
                candidate(1, w)

            state_edges(0, 0)
            scan_step(1)
            with act.Fori(2, W) as w:
                scan_step(w)

            act.wait_ge(added[0], W)
            to_stage(a, 0, 1, ACT.Copy).then_inc(staged[1], 1)
            act.wait_ge(added[1], W)
            sp6 = spec[:, :].rearrange("p (g k t r b) -> p g k t r b", g=2, k=H, t=4, r=2)
            s9 = spec9.rearrange("p (k r b) -> p k r b", r=2, b=B)

            def move_by_w(j):
                for i, n in enumerate(BY_ACT):
                    act.wait_ge(t_done, j * 8 + (n + 1))
                    a(by_w[:, 512 * n:512 * n + 512], psum[:, n, :], ACT.Copy).then_inc(t_act, 1)

            def forward(j, last_group=False):
                for k in range(6):
                    act.wait_ge(w_done, j * 6 + (k + 1))
                    for ri in range(2):
                        to_by_h(a, k, 0, ri, ACT.Copy).then_inc(w_act, 1)
                if not last_group:
                    move_by_w(j + 1)
                for n in (0, 1, 2, 4, 6, 8):
                    act.wait_ge(h_done, j * 9 + (n + 1))
                    to_spectrum(a, j, n, ACT.Copy).then_inc(h_act, 1)
                    if last_group and n == 8:
                        act.wait_ge(stat2, B + 5)
                        a(rstd_in[:, 0:B], var[:, 0:B], ACT.Sqrt, bias=eps_c).then_inc(dev2, 1)

            move_by_w(0)
            act.wait_ge(t_done, 8)
            to_stage(a, 1, 1, ACT.Copy).then_inc(staged[1], 1)
            with act.Fori(0, NG - 1) as j:
                forward(j)
            forward(NG - 1, True)

            def square(s_):
                if s_ >= 2:
                    act.wait_ge(sq_summed, s_ - 1)
                buf = squares[s_ % 2]
                a(buf, chunk(s_ % 4), ACT.Square).then_inc(sq_done, 1)
                if s_ % 4 == 0:
                    act.wait_ge(sq_done, s_ + 1 + s_ // 4)
                    a(buf[0:C, 0:B], buf[0:C, 0:B], ACT.Copy, scale=0.5).then_inc(sq_done, 1)

            act.wait_ge(h_dve, 3 * NG)
            act.wait_ge(stat2, B + 8)
            for c in range(4):
                if c >= 2:
                    act.wait_ge(l2_done, c - 1)
                for m in range(HM):
                    act.wait_ge(*((l2_pos, 3 * c + m + 1) if m < 3 else (l2_pool, c + 1)))
                    negative(a, c % 2, m).then_inc(l2_neg, 1)
                square(c)
            act.wait_ge(l2_done, 4)
            for m in range(HM):
                a(l2_copy[C * m:C * m + C, :].rearrange("p (k r b) -> p k r b", r=2, b=B), low_result(3, m),
                  ACT.Copy).then_inc(l2_moved, 1)
            act.wait_ge(l2_added, L2_ADDED)
            act.wait_ge(l2_pool_added, len(ON_POOL))
            for s_ in range(4, 8):
                square(s_)
            act.wait_ge(stat3, STAT3 - 2)
            a(rstd_in[:, 0:B], var[:, 0:B], ACT.Sqrt, bias=eps_c).then_inc(dev3, 1)

            def negatives(s_, slot):
                for m in range(HM):
                    act.wait_ge(*((pos_ready, s_ * 3 + (m + 1)) if m < 3 else (pos_pool, s_ + 1)))
                    negative(a, slot, m).then_inc(neg_ready, 1)

            def move_y(c, i, need):
                act.wait_ge(mix_done, need)
                a(chunk(c), psum[:, i, :], ACT.Copy).then_inc(y_moved, 1)

            def full(q):
                for i in range(4):
                    negatives(q * 4 + (i + 1), (i + 1) % 4)
                    if i == 0:
                        move_y(q * 4 - 1, 3, q * 4 + 1)
                    else:
                        move_y(q * 4 + (i - 1), i - 1, q * 4 + (i + 1))

            for i in range(4):
                negatives(i, i)
                if i > 0:
                    move_y(i - 1, i - 1, i)
            act.wait_ge(mix_done, 1)
            negatives(4, 0)
            with act.Fori(1, NCHUNK // 8) as q:
                full(q)
            src = psum[0:C, 4:8, :].rearrange("p n (k r m) -> p (n k) r m", k=4, r=2)
            nyq_v = nyq[0:C, :].rearrange("p (r q k b) -> p r q k b", r=2, q=4, b=B)
            for ri in range(2):
                a(nyq_v[:, ri].rearrange("p q k b -> p k q b"),
                  src[:, :, ri, :].rearrange("p k (q b) -> p k q b", b=B), ACT.Copy).then_inc(nyq_moved, 1)
            with act.Fori(NCHUNK // 8, NCHUNK // 4) as q:
                full(q)
            move_y(NCHUNK - 1, 3, NCHUNK + 1)
            def move_transposes(j, order):
                for i, n in enumerate(order):
                    if i in BY_ACT:
                        act.wait_ge(a_done, j * 8 + (i + 1))
                        a(by_kh[:, 512 * n:512 * n + 512], psum[:, n, :], ACT.Copy).then_inc(a_act, 1)

            def move_kh(j):
                for k in range(4):
                    act.wait_ge(b_done, j * 8 + (2 * k + 2))
                    for ri in range(2):
                        to_kw(a, k, 0, ri, ACT.Copy).then_inc(b_act, 1)

            yv = ystage.rearrange("p (n b) -> p n b", b=GB)
            sv_ = spec[:, :].rearrange("p (n b) -> p n b", b=B)
            move_transposes(0, T_ORDER)
            a(yv[:, 0:512], sv_[:, 0:512, GB:2 * GB], ACT.Copy).then_inc(ystaged, 1)
            with act.Fori(0, NG - 1) as j:
                move_kh(j)
                move_transposes(j + 1, range(8))
            move_kh(NG - 1)

        @block.vector
        def _(dve):
            v = nc.vector

            def chain(norm, lo, n, base):
                half_sem, stat_sem, sum_sem, dev_sem, bnv, mv_, gs_, sq_, var_, dev_in, bank, scale, shifted = norm
                cols = slice(lo, lo + n)
                m = mv_.rearrange("p (u k) -> p u k", k=2)[:, cols]
                g = gs_.rearrange("p (u k) -> p u k", k=2)[:, cols]
                q = sq_[:, cols]
                count = [0]

                def step(ins):
                    count[0] += 1
                    ins.then_inc(stat_sem, 1)

                def settle():
                    dve.wait_ge(stat_sem, base + count[0])

                def to_mean(halves):
                    dve.wait_ge(half_sem, halves)
                    step(v.memset(q, 0.0))
                    for u in range(lo, lo + n):
                        step(v.bn_aggr(mv_[:, 2 * u:2 * u + 2], bnv[:, 12 * u:12 * u + 12]))
                    settle()
                    step(v.tensor_tensor(q, m[:, :, 0], m[:, :, 0], ALU.mult))
                    settle()
                    step(v.tensor_tensor(m[:, :, 1], m[:, :, 1], q, ALU.add))
                    assert count[0] == steps_mean(n)

                def to_var(sums):
                    dve.wait_ge(sum_sem, sums)
                    step(v.tensor_copy(gs_[:, 2 * lo:2 * (lo + n)], psum[:, bank, 2 * lo:2 * (lo + n)]))
                    settle()
                    step(v.tensor_tensor(q, g[:, :, 0], g[:, :, 0], ALU.mult))
                    settle()
                    step(v.tensor_tensor(var_[:, cols], g[:, :, 1], q, ALU.subtract))
                    assert count[0] == steps_var(n)

                def to_scale(devs):
                    dve.wait_ge(dev_sem, devs)
                    step(v.reciprocal(scale[:, cols], dev_in[:, cols]))
                    settle()
                    step(v.scalar_tensor_tensor(out=shifted[:, cols], in0=g[:, :, 0], scalar=-1.0, in1=scale[:, cols],
                                                op0=ALU.mult, op1=ALU.mult))
                    settle()
                    assert count[0] == steps_all(n)

                return to_mean, to_var, to_scale

            norm0 = (half0, stat0, sum0, dev0, bn0, mv0, gs0, sq0, var0, rstd_in0, 7, sc0, sh0)
            norm1 = (half1, stat1, sum1, dev1, bn1, mv1, gs1, sq1, var1, rstd_in1, 6, sc1, sh1)

            def half_stats(bnv, half_sem, j, u):
                for k in (2 * u, 2 * u + 1):
                    at_ = 6 * (k % 8)
                    v.bn_stats(bnv[:, at_:at_ + 6],
                               image[:, ds(j * (GB * ROWS) + 512 * k, 512)]).then_inc(half_sem, 1)

            def normalise(j, u, first):
                if not (first and u < 2):
                    dve.wait_ge(conv_done, j * 8 + 2 * (u - 1))
                xn = padded[u % 2].rearrange("p (h w) -> p h w", w=PADW)
                v.tensor_scalar(xn[:, :, 1:1 + W],
                                image[:, ds(j * (GB * ROWS) + u * ROWS, ROWS)].rearrange("p (h w) -> p h w", w=W),
                                sc0[:, u:u + 1], sh0[:, u:u + 1], ALU.mult, ALU.add).then_inc(padded_ready, 1)

            def add_conv(j, u):
                for half in range(2):
                    dve.wait_ge(conv_done, j * 8 + (2 * u + half + 1))
                    part = image[:, ds(j * (GB * ROWS) + (2 * u + half) * 512, 512)]
                    v.scalar_tensor_tensor(out=part, in0=psum[:, (2 * u + half) % 4, :], scalar=bias_c[:, 0:1],
                                           in1=part, op0=ALU.add, op1=ALU.add).then_inc(conv_added, 1)

            def conv_group(j, first, last):
                before1 = chain(norm1, 0, GB, (j - 1) * KGN) if not first else None
                next0 = chain(norm0, 0, GB, (j + 1) * KGN + EXTRA0) if not last else None
                for u in range(GB):
                    if u < GB - 1:
                        normalise(j, u + 1, first)
                    elif not last:
                        next0[1](j + 3)
                    if u == 1 and not first:
                        before1[1](j)
                    if first and u == 1:
                        dve.wait_ge(conv_b_in, 16 * HM)
                    if not (first and u == 0):
                        add_conv(j, u - 1)
                        if not (first and u == 1):
                            dve.wait_ge(carried, j * GB + (u - 1))
                        dve.wait_ge(conv_added, j * 8 + 2 * u)
                        v.memset(carrier, 0.0).then_inc(carried, 1)
                        half_stats(bn1, half1, *((j - 1, GB - 1) if u == 0 else (j, u - 1)))
                    if u < GB - 1 and not last:
                        for i in ((0,), (1, 2), (3,))[u]:
                            half_stats(bn0, half0, j + 1, i)
                    if u == 0 and not first:
                        before1[0](j * 8)
                    if u == 1 and not first:
                        before1[2](j)
                    if u == 2 and not last:
                        next0[0](j * 8 + 16)
                    if u == GB - 1 and not last:
                        next0[2](j + 3)
                        normalise(j + 1, 0, False)

            v.memset(conv_m[:, :], 0.0).then_inc(conv_zeroed, 1)
            v.memset(eps_c, EPS).then_inc(eps_set, 1)
            for i in range(2):
                xn = padded[i].rearrange("p (h w) -> p h w", w=PADW)
                v.memset(xn[:, :, 0:1], 0.0).then_inc(pads_zeroed, 1)
                v.memset(xn[:, :, PADW - 1:PADW], 0.0).then_inc(pads_zeroed, 1)
                v.memset(edges[i], 0.0).then_inc(pads_zeroed, 1)
                v.memset(sedge[i], 0.0).then_inc(pads_zeroed, 1)
            dve.wait_ge(x_first[0], 16)
            half_stats(bn0, half0, 0, 0)
            one, rest = chain(norm0, 0, 1, 0), chain(norm0, 1, GB - 1, steps_all(1))
            one[0](2)
            dve.wait_ge(x_first[1], 16)
            half_stats(bn0, half0, 0, 1)
            one[1](1)
            dve.wait_ge(pads_zeroed, 8)
            one[2](1)
            normalise(0, 0, True)
            for u in range(2, GB):
                dve.wait_ge(x_first[u], 16)
                half_stats(bn0, half0, 0, u)
            rest[0](8)
            rest[1](2)
            rest[2](2)
            dve.wait_ge(x_in[1], 16)
            conv_group(0, True, False)
            for j in range(2, NG):
                dve.wait_ge(x_in[j], 16)
            with dve.Fori(1, NG - 1) as j:
                conv_group(j, False, False)
            conv_group(NG - 1, False, True)
            three, one = chain(norm1, 0, GB - 1, (NG - 1) * KGN), chain(norm1, GB - 1, 1, (NG - 1) * KGN + steps_all(GB - 1))
            three[0](8 * NG - 2)
            add_conv(NG - 1, GB - 1)
            dve.wait_ge(conv_added, 2 * B)
            half_stats(bn1, half1, NG - 1, GB - 1)
            three[1](NG)
            dve.wait_ge(columns_ready, B - GB)
            three[2](NG)
            one[0](8 * NG)
            one[1](NG + 1)
            one[2](NG + 1)
            to_cols(v.tensor_scalar, NG - 1, GB - 1, slice(W // 2, W), sc1[:, GB - 1:GB], sh1[:, GB - 1:GB],
                    ALU.mult, ALU.add).then_inc(last_columns, 1)

            dve.wait_ge(small_in, 16 * 8)
            v.tensor_tensor(bias_rz, bias_s[:, 0:2], bias_s[:, 3:5], ALU.add).then_inc(bias_ready, 1)
            for h in range(2):
                if h == 1:
                    dve.wait_ge(columns_ready, B)
                v.tensor_copy(state[h], columns[:, h * HB:h * HB + HB]).then_inc(state_ready[h], 1)

            def new_state(h, w):
                dve.wait_ge(r_gate[h], w)
                v.scalar_tensor_tensor(out=pre1[h], in0=psum[:, 4 * h + 3, 0:HB], scalar=bias_s[:, 5:6], in1=gr[h],
                                       op0=ALU.add, op1=ALU.mult).then_inc(reset_done[h], 1)
                dve.wait_ge(n_sum[h], w)
                dve.wait_ge(reset_done[h], w)
                v.tensor_tensor(pre2[h], pre1[h], psum[:, 4 * h + 2, 0:HB], ALU.add).then_inc(pre_ready[h], 1)
                dve.wait_ge(z_gate[h], w)
                v.scalar_tensor_tensor(out=keep[h], in0=gz[h], scalar=1.0, in1=columns[:, ds(w * (2 * HB) + h * HB, HB)],
                                       op0=ALU.subtract, op1=ALU.mult).then_inc(keep_ready[h], 1)
                dve.wait_ge(n_gate[h], w)
                v.tensor_tensor(mix[h], gn[h], gz[h], ALU.mult).then_inc(mix_ready[h], 1)
                dve.wait_ge(mix_ready[h], w)
                dve.wait_ge(keep_ready[h], w)
                dve.wait_ge(added[h], w)
                dve.wait_ge(sedge_ready[h], w * 2)
                v.tensor_tensor(state[h], mix[h], keep[h], ALU.subtract).then_inc(state_ready[h], 1)

            with dve.Fori(1, W) as w:
                for h in range(2):
                    new_state(h, w)

            dve.wait_ge(added[0], W)
            to_stage(v.tensor_copy, 0, 0).then_inc(staged[0], 1)
            dve.wait_ge(added[1], W)

            n2 = [0]

            def step2(ins):
                n2[0] += 1
                ins.then_inc(stat2, 1)

            def settle2():
                dve.wait_ge(stat2, n2[0])

            m16 = mv.rearrange("p (b k) -> p b k", k=2)
            g16 = gs.rearrange("p (b k) -> p b k", k=2)

            def mean_of_all():
                dve.wait_ge(st2, 32)
                for b in range(B):
                    step2(v.bn_aggr(mv[:, 2 * b:2 * b + 2], bn[:, 12 * b:12 * b + 12]))
                settle2()
                step2(v.tensor_tensor(sq, m16[:, :, 0], m16[:, :, 0], ALU.mult))
                settle2()
                step2(v.tensor_tensor(m16[:, :, 1], m16[:, :, 1], sq, ALU.add))
                assert n2[0] == B + 2

            def variance_of_all():
                dve.wait_ge(sum2, 1)
                step2(v.tensor_copy(gs, psum[:, 1, 0:2 * B]))
                settle2()
                step2(v.tensor_tensor(sq, g16[:, :, 0], g16[:, :, 0], ALU.mult))
                settle2()
                step2(v.tensor_tensor(var, g16[:, :, 1], sq, ALU.subtract))
                assert n2[0] == B + 5

            def move_by_w(j):
                for n in BY_DVE:
                    dve.wait_ge(t_done, j * 8 + (n + 1))
                    v.tensor_copy(by_w[:, 512 * n:512 * n + 512], psum[:, n, :]).then_inc(t_dve, 1)

            def forward(j, last_group=False):
                for k in range(6):
                    dve.wait_ge(w_done, j * 6 + (k + 1))
                    for ri in range(2):
                        to_by_h(v.tensor_copy, k, 1, ri).then_inc(w_dve, 1)
                if not last_group:
                    move_by_w(j + 1)
                for k in range(8):
                    v.bn_stats(bn[:, ds(j * 48 + 6 * k, 6)],
                               image[:, ds(j * (GB * ROWS) + 512 * k, 512)]).then_inc(st2, 1)
                    if not last_group and k in (3, 5, 7):
                        dve.wait_ge(h_done, j * 9 + (k + 1))
                        to_spectrum(v.tensor_copy, j, k).then_inc(h_dve, 1)
                if last_group:
                    mean_of_all()
                    for n in (3, 5, 7):
                        dve.wait_ge(h_done, j * 9 + (n + 1))
                        to_spectrum(v.tensor_copy, j, n).then_inc(h_dve, 1)
                    variance_of_all()

            move_by_w(0)
            with dve.Fori(0, NG - 1) as j:
                forward(j)
            forward(NG - 1, True)

            dve.wait_ge(dev2, 1)
            step2(v.reciprocal(rstd, rstd_in))
            step2(v.tensor_scalar(shift, g16[:, :, 0], float(H * W), None, ALU.mult))
            dve.wait_ge(h_act, 6 * NG)
            dve.wait_ge(h_dve, 3 * NG)
            settle2()
            dc = spec[0:C, 0:B]
            step2(v.tensor_tensor(dc, dc, shift[0:C, :], ALU.subtract))
            settle2()
            assert n2[0] == B + 8
            dve.wait_ge(diag_zeroed, 2)
            for c in range(4):
                if c >= 2:
                    dve.wait_ge(l2_done, c - 1)
                for m in range(3):
                    positive(v.tensor_tensor, c % 2, m, chunk(c)).then_inc(l2_pos, 1)
            v.memset(delta, 0.0).then_inc(l2_added, 1)
            dve.wait_ge(l2_done, 4)
            dve.wait_ge(sq_done, 5)
            res = psum[:, 0:4, :].rearrange("p n (k r q b) -> p (n k) r q b", k=4, r=2, q=4)
            col0 = spec[0:C, 0:H * 4 * XT].rearrange("p (k t r b) -> p k t r b", t=4, r=2, b=B)[:, :, 0]
            o = res[0:C, :, :, 0, :]
            v.scalar_tensor_tensor(out=sq[0:C, :], in0=o[:, 0, 0, :], scalar=1.0, in1=shift[0:C, :],
                                   op0=ALU.mult, op1=ALU.add).then_inc(l2_added, 1)
            dve.wait_ge(l2_added, 2)
            v.tensor_tensor(dc, dc, sq[0:C, :], ALU.add).then_inc(l2_added, 1)
            dve.wait_ge(l2_added, 3)
            v.tensor_copy(delta[0:C, :], dc).then_inc(stat3, 1)
            half = col0[:, 1:MODES]
            for sign, ri, dst in ((0.5, 0, half[:, :, 0, :]), (0.5, 1, half[:, :, 1, :]),
                                  (0.5, 0, col0[:, H - 1:H - MODES:-1, 0, :]),
                                  (-0.5, 1, col0[:, H - 1:H - MODES:-1, 1, :])):
                v.scalar_tensor_tensor(out=dst, in0=o[:, 1:MODES, ri, :], scalar=sign, in1=dst,
                                       op0=ALU.mult, op1=ALU.add).then_inc(l2_added, 1)
            for t in range(4):
                for m in range(HM):
                    if (t, m) != (0, 0) and (t, m) not in ON_POOL:
                        add_low(v.tensor_tensor, t, m).then_inc(l2_added, 1)
            n3 = [1]

            def step3(ins):
                n3[0] += 1
                ins.then_inc(stat3, 1)

            def settle3():
                dve.wait_ge(stat3, n3[0])

            dve.wait_ge(sq_summed, 4)
            step3(v.tensor_reduce(energy, psum[:, 6, :].rearrange("p (n b) -> p b n", b=B),
                                  mybir.AxisListType.X, ALU.add))
            dve.wait_ge(sum3, 1)
            step3(v.tensor_scalar(mean, psum[:, 5, 0:B], 8.0 / (2 * H * W), None, ALU.mult))
            settle3()
            step3(v.scalar_tensor_tensor(out=energy, in0=energy, scalar=-ENERGY, in1=var, op0=ALU.mult, op1=ALU.add))
            step3(v.tensor_tensor(sq, mean, mean, ALU.mult))
            settle3()
            step3(v.tensor_tensor(energy, energy, sq, ALU.subtract))
            settle3()
            dve.wait_ge(sq_summed, 8)
            step3(v.tensor_reduce(sq, psum[:, 7, :].rearrange("p (n b) -> p b n", b=B),
                                  mybir.AxisListType.X, ALU.add))
            settle3()
            step3(v.scalar_tensor_tensor(out=var, in0=sq, scalar=ENERGY, in1=energy, op0=ALU.mult, op1=ALU.add))
            assert n3[0] == STAT3 - 2
            step3(v.scalar_tensor_tensor(out=dc, in0=mean[0:C, :], scalar=-float(H * W), in1=dc,
                                         op0=ALU.mult, op1=ALU.add))
            dve.wait_ge(dev3, 1)
            step3(v.reciprocal(rstd, rstd_in))
            settle3()

            def positives(s_, slot, columns_, need):
                if need is not None:
                    dve.wait_ge(mix_done, need)
                for m in range(3):
                    positive(v.tensor_tensor, slot, m, columns_).then_inc(pos_ready, 1)

            def full(q):
                for i in range(4):
                    positives(None, (i + 1) % 4, chunk(q * 4 + i), q * 4 + (i - 2))

            def symmetrise(ri, half_b, before):
                part = slice(half_b * (B // 2), (half_b + 1) * (B // 2))
                y0 = spec[0:C, 0:H * 4 * XT].rearrange("p (k r q b) -> p k r q b", r=2, q=4, b=B)[:, :, ri, 0, part]
                n32 = nyq[0:C, :].rearrange("p (r k b) -> p r k b", r=2, b=B)[:, 1 - ri, :, part]
                ts = t_sum[0:C, :].rearrange("p (k b) -> p k b", b=B // 2)
                back_ = slice(H - 1, 0, -1)
                mirror = ALU.add if ri == 0 else ALU.subtract
                v.tensor_tensor(ts[:, 1:H], y0[:, 1:H], y0[:, back_], mirror).then_inc(sym, 1)
                v.tensor_tensor(ts[:, 0:1], y0[:, 0:1], y0[:, 0:1], mirror).then_inc(sym, 1)
                dve.wait_ge(sym, before + 2)
                v.tensor_tensor(ts, ts, n32, ALU.subtract if ri == 0 else ALU.add).then_inc(sym, 1)
                dve.wait_ge(sym, before + 3)
                v.tensor_tensor(y0[:, 1:H], ts[:, 1:H], n32[:, back_], ALU.add).then_inc(sym, 1)
                v.tensor_tensor(y0[:, 0:1], ts[:, 0:1], n32[:, 0:1], ALU.add).then_inc(sym, 1)
                dve.wait_ge(sym, before + 5)

            dve.wait_ge(diag_zeroed, 4)
            for i in range(4):
                positives(i, i, chunk(i), None)
            positives(4, 0, spec9, 1)
            with dve.Fori(1, NCHUNK // 8 + 1) as q:
                full(q)
            dve.wait_ge(nyq_moved, 2)
            dve.wait_ge(y_moved, NCHUNK // 2)
            symmetrise(0, 0, 0)
            symmetrise(0, 1, 5)
            with dve.Fori(NCHUNK // 8 + 1, NCHUNK // 4 - 1) as q:
                full(q)
            symmetrise(1, 0, 10)
            symmetrise(1, 1, 15)
            full(NCHUNK // 4 - 1)
            def move_transposes(j, order):
                for i, n in enumerate(order):
                    if i in BY_DVE:
                        dve.wait_ge(a_done, j * 8 + (i + 1))
                        v.tensor_copy(by_kh[:, 512 * n:512 * n + 512], psum[:, n, :]).then_inc(a_dve, 1)

            def move_kh(j):
                for k in range(4):
                    dve.wait_ge(b_done, j * 8 + (2 * k + 2))
                    for ri in range(2):
                        to_kw(v.tensor_copy, k, 1, ri).then_inc(b_dve, 1)

            def add_result(j):
                for n in range(8):
                    dve.wait_ge(c_done, j * 8 + (n + 1))
                    for i in range(2):
                        part = images(j).rearrange("p (b h w) -> p h b w", b=GB, w=W)[:, 2 * n + i]
                        res = psum[:, n, 256 * i:256 * i + 256].rearrange("p (b w) -> p b w", b=GB)
                        v.scalar_tensor_tensor(out=part, in0=res, scalar=bias_o[:, 0:1], in1=part,
                                               op0=ALU.add, op1=ALU.add).then_inc(image_done, 1)

            yv = ystage.rearrange("p (n b) -> p n b", b=GB)
            sv_ = spec[:, :].rearrange("p (n b) -> p n b", b=B)
            move_transposes(0, T_ORDER)
            dve.wait_ge(y_moved, NCHUNK)
            v.tensor_copy(yv[:, 512:1024], sv_[:, 512:1024, GB:2 * GB]).then_inc(ystaged, 1)
            with dve.Fori(0, NG - 1) as j:
                move_kh(j)
                move_transposes(j + 1, range(8))
                add_result(j)
            move_kh(NG - 1)
            add_result(NG - 1)



def kernel(x, L0_conv_weight, L0_conv_bias, L1_conv_weight_ih, L1_conv_bias_ih, L1_conv_weight_hh,
           L1_conv_bias_hh, L2_conv_w_real, L2_conv_w_imag, L3_conv_kernel_re, L3_conv_kernel_im, L3_conv_bias):
    import concourse.bacc as bacc
    from concourse.bass_utils import run_bass_kernel_spmd

    def rows(a, n=P):
        return np.ascontiguousarray(a).reshape(n, -1)

    x_l = rows(np.asarray(x).reshape(B, C, H4, HM, W).transpose(3, 1, 0, 2, 4))
    conv_w = np.ascontiguousarray(np.asarray(L0_conv_weight)[:, :, ::-1].transpose(1, 3, 2, 0)).reshape(C, 3, 3 * C)
    wi = np.ascontiguousarray(np.asarray(L1_conv_weight_ih).reshape(3, C, 3, C)[:, :, ::-1].transpose(3, 0, 2, 1)).reshape(C, 3, 3 * C)
    wh = np.ascontiguousarray(np.asarray(L1_conv_weight_hh).reshape(3, C, C).transpose(2, 0, 1))
    sb_ = np.ascontiguousarray(np.concatenate([np.asarray(L1_conv_bias_ih).reshape(3, C),
                                               np.asarray(L1_conv_bias_hh).reshape(3, C)]).T)
    w2 = np.stack([np.asarray(L2_conv_w_real), np.asarray(L2_conv_w_imag)])
    w2 = rows(w2.reshape(2, C, C, MODES, 4, 4).transpose(5, 1, 3, 4, 0, 2))
    k = np.stack([np.asarray(L3_conv_kernel_re), np.asarray(L3_conv_kernel_im)])
    w3 = rows(k[..., :KW].reshape(2, C, C, H, 2, 4, 4).transpose(6, 2, 4, 3, 5, 0, 1))
    w9 = rows(k[..., KW].reshape(2, C, C, 4, 16).transpose(3, 2, 4, 0, 1))
    group, parts = constants()
    const = np.ascontiguousarray(np.concatenate([parts[n] for n in (*KEPT_COLS, *FORWARD_COLS)], 1))
    arrays = dict(x=x_l, conv_w=conv_w, conv_b=np.asarray(L0_conv_bias).reshape(C, 1), scan_wi=wi, scan_wh=wh,
                  scan_b=sb_, w2=w2, w3=w3, w9=w9, out_b=np.asarray(L3_conv_bias).reshape(C, 1),
                  group=group, const=const)
    nc = bacc.Bacc("TRN2", target_bir_lowering=False, num_devices=1)
    args = [nc.dram_tensor(f"{n}_dram", a.shape, F32, kind="ExternalInput").ap() for n, a in arrays.items()]
    args.append(nc.dram_tensor("out_dram", [P, B * ROWS], F32, kind="ExternalOutput").ap())
    program(nc, *args)
    r = run_bass_kernel_spmd(nc, [{f"{n}_dram": a for n, a in arrays.items()}], core_ids=[0])
    y = r.results[0]["out_dram"].reshape(HM, C, B, H4, W)
    return np.ascontiguousarray(y.transpose(2, 1, 3, 0, 4)).reshape(B, C, H, W)
```

```python
import numpy as np
import concourse.bass as bass
from concourse import mybir
from contextlib import ExitStack

F32 = mybir.dt.float32
ALU = mybir.AluOpType
ACT = mybir.ActivationFunctionType

B, C, H, W = 16, 32, 64, 64
HM = 4
H4 = H // HM
P = HM * C
ROWS = H4 * W
KW = W // 2
NYQ = W // 2 + 1
MODES = 16
GB = 4
NG = B // GB
TILE = 2 * HM * B
XT = 2 * B
CHUNK_T = 16
CHUNK = CHUNK_T * XT
NCHUNK = 2 * H * 4 // CHUNK_T
PLANES = 3 * HM * B
EPS = 1e-5
WARM_X, WARM_CONV_NORM, WARM_SCAN_END, WARM_OPERAND, WARM_SQUARES, WARM_NORM = 6, 8, 8, 16, 8, 16


def constants():
    ang = 2 * np.pi * np.outer(np.arange(64), np.arange(64)) / 64
    cos, sin = np.cos(ang), np.sin(ang)
    cos[np.abs(cos) < 1e-12] = 0
    sin[np.abs(sin) < 1e-12] = 0
    ident = np.eye(P)
    group = np.kron(np.ones((HM, HM)), np.kron(np.eye(C // 2), np.ones((2, 2)))) / (2 * HM)
    fw = np.zeros((2, W, 2, 2, NYQ))
    for b in range(2):
        fw[b, :, 0, b] = cos[:, :NYQ]
        fw[b, :, 1, b] = -sin[:, :NYQ]
    fh = np.stack([np.stack([cos, -sin], 1), np.stack([sin, cos], 1)])
    ih = np.stack([np.stack([cos, sin], 1), np.stack([-sin, cos], 1)], 1).reshape(P, P)
    p = np.arange(KW)
    kw = 16 * (p // 16) + 4 * (p % 4) + (p // 4) % 4
    scale = np.where(kw == 0, 0.5, 2.0)[:, None] / (H * W)
    back_r = cos[kw] * scale
    back_i = -sin[kw] * scale
    back_i[0] = 0.5 * (-1.0) ** np.arange(W) / (H * W)
    iw = np.concatenate([np.kron(np.eye(2), back_r), np.kron(np.eye(2), back_i)])
    parts = dict(ident=ident, fw=fw.reshape(P, -1), fh=fh.reshape(P, -1), ih=ih, iw=iw)
    return group.astype(np.float32), {k: v.astype(np.float32) for k, v in parts.items()}


KEPT_COLS = dict(ident=P, ih=P, iw=2 * W)
FORWARD_COLS = dict(fw=4 * NYQ, fh=2 * H)


def program(nc, x, conv_w, conv_b, scan_wi, scan_wh, scan_b, w2, w3, w9, out_b, group_d, const_d, out):
    ctx = ExitStack()
    with ctx:
        def sem(name):
            return ctx.enter_context(nc.semaphore(name))

        def sb(name, cols):
            return ctx.enter_context(nc.sbuf_tensor(name, [P, cols], F32))

        image = sb("image", B * ROWS)
        spec = sb("spec", 2 * H * 4 * XT)
        work = sb("work", B * ROWS + 128)
        kept = sb("kept", sum(KEPT_COLS.values()))
        nf = sum(FORWARD_COLS.values())
        matrices = sb("matrices", 2 * H * B + H * B // 2)
        forward_m = matrices[:, 0:nf]
        conv_m = matrices[:, nf:nf + 5 * P]
        scan_m = matrices[:, nf + 5 * P:nf + 14 * P]
        group_m = matrices[:, nf + 14 * P:nf + 15 * P]
        small = sb("small", 560)
        psum = ctx.enter_context(nc.psum_tensor("psum", [P, 8, 512], F32))

        cm = {}
        for buf, widths in ((kept, KEPT_COLS), (forward_m, FORWARD_COLS)):
            at = 0
            for k, n in widths.items():
                cm[k] = buf[:, at:at + n]
                at += n
        at = [0]

        def sm(n):
            at[0] += n
            return small[:, at[0] - n:at[0]]

        bn = sm(32 * 6)
        bn0, bn1 = bn[:, 0:48], bn[:, 48:96]
        mv0, gs0, mv1, gs1 = [bn[:, 96 + 8 * i:104 + 8 * i] for i in range(4)]
        carrier = bn[:, 152:153]
        sq0, var0, rstd_in0, sq1, var1, rstd_in1 = [bn[:, 128 + 4 * i:132 + 4 * i] for i in range(6)]
        mv = sm(32)
        gs = sm(32)
        sq = sm(16)
        mean, rstd, shift = sm(16), sm(16), sm(16)
        energy = sm(16)
        delta = sm(16)
        primed = sm(1)
        var, rstd_in = sm(16), sm(16)
        sc0, sh0, sc1, sh1 = sm(GB), sm(GB), sm(GB), sm(GB)
        bias_c, bias_o, eps_c = sm(1), sm(1), sm(1)
        bias_s = sm(6)
        bias_rz = sm(2)
        PADW = W + 2
        padded = [spec[:, i * H4 * PADW:(i + 1) * H4 * PADW] for i in range(2)]
        edges = [spec[:, (2 + i) * H4 * PADW:(3 + i) * H4 * PADW] for i in range(2)]
        HB = B * H4 // 2
        off = 4 * H4 * PADW

        def scan_buf():
            nonlocal off
            off += HB
            return spec[:, off - HB:off]

        state = [scan_buf() for _ in range(2)]
        sedge = [scan_buf() for _ in range(2)]
        gr, gz, gn, pre1, pre2, keep, mix = [[scan_buf() for _ in range(2)] for _ in range(7)]
        columns = work[:, 0:B * ROWS]
        stage = work[:, 0:4096]
        by_w = work[:, 4096:8192]
        by_h = work[:, 8192:8192 + C * 4 * NYQ]
        w2_m = work[:, 12416:16512]
        diag = [work[:, i * CHUNK_T * PLANES:(i + 1) * CHUNK_T * PLANES] for i in range(4)]
        w3_m = [w2_m[:, 1024 * i:1024 + 1024 * i] for i in range(4)]
        spec9 = conv_m[:, 0:16 * XT]
        squares = [diag[3][:, CHUNK * (i + 1):CHUNK * (i + 2)] for i in range(4)] \
            + [scan_m[:, CHUNK * (i % 2):CHUNK * (i % 2) + CHUNK] for i in range(4)]
        l2_copy = diag[3][:, 0:CHUNK]
        nyq = matrices[:, 0:2 * H * B]
        t_sum = matrices[:, 2 * H * B:2 * H * B + H * B // 2]
        ystage = work[:, 0:4096]
        by_kh = work[:, 4096:8192]
        by_kw = work[:, 8192:12288]

        x_first = [sem(f"x_first{u}") for u in range(GB)]
        x_in = [None] + [sem(f"x_in{j}") for j in range(1, NG)]
        conv_w_in, scan_w_in, group_in, const_in = map(sem, ("conv_w_in", "scan_w_in", "group_in", "const_in"))
        conv_b_in, small_in = sem("conv_b_in"), sem("small_in")
        w2_in = sem("w2_in")
        w3_in = [sem(f"w3_in{i}") for i in range(4)]
        conv_zeroed, scan_zeroed, pads_zeroed, eps_set = map(sem, ("conv_zeroed", "scan_zeroed", "pads_zeroed", "eps_set"))
        table_in = sem("table_in")
        half0, half1 = sem("half0"), sem("half1")
        carried = sem("carried")
        stat0, stat1 = sem("stat0"), sem("stat1")
        sum0, sum1 = sem("sum0"), sem("sum1")
        dev0, dev1 = sem("dev0"), sem("dev1")
        padded_ready, edges_ready = sem("padded_ready"), sem("edges_ready")
        conv_done, conv_added = sem("conv_done"), sem("conv_added")
        columns_ready, last_columns = sem("columns_ready"), sem("last_columns")
        bias_ready = sem("bias_ready")
        state_ready = [sem(f"state_ready{h}") for h in range(2)]
        sedge_ready = [sem(f"sedge_ready{h}") for h in range(2)]
        r_sum, z_sum, n_sum = [[sem(f"{g}_sum{h}") for h in range(2)] for g in "rzn"]
        r_gate, z_gate, n_gate = [[sem(f"{g}_gate{h}") for h in range(2)] for g in "rzn"]
        reset_done = [sem(f"reset_done{h}") for h in range(2)]
        pre_ready = [sem(f"pre_ready{h}") for h in range(2)]
        keep_ready = [sem(f"keep_ready{h}") for h in range(2)]
        mix_ready = [sem(f"mix_ready{h}") for h in range(2)]
        added = [sem(f"added{h}") for h in range(2)]
        staged = [sem(f"staged{q}") for q in range(2)]
        t_done, t_act, t_dve = sem("t_done"), sem("t_act"), sem("t_dve")
        w_done, w_act, w_dve = sem("w_done"), sem("w_act"), sem("w_dve")
        h_done, h_act, h_dve = sem("h_done"), sem("h_act"), sem("h_dve")
        half2 = sem("half2")
        stat2, sum2, dev2 = sem("stat2"), sem("sum2"), sem("dev2")
        stat3, sum3, dev3 = sem("stat3"), sem("sum3"), sem("dev3")
        diag_zeroed = sem("diag_zeroed")
        l2_pos, l2_pool, l2_neg = sem("l2_pos"), sem("l2_pool"), sem("l2_neg")
        l2_done, l2_moved = sem("l2_done"), sem("l2_moved")
        l2_added, l2_pool_added = sem("l2_added"), sem("l2_pool_added")
        sq_done, sq_summed = sem("sq_done"), sem("sq_summed")
        pos_ready, pos_pool, neg_ready = sem("pos_ready"), sem("pos_pool"), sem("neg_ready")
        mix_done, y_moved = sem("mix_done"), sem("y_moved")
        nyq_moved, sym = sem("nyq_moved"), sem("sym")
        ystaged = sem("ystaged")
        a_done, a_act, a_dve = sem("a_done"), sem("a_act"), sem("a_dve")
        b_done, b_act, b_dve = sem("b_done"), sem("b_act"), sem("b_dve")
        c_done, image_done = sem("c_done"), sem("image_done")
        stored = sem("stored")

        def steps_mean(n):
            return 1 + n + 2

        def steps_var(n):
            return steps_mean(n) + 3

        def steps_all(n):
            return steps_var(n) + 2

        KGN = steps_all(GB)
        EXTRA0 = steps_all(1) + steps_all(GB - 1) - KGN

        HALF_ADDED = 4 + 15 - 4
        L2_ADDED = 3 + 2 * HALF_ADDED
        STAT3 = 10
        ENERGY = 8.0 / (H * W) ** 2
        ds = bass.ds

        def images(j, n=GB):
            return image[:, ds(j * (GB * ROWS), n * ROWS)]

        def to_cols(op, j, u, cols, *func, **kw_):
            dst = columns.rearrange("p (w b h) -> p w b h", b=B, h=H4)[:, cols, ds(j * GB + u, 1), :] \
                .rearrange("p w o h -> p (o h) w")
            src = image[:, ds(j * (GB * ROWS) + u * ROWS, ROWS)].rearrange("p (h w) -> p h w", w=W)[:, :, cols]
            return op(dst, src, *func, **kw_)

        def to_stage(copy, j, q, *func, rows_=slice(0, H4)):
            src = images(j)[:, q * 2 * ROWS:(q + 1) * 2 * ROWS].rearrange("p (b h w) -> p b h w", b=2, w=W)
            dst = stage[:, q * 2 * ROWS:(q + 1) * 2 * ROWS].rearrange("p (h b w) -> p b h w", b=2, w=W)
            return copy(dst[:, :, rows_], src[:, :, rows_], *func)

        def to_by_h(copy, k, q, ri, *func):
            banks, chans = (2, 3) if k < 5 else (1, 2)
            at_ = (2 * k + 4) % 8
            src = psum[H * q:H * q + H, at_:at_ + banks, 0:4 * NYQ * chans] \
                .rearrange("p n (c r m) -> p n c r m", c=chans, r=2)[:, :, :, ri]
            dst = by_h[H * ri:H * ri + H, :].rearrange("p (q m c) -> p q m c", q=2, c=C)[:, q, :, 6 * k:6 * k + banks * chans] \
                .rearrange("p m (n c) -> p n c m", n=banks)
            return copy(dst, src, *func)

        def to_spectrum(copy, j, n, *func):
            if n < 8:
                g, t = n // 4, n % 4
                src = psum[:, n, :].rearrange("p (b r k) -> p b r k", b=GB, r=2)
                dst = spec[:, :].rearrange("p (g k t r b) -> p g t b r k", g=2, k=H, t=4, r=2)
                dst = dst[:, g, t, ds(j * GB, GB)]
            else:
                src = psum[:, 0, 0:2 * 16 * GB].rearrange("p (b r k) -> p b r k", b=GB, r=2)
                dst = spec9.rearrange("p (k r b) -> p b r k", k=16, r=2)[:, ds(j * GB, GB)]
            return copy(dst, src, *func)

        def positive(multiply, slot, m, columns_):
            src = columns_[C * m:C * m + C, :].rearrange("p (t r b) -> p t r b", r=2, b=B)
            dst = diag[slot][C * m:C * m + C, :].rearrange("p (t k q b) -> p t k q b", k=3, q=4, b=B)[:, :, 1:3, m, :]
            scale = rstd[C * m:C * m + C, :].unsqueeze(1).unsqueeze(1).broadcast_to([C, CHUNK_T, 2, B])
            return multiply(dst, src, scale, ALU.mult)

        def negative(activation, slot, m):
            d = diag[slot][C * m:C * m + C, :].rearrange("p (t k q b) -> p t k q b", k=3, q=HM, b=B)
            return activation(d[:, :, 0, m, :], d[:, :, 2, m, :], ACT.Copy, scale=-1.0)

        def chunk(c):
            return spec[:, ds(c * CHUNK, CHUNK)]

        def low_result(t, m, half):
            return psum[C * t:C * t + C, 2 * half:2 * half + 2, :] \
                .rearrange("p n (k r q b) -> p (n k) r q b", k=4, r=2, q=4)[:, :, :, m, :]

        def low_copy(m, half):
            return l2_copy[C * m:C * m + C, half * CHUNK // 2:(half + 1) * CHUNK // 2] \
                .rearrange("p (k r b) -> p k r b", r=2, b=B)

        def add_low(add, t, m, half):
            res = low_copy(m, half) if t == 3 else low_result(t, m, half)
            low = spec[C * m:C * m + C, 2 * half * CHUNK:2 * (half + 1) * CHUNK] \
                .rearrange("p (k t r b) -> p k t r b", t=4, r=2, b=B)[:, :, t]
            return add(low, low, res, ALU.add)

        ON_POOL = [(3, m) for m in range(HM)]

        BY_ACT, BY_DVE = (0, 1, 3, 4, 6, 7), (2, 5)
        T_ORDER = (4, 6, 0, 2, 5, 7, 1, 3)

        def to_kw(copy, k, x_, ri, *func):
            src = psum[H * x_:H * x_ + H, 2 * k:2 * k + 2, :].rearrange("p n (o r h) -> p (n o) r h", o=4, r=2)[:, :, ri]
            dst = by_kw[H * ri:H * ri + H, :].rearrange("p (x h o) -> p x o h", x=2, o=C)[:, x_, 8 * k:8 * k + 8]
            return copy(dst, src, *func)

        block = ctx.enter_context(nc.Block())

        @block.sync
        def _(sp):
            for u in range(GB):
                sp.dma_start(image[:, u * ROWS:(u + 1) * ROWS], x[:, u * ROWS:(u + 1) * ROWS]).then_inc(x_first[u], 16)
            sp.wait_ge(conv_w_in, 16 * 8)
            for j in range(1, NG):
                sp.dma_start(images(j), x[:, j * GB * ROWS:(j + 1) * GB * ROWS]).then_inc(x_in[j], 16)
            sp.wait_ge(scan_zeroed, 1)
            sv = scan_m[:, :].rearrange("p (k m) -> p k m", m=P)
            for hi in range(HM):
                lo, up = max(0, hi - 1), min(HM, hi + 2)
                sp.dma_start(sv[C * hi:C * hi + C, 0:3, C * lo:C * up],
                             scan_wi[:, :, C * (lo - hi + 1):C * (up - hi + 1)]).then_inc(scan_w_in, 16)
                sp.dma_start(sv[C * hi:C * hi + C, 6:9, C * hi:C * hi + C], scan_wh).then_inc(scan_w_in, 16)
            sp.dma_start(sv[0:C, 3:6, 0:C], scan_wi[:, :, 2 * C:3 * C]).then_inc(scan_w_in, 16)
            sp.dma_start(sv[C:2 * C, 3:6, P - C:P], scan_wi[:, :, 0:C]).then_inc(scan_w_in, 16)
            sp.dma_start(kept[:, :], const_d[:, 0:sum(KEPT_COLS.values())]).then_inc(const_in, 16)
            sp.dma_start(forward_m, const_d[:, sum(KEPT_COLS.values()):]).then_inc(const_in, 16)
            sp.wait_ge(state_ready[0], W)
            sp.wait_ge(state_ready[1], W)
            sp.dma_start(w2_m, w2).then_inc(w2_in, 16)
            for i in range(4):
                sp.wait_ge(l2_done, i + 1)
                sp.dma_start(w3_m[i], w3[:, i * 1024:(i + 1) * 1024]).then_inc(w3_in[i], 16)
            sp.wait_ge(mix_done, 1)
            sp.dma_start(w3_m[0], w9).then_inc(w3_in[0], 16)
            with sp.Fori(1, NCHUNK // 4) as q:
                for i in range(4):
                    sp.wait_ge(mix_done, q * 4 + (i - 2))
                    slot = (i + 1) % 4
                    sp.dma_start(w3_m[slot], w3[:, ds(q * 4096 + i * 1024, 1024)]).then_inc(w3_in[slot], 16)
            with sp.Fori(0, NG - 1) as j:
                sp.wait_ge(image_done, j * 16 + 16)
                sp.dma_start(out[:, ds(j * (GB * ROWS), GB * ROWS)], images(j)).then_inc(stored, 16)
            last = (NG - 1) * GB * ROWS
            for i in range(4):
                sp.wait_ge(image_done, (NG - 1) * 16 + 4 * (i + 1))
                band = [t[:, last:last + GB * ROWS].rearrange("p (b i m) -> p b i m", b=GB, i=4)[:, :, i] for t in (out, image)]
                sp.dma_start(band[0], band[1]).then_inc(stored, 16)
            sp.wait_ge(stored, 16 * (NG + 3))

        @block.gpsimd
        def _(pool):
            pool.dma_start(group_m[:, :], group_d).then_inc(group_in, 16)
            for hm in range(HM):
                q = slice(C * hm, C * hm + C)
                pool.dma_start(bias_c[q, :], conv_b).then_inc(conv_b_in, 16)
            for hm in range(HM):
                q = slice(C * hm, C * hm + C)
                pool.dma_start(bias_o[q, :], out_b).then_inc(small_in, 16)
                pool.dma_start(bias_s[q, :], scan_b).then_inc(small_in, 16)
            nc.gpsimd.memset(scan_m[:, :], 0.0).then_inc(scan_zeroed, 1)
            with pool.Fori(0, W) as w:
                for h in range(2):
                    pool.wait_ge(state_ready[h], w + 1)
                    col = image[:, h * (B // 2 * ROWS):(h + 1) * (B // 2 * ROWS)] \
                        .rearrange("p (n w) -> p n w", w=W)[:, :, ds(w, 1)]
                    nc.gpsimd.tensor_tensor(col, col, state[h].unsqueeze(2), ALU.add).then_inc(added[h], 1)
            pool.wait_ge(t_done, 8)
            to_stage(nc.gpsimd.tensor_copy, 1, 0).then_inc(staged[0], 1)
            with pool.Fori(2, NG) as j:
                pool.wait_ge(t_done, j * 8)
                for q in range(2):
                    to_stage(nc.gpsimd.tensor_copy, j, q).then_inc(staged[q], 1)
            pool.wait_ge(w_done, 6 * NG)
            for i in range(2):
                nc.gpsimd.memset(diag[i], 0.0).then_inc(diag_zeroed, 1)
            pool.wait_ge(diag_zeroed, 2)
            pool.wait_ge(h_act, 6 * NG)
            pool.wait_ge(h_dve, 3 * NG)
            pool.wait_ge(stat2, B + 8)
            for c in range(4):
                if c >= 2:
                    pool.wait_ge(l2_done, c - 1)
                positive(nc.gpsimd.tensor_tensor, c % 2, 3, chunk(c)).then_inc(l2_pool, 1)
            for half in range(2):
                pool.wait_ge(l2_moved, HM * (half + 1))
                pool.wait_ge(sq_done, 2 * half + 3)
                for i, (t, m) in enumerate(ON_POOL):
                    pool.wait_ge(*((l2_pool_added, half * HM + i) if i or half else (l2_pool, 4)))
                    add_low(nc.gpsimd.tensor_tensor, t, m, half).then_inc(l2_pool_added, 1)
            pool.wait_ge(l2_pool_added, HM * 2)
            nc.gpsimd.memset(diag[2], 0.0).then_inc(diag_zeroed, 1)
            pool.wait_ge(sq_summed, 4)
            nc.gpsimd.memset(diag[3], 0.0).then_inc(diag_zeroed, 1)
            pool.wait_ge(diag_zeroed, 4)
            pool.wait_ge(l2_added, L2_ADDED)
            pool.wait_ge(stat3, STAT3)
            for s_ in range(5):
                if s_ == 4:
                    pool.wait_ge(mix_done, 1)
                positive(nc.gpsimd.tensor_tensor, s_ % 4, 3, spec9 if s_ == 4 else chunk(s_)).then_inc(pos_pool, 1)
            with pool.Fori(1, NCHUNK // 4) as q:
                for i in range(4):
                    pool.wait_ge(mix_done, q * 4 + (i - 2))
                    positive(nc.gpsimd.tensor_tensor, (i + 1) % 4, 3, chunk(q * 4 + i)).then_inc(pos_pool, 1)
            pool.wait_ge(y_moved, NCHUNK)
            pool.wait_ge(sym, 20)
            pool.wait_ge(pos_pool, NCHUNK + 1)
            with pool.Fori(2, NG) as j:
                pool.wait_ge(a_done, j * 8)
                nc.gpsimd.tensor_copy(ystage.rearrange("p (n b) -> p n b", b=GB),
                                      spec[:, :].rearrange("p (n b) -> p n b", b=B)[:, :, ds(j * GB, GB)]
                                      ).then_inc(ystaged, 1)

        @block.tensor
        def _(pe):
            mm = nc.tensor.matmul
            cv = conv_m[:, :].rearrange("p (k m) -> p k m", m=P)
            sv = scan_m[:, :].rearrange("p (k m) -> p k m", m=P)

            def keep_warm(n, data):
                for _ in range(n):
                    mm(psum[:, 4, 0:P], data, data, start=True, stop=True)

            def sum0_of(lo, n, need):
                pe.wait_ge(stat0, need)
                mm(psum[:, 7, 2 * lo:2 * (lo + n)], group_m[:, :], mv0[:, 2 * lo:2 * (lo + n)],
                   start=True, stop=True).then_inc(sum0, 1)

            def sum1_of(lo, n, need):
                pe.wait_ge(stat1, need)
                mm(psum[:, 6, 2 * lo:2 * (lo + n)], group_m[:, :], mv1[:, 2 * lo:2 * (lo + n)],
                   start=True, stop=True).then_inc(sum1, 1)

            def conv_group(j, first, last):
                for u in range(GB):
                    if u == 1 and not first:
                        sum1_of(0, GB, (j - 1) * KGN + steps_mean(GB))
                    if u == 3 and not last:
                        sum0_of(0, GB, (j + 1) * KGN + (EXTRA0 + steps_mean(GB)))
                    xn = padded[u % 2].rearrange("p (h w) -> p h w", w=PADW)
                    en = edges[u % 2].rearrange("p (h w) -> p h w", w=PADW)
                    pe.wait_ge(padded_ready, j * GB + (u + 1))
                    for half in range(2):
                        n = 2 * u + half
                        if not (first and n < 4):
                            pe.wait_ge(conv_added, j * 8 + (n - 3))
                        for kx in range(3):
                            mm(psum[:, n % 4, :], cv[:, kx, :], xn[:, 8 * half:8 * half + 8, kx:kx + W],
                               start=kx == 0, stop=False)
                    if first and u == 0:
                        sum0_of(1, GB - 1, steps_all(1) + steps_mean(GB - 1))
                    pe.wait_ge(edges_ready, j * (4 * GB) + 4 * (u + 1))
                    for half in range(2):
                        n = 2 * u + half
                        mm(psum[:, n % 4, :], cv[:, 3, :], en[:, 8 * half:8 * half + 8, 0:W],
                           start=False, stop=False)
                        mm(psum[:, n % 4, :], cv[:, 4, :], en[:, 8 * half:8 * half + 8, 2:2 + W],
                           start=False, stop=True).then_inc(conv_done, 1)

            pe.wait_ge(group_in, 16)
            sum0_of(0, 1, steps_mean(1))
            pe.wait_ge(pads_zeroed, 8)
            keep_warm(WARM_X, sedge[0])
            pe.wait_ge(conv_w_in, 16 * 8)
            conv_group(0, True, False)
            with pe.Fori(1, NG - 1) as j:
                conv_group(j, False, False)
            conv_group(NG - 1, False, True)
            sum1_of(0, GB - 1, (NG - 1) * KGN + steps_mean(GB - 1))
            keep_warm(WARM_CONV_NORM, group_m)
            sum1_of(GB - 1, 1, (NG - 1) * KGN + steps_all(GB - 1) + steps_mean(1))
            keep_warm(WARM_CONV_NORM, group_m)

            def from_column(h, w):
                for g, bank in ((0, 0), (1, 1), (2, 3)):
                    mm(psum[:, 4 * h + bank, 0:HB], sv[:, 6 + g, :], columns[:, ds(w * (2 * HB) + h * HB, HB)],
                       start=True, stop=bank == 3)

            def banks_free(h, w):
                pe.wait_ge(r_gate[h], w - 1)
                pe.wait_ge(z_gate[h], w - 1)
                pe.wait_ge(reset_done[h], w - 1)

            def from_state(h, w):
                pe.wait_ge(state_ready[h], w)
                for g in (0, 2, 1):
                    mm(psum[:, 4 * h + g, 0:HB], sv[:, g, :], state[h], start=g == 2, stop=False)
                pe.wait_ge(sedge_ready[h], w * 2)
                for g, s in ((0, r_sum), (2, n_sum), (1, z_sum)):
                    mm(psum[:, 4 * h + g, 0:HB], sv[:, 3 + g, :], sedge[h], start=False, stop=True).then_inc(s[h], 1)

            pe.wait_ge(scan_w_in, 16 * 10)
            pe.wait_ge(columns_ready, B // 2)
            pe.wait_ge(conv_added, 2 * B)
            from_column(0, 1)
            from_state(0, 1)
            pe.wait_ge(columns_ready, B)
            pe.wait_ge(last_columns, 1)
            pe.wait_ge(stat1, (NG - 1) * KGN + steps_all(GB - 1) + steps_all(1))
            from_column(1, 1)
            from_state(1, 1)
            banks_free(0, 2)
            from_column(0, 2)

            def scan_step(w):
                from_state(0, w)
                banks_free(1, w)
                from_column(1, w)
                from_state(1, w)
                banks_free(0, w + 1)
                from_column(0, w + 1)

            with pe.Fori(0, (W - 4) // 4) as i:
                for k in range(4):
                    scan_step(i * 4 + (k + 2))
            scan_step(W - 2)
            from_state(0, W - 1)
            banks_free(1, W - 1)
            from_column(1, W - 1)
            from_state(1, W - 1)

            bw = by_w.rearrange("p (q h c) -> p q h c", q=2, c=C)
            bh = by_h.rearrange("p (b k c) -> p b k c", b=GB, c=C)
            sg = stage.rearrange("p (q h b w) -> p q h b w", q=2, b=2, w=W)
            pe.wait_ge(const_in, 32)
            pe.wait_ge(r_gate[1], W - 1)
            keep_warm(WARM_SCAN_END, cm["ident"])
            for h in range(2):
                pe.wait_ge(z_gate[h], W - 1)
                pe.wait_ge(pre_ready[h], W - 1)

            def transposes(j, first=False):
                for n in range(8):
                    if first and n % 2 == 0 and n < 4:
                        pe.wait_ge(staged[0], 1 + n // 2)
                    elif n % 4 == 0:
                        pe.wait_ge(staged[n // 4], j + (2 if n == 0 else 1))
                    if not first and n % 2 == 0:
                        pe.wait_ge(w_act, j * 12 + (n - 6))
                        pe.wait_ge(w_dve, j * 12 + (n - 6))
                    for i in range(4):
                        h4 = 4 * (n % 4) + i
                        last = nc.tensor.transpose(psum[:, n, P * i:P * i + P], sg[:, n // 4, h4, :, :], cm["ident"])
                    last.then_inc(t_done, 1)

            def over_w(j, first):
                pe.wait_ge(t_act, j * 6 + 6)
                pe.wait_ge(t_dve, j * 2 + 2)
                for k in range(6):
                    if not first and k < 3:
                        pe.wait_ge(h_act, j * 6 + (k - 2))
                        if k < 2:
                            pe.wait_ge(h_dve, j * 3 + (k - 1))
                    if k >= 4:
                        pe.wait_ge(w_act, j * 12 + 2 * (k - 3))
                        pe.wait_ge(w_dve, j * 12 + 2 * (k - 3))
                    for c in range(6 * k, min(6 * k + 6, C)):
                        last = mm(psum[:, (c // 3 + 4) % 8, 132 * (c % 3):132 * (c % 3) + 132], bw[:, :, :, c], cm["fw"],
                                  start=True, stop=True)
                    last.then_inc(w_done, 1)

            def over_h(j, last_group=False):
                pe.wait_ge(w_act, j * 12 + 12)
                pe.wait_ge(w_dve, j * 12 + 12)
                for n in range(8):
                    if not last_group:
                        if n in BY_DVE:
                            pe.wait_ge(t_dve, j * 2 + (3 + BY_DVE.index(n)))
                        else:
                            pe.wait_ge(t_act, j * 6 + (7 + BY_ACT.index(n)))
                    for b in range(GB):
                        last = mm(psum[:, n, 2 * H * b:2 * H * b + 2 * H], bh[:, b, 4 * n:4 * n + 4, :], cm["fh"],
                                  start=True, stop=True)
                    last.then_inc(h_done, 1)
                if last_group:
                    pe.wait_ge(h_act, j * 6 + 2)
                    pe.wait_ge(stat2, B + 2)
                    mm(psum[:, 1, 0:2 * B], group_m, mv, start=True, stop=True).then_inc(sum2, 1)
                pe.wait_ge(h_act, j * 6 + 1)
                fh = cm["fh"].rearrange("p (r k) -> p r k", r=2)
                for b in range(GB):
                    for q in range(4):
                        last = mm(psum[C * q:C * q + C, 0, 32 * b:32 * b + 32], bh[:, b, KW, :],
                                  fh[:, :, 16 * q:16 * q + 16], start=True, stop=True)
                last.then_inc(h_done, 1)

            transposes(0, True)
            over_w(0, True)
            transposes(1)
            over_h(0)
            with pe.Fori(1, NG - 1) as j:
                over_w(j, False)
                transposes(j + 1)
                over_h(j)
            over_w(NG - 1, False)
            over_h(NG - 1, True)


            def tiles(weights, planes, bank, done, starts=True):
                wt = weights.rearrange("p (t r o) -> p t r o", r=2, o=C)
                pl = planes.rearrange("p (t m) -> p t m", m=PLANES)
                for k in range(CHUNK_T // 4):
                    for r, from_, to in ((0, 64, 192), (1, 0, 128)):
                        for q in range(4):
                            o = psum[C * q:C * q + C, bank, TILE * k:TILE * k + TILE]
                            t = 4 * k + q
                            last = mm(o, wt[:, t, r, :], pl[:, t, from_:to], start=starts and k == 0 and r == 0,
                                      stop=r == 1, skip_group_check=True)
                last.then_inc(done, 1)

            def sum_squares(s_):
                pe.wait_ge(sq_done, s_ + 2 + s_ // 4)
                mm(psum[:, 6 + s_ // 4, :], group_m, squares[s_], start=s_ % 4 == 0, stop=s_ % 4 == 3
                   ).then_inc(sq_summed, 1)

            pe.wait_ge(h_act, 6 * NG - 1)
            keep_warm(WARM_OPERAND, cm["ident"])
            pe.wait_ge(w2_in, 16)
            for c in range(4):
                pe.wait_ge(l2_pos, 3 * (c + 1))
                pe.wait_ge(l2_pool, c + 1)
                pe.wait_ge(l2_neg, 4 * (c + 1))
                tiles(w2_m[:, 1024 * c:1024 * c + 1024], diag[c % 2], c, l2_done)
            for s_ in range(4):
                sum_squares(s_)
            pe.wait_ge(stat3, 1)
            mm(psum[:, 5, 0:B], group_m, delta, start=True, stop=True).then_inc(sum3, 1)
            for s_ in range(4, 8):
                if s_ == 6:
                    keep_warm(WARM_SQUARES, cm["ident"])
                sum_squares(s_)
            keep_warm(WARM_NORM, cm["ident"])

            def mix(s_, slot, bank, weights_in, y_needed, starts=True):
                pe.wait_ge(w3_in[slot], weights_in)
                pe.wait_ge(pos_ready, s_ * 3 + 3)
                pe.wait_ge(pos_pool, s_ + 1)
                pe.wait_ge(neg_ready, s_ * 4 + 4)
                if y_needed is not None:
                    pe.wait_ge(y_moved, y_needed)
                tiles(w3_m[slot], diag[slot], bank, mix_done, starts)

            for i in range(4):
                mix(i, i, i, 16, None, starts=False)
            pe.wait_ge(stat3, STAT3)
            mix(4, 0, 4, 32, None)
            with pe.Fori(1, NCHUNK // 4) as q:
                for i in range(4):
                    mix(q * 4 + (i + 1), (i + 1) % 4, i, q * 16 + (16 if i < 3 else 32), q * 4 + (i - 3))

            ys = ystage.rearrange("p (g k r q b) -> p g k r q b", g=2, k=H, r=2, q=4)
            kh = by_kh.rearrange("p (b k o) -> p b k o", b=GB, k=KW)
            kwv = by_kw.rearrange("p (x h m) -> p x h m", x=2, m=P)

            def back_transposes(j, first):
                if first:
                    src = spec[:, :].rearrange("p (g k r q b) -> p g k r q b", g=2, k=H, r=2, q=4)
                    pe.wait_ge(nyq_moved, 8)
                    pe.wait_ge(sym, 20)
                else:
                    src = ys
                    pe.wait_ge(ystaged, j + 1)
                for i_, n in enumerate(T_ORDER if first else range(8)):
                    if first and i_ == 2:
                        pe.wait_ge(y_moved, NCHUNK)
                    if not first and n % 2 == 0:
                        pe.wait_ge(b_act, j * 8 + (n - 6))
                        pe.wait_ge(b_dve, j * 8 + (n - 6))
                    b, g = n // 2, n % 2
                    for i in range(4):
                        last = nc.tensor.transpose(psum[:, n, P * i:P * i + P], src[:, g, :, :, i, b], cm["ident"])
                    last.then_inc(a_done, 1)

            def back(j, first, last_group=False):
                pe.wait_ge(a_act, j * 6 + 6)
                pe.wait_ge(a_dve, j * 2 + 2)
                for n in range(8):
                    if not first:
                        pe.wait_ge(image_done, j * 16 + (2 * n - 14))
                    for i in range(4):
                        last = mm(psum[:, n, P * i:P * i + P], kh[:, :, :, 4 * n + i], cm["ih"],
                                  start=True, stop=True)
                    last.then_inc(b_done, 1)
                if not last_group:
                    back_transposes(j + 1, False)
                pe.wait_ge(b_act, j * 8 + 8)
                pe.wait_ge(b_dve, j * 8 + 8)
                for n in range(8):
                    if not last_group:
                        if n in BY_DVE:
                            pe.wait_ge(a_dve, j * 2 + (3 + BY_DVE.index(n)))
                        else:
                            pe.wait_ge(a_act, j * 6 + (7 + BY_ACT.index(n)))
                    for i in range(2):
                        for x_ in range(2):
                            at_ = 256 * i + 128 * x_
                            last = mm(psum[:, n, at_:at_ + 128], kwv[:, x_, 2 * n + i, :], cm["iw"], start=True, stop=True)
                    last.then_inc(c_done, 1)

            back_transposes(0, True)
            back(0, True)
            with pe.Fori(1, NG - 1) as j:
                back(j, False)
            back(NG - 1, False, True)

        @block.scalar
        def _(act):
            a = nc.scalar.activation

            def deviation(d, v_, lo, n, stat_sem, need, dev_sem):
                act.wait_ge(stat_sem, need)
                a(d[:, lo:lo + n], v_[:, lo:lo + n], ACT.Sqrt, bias=eps_c).then_inc(dev_sem, 1)

            def edge_rows(j, u):
                act.wait_ge(padded_ready, j * GB + (u + 1))
                xn = padded[u % 2].rearrange("p (h w) -> p h w", w=PADW)
                en = edges[u % 2].rearrange("p (h w) -> p h w", w=PADW)
                a(en[0:C, 1:H4, :], xn[P - C:P, 0:H4 - 1, :], ACT.Copy).then_inc(edges_ready, 1)
                a(en[C:2 * C, 0:H4 - 1, :], xn[0:C, 1:H4, :], ACT.Copy).then_inc(edges_ready, 1)
                a(en[2 * C:3 * C, 1:H4, 0:PADW - 1], xn[P - C:P, 0:H4 - 1, 1:PADW], ACT.Copy).then_inc(edges_ready, 1)
                a(en[3 * C:4 * C, 0:H4 - 1, 0:PADW - 1], xn[0:C, 1:H4, 1:PADW], ACT.Copy).then_inc(edges_ready, 1)

            def to_columns(j, images_):
                for u in images_:
                    to_cols(a, j, u, slice(0, W), ACT.Identity, scale=sc1[:, u:u + 1],
                            bias=sh1[:, u:u + 1]).then_inc(columns_ready, 1)

            def conv_group(j, first, last):
                for u in range(GB):
                    if u < GB - 1:
                        edge_rows(j, u + 1)
                    elif not last:
                        deviation(rstd_in0, var0, 0, GB, stat0, (j + 1) * KGN + (EXTRA0 + steps_var(GB)), dev0)
                        edge_rows(j + 1, 0)
                    if u == 1 and not first:
                        deviation(rstd_in1, var1, 0, GB, stat1, (j - 1) * KGN + steps_var(GB), dev1)
                    if u >= 2 and not first:
                        act.wait_ge(stat1, (j - 1) * KGN + KGN)
                        to_columns(j - 1, (2 * u - 4, 2 * u - 3))

            act.wait_ge(eps_set, 1)
            a(primed, eps_c, ACT.Sqrt).then_inc(table_in, 1)
            act.wait_ge(conv_zeroed, 1)
            cv = conv_m[:, :].rearrange("p (k m) -> p k m", m=P)
            for hi in range(HM):
                lo, up = max(0, hi - 1), min(HM, hi + 2)
                act.dma_start(cv[C * hi:C * hi + C, 0:3, C * lo:C * up],
                              conv_w[:, :, C * (lo - hi + 1):C * (up - hi + 1)]).then_inc(conv_w_in, 16)
            for quad in range(4):
                taps, rows_ = slice(0, C), slice(P - C, P)
                if quad % 2 == 0:
                    taps, rows_ = slice(2 * C, 3 * C), slice(0, C)
                kx = slice(0, 3, 2) if quad < 2 else slice(1, 2)
                act.dma_start(cv[C * quad:C * quad + C, slice(3, 5 if quad < 2 else 4), rows_],
                              conv_w[:, kx, taps]).then_inc(conv_w_in, 16)
            deviation(rstd_in0, var0, 0, 1, stat0, steps_var(1), dev0)
            edge_rows(0, 0)
            deviation(rstd_in0, var0, 1, GB - 1, stat0, steps_all(1) + steps_var(GB - 1), dev0)
            conv_group(0, True, False)
            with act.Fori(1, NG - 1) as j:
                conv_group(j, False, False)
            conv_group(NG - 1, False, True)
            before = (NG - 1) * KGN
            deviation(rstd_in1, var1, 0, GB - 1, stat1, before + steps_var(GB - 1), dev1)
            act.wait_ge(stat1, before + steps_all(GB - 1))
            to_columns(NG - 1, (0, 1))
            before += steps_all(GB - 1)
            deviation(rstd_in1, var1, GB - 1, 1, stat1, before + steps_var(1), dev1)
            to_columns(NG - 1, (2,))
            act.wait_ge(stat1, before + steps_all(1))
            to_cols(a, NG - 1, GB - 1, slice(0, W // 2), ACT.Identity, scale=sc1[:, GB - 1:GB],
                    bias=sh1[:, GB - 1:GB]).then_inc(columns_ready, 1)

            def state_edges(h, w):
                act.wait_ge(state_ready[h], w + 1)
                s = state[h].rearrange("p (b h) -> p b h", h=H4)
                e = sedge[h].rearrange("p (b h) -> p b h", h=H4)
                a(e[0:C, :, 1:H4], s[P - C:P, :, 0:H4 - 1], ACT.Copy).then_inc(sedge_ready[h], 1)
                a(e[C:2 * C, :, 0:H4 - 1], s[0:C, :, 1:H4], ACT.Copy).then_inc(sedge_ready[h], 1)

            def gates(h, w):
                act.wait_ge(r_sum[h], w)
                a(gr[h], psum[:, 4 * h, 0:HB], ACT.Sigmoid, bias=bias_rz[:, 0:1]).then_inc(r_gate[h], 1)
                act.wait_ge(z_sum[h], w)
                a(gz[h], psum[:, 4 * h + 1, 0:HB], ACT.Sigmoid, bias=bias_rz[:, 1:2]).then_inc(z_gate[h], 1)

            def candidate(h, w):
                act.wait_ge(pre_ready[h], w)
                a(gn[h], pre2[h], ACT.Tanh, bias=bias_s[:, 2:3]).then_inc(n_gate[h], 1)

            act.wait_ge(bias_ready, 1)

            def scan_step(w):
                gates(0, w)
                state_edges(1, w - 1)
                candidate(0, w)
                gates(1, w)
                state_edges(0, w)
                candidate(1, w)

            state_edges(0, 0)
            scan_step(1)
            scan_step(2)
            scan_step(3)
            with act.Fori(1, W // 4) as i:
                for k in range(4):
                    scan_step(i * 4 + k)

            act.wait_ge(added[0], W)
            for i in range(2):
                to_stage(a, 0, 0, ACT.Copy, rows_=slice(8 * i, 8 * i + 8)).then_inc(staged[0], 1)
            act.wait_ge(added[1], W)

            def move_by_w(j):
                for i, n in enumerate(BY_ACT):
                    act.wait_ge(t_done, j * 8 + (n + 1))
                    a(by_w[:, 512 * n:512 * n + 512], psum[:, n, :], ACT.Copy).then_inc(t_act, 1)

            def forward(j, last_group=False):
                for k in range(6):
                    act.wait_ge(w_done, j * 6 + (k + 1))
                    for ri in range(2):
                        to_by_h(a, k, 0, ri, ACT.Copy).then_inc(w_act, 1)
                if not last_group:
                    move_by_w(j + 1)
                else:
                    a(primed, eps_c, ACT.Sqrt).then_inc(table_in, 1)
                for n in (0, 1, 2, 4, 6, 8):
                    act.wait_ge(h_done, j * 9 + (n + 1))
                    to_spectrum(a, j, n, ACT.Copy).then_inc(h_act, 1)
                    if last_group and n == 8:
                        act.wait_ge(stat2, B + 5)
                        a(rstd_in[:, 0:B], var[:, 0:B], ACT.Sqrt, bias=eps_c).then_inc(dev2, 1)

            move_by_w(0)
            act.wait_ge(t_done, 8)
            to_stage(a, 1, 1, ACT.Copy).then_inc(staged[1], 1)
            with act.Fori(0, NG - 1) as j:
                forward(j)
            forward(NG - 1, True)

            def square(s_):
                if s_ >= 6:
                    act.wait_ge(sq_summed, s_ - 1)
                buf = squares[s_]
                a(buf, chunk(s_ % 4), ACT.Square).then_inc(sq_done, 1)
                if s_ % 4 == 0:
                    act.wait_ge(sq_done, s_ + 1 + s_ // 4)
                    a(buf[0:C, 0:B], buf[0:C, 0:B], ACT.Copy, scale=0.5).then_inc(sq_done, 1)

            act.wait_ge(h_dve, 3 * NG)
            act.wait_ge(stat2, B + 8)
            for c in range(4):
                if c >= 2:
                    act.wait_ge(l2_done, c - 1)
                for m in range(HM):
                    act.wait_ge(*((l2_pos, 3 * c + m + 1) if m < 3 else (l2_pool, c + 1)))
                    negative(a, c % 2, m).then_inc(l2_neg, 1)
                square(c)
            for half in range(2):
                act.wait_ge(l2_done, 2 * half + 2)
                for m in range(HM):
                    a(low_copy(m, half), low_result(3, m, half), ACT.Copy).then_inc(l2_moved, 1)
            for half in range(2):
                act.wait_ge(l2_added, 3 + HALF_ADDED * (half + 1))
                act.wait_ge(l2_pool_added, HM * (half + 1))
                square(4 + 2 * half)
                square(5 + 2 * half)
            act.wait_ge(stat3, STAT3 - 2)
            a(rstd_in[:, 0:B], var[:, 0:B], ACT.Sqrt, bias=eps_c).then_inc(dev3, 1)

            def negatives(s_, slot):
                for m in range(HM):
                    act.wait_ge(*((pos_ready, s_ * 3 + (m + 1)) if m < 3 else (pos_pool, s_ + 1)))
                    negative(a, slot, m).then_inc(neg_ready, 1)

            def move_y(c, i, need):
                act.wait_ge(mix_done, need)
                a(chunk(c), psum[:, i, :], ACT.Copy).then_inc(y_moved, 1)

            def move_nyquist(t):
                src = psum[C * t:C * t + C, 4, :].rearrange("p (k r q b) -> p r q k b", k=4, r=2, q=4)
                dst = nyq[0:C, :].rearrange("p (r q k t b) -> p r q k t b", r=2, q=4, k=4, b=B)
                for ri in range(2):
                    a(dst[:, ri, :, :, t], src[:, ri], ACT.Copy).then_inc(nyq_moved, 1)

            def full(q, with_nyquist=False):
                for i in range(4):
                    if with_nyquist:
                        move_nyquist(i)
                    negatives(q * 4 + (i + 1), (i + 1) % 4)
                    if i == 0:
                        move_y(q * 4 - 1, 3, q * 4 + 1)
                    else:
                        move_y(q * 4 + (i - 1), i - 1, q * 4 + (i + 1))

            for i in range(4):
                negatives(i, i)
                if i > 0:
                    move_y(i - 1, i - 1, i)
            act.wait_ge(mix_done, 1)
            negatives(4, 0)
            with act.Fori(1, NCHUNK // 8 - 1) as q:
                full(q)
            full(NCHUNK // 8 - 1, with_nyquist=True)
            with act.Fori(NCHUNK // 8, NCHUNK // 4) as q:
                full(q)
            move_y(NCHUNK - 1, 3, NCHUNK + 1)
            def move_transposes(j, order):
                for i, n in enumerate(order):
                    if i in BY_ACT:
                        act.wait_ge(a_done, j * 8 + (i + 1))
                        a(by_kh[:, 512 * n:512 * n + 512], psum[:, n, :], ACT.Copy).then_inc(a_act, 1)

            def move_kh(j):
                for k in range(4):
                    act.wait_ge(b_done, j * 8 + (2 * k + 2))
                    for ri in range(2):
                        to_kw(a, k, 0, ri, ACT.Copy).then_inc(b_act, 1)

            yv = ystage.rearrange("p (n b) -> p n b", b=GB)
            sv_ = spec[:, :].rearrange("p (n b) -> p n b", b=B)
            move_transposes(0, T_ORDER)
            a(yv[:, 0:512], sv_[:, 0:512, GB:2 * GB], ACT.Copy).then_inc(ystaged, 1)
            with act.Fori(0, NG - 1) as j:
                move_kh(j)
                move_transposes(j + 1, range(8))
            move_kh(NG - 1)

        @block.vector
        def _(dve):
            v = nc.vector

            def chain(norm, lo, n, base):
                half_sem, stat_sem, sum_sem, dev_sem, bnv, mv_, gs_, sq_, var_, dev_in, bank, scale, shifted = norm
                cols = slice(lo, lo + n)
                m = mv_.rearrange("p (u k) -> p u k", k=2)[:, cols]
                g = gs_.rearrange("p (u k) -> p u k", k=2)[:, cols]
                q = sq_[:, cols]
                count = [0]

                def step(ins):
                    count[0] += 1
                    ins.then_inc(stat_sem, 1)

                def settle():
                    dve.wait_ge(stat_sem, base + count[0])

                def to_mean(halves):
                    dve.wait_ge(half_sem, halves)
                    step(v.memset(q, 0.0))
                    for u in range(lo, lo + n):
                        step(v.bn_aggr(mv_[:, 2 * u:2 * u + 2], bnv[:, 12 * u:12 * u + 12]))
                    settle()
                    step(v.tensor_tensor(q, m[:, :, 0], m[:, :, 0], ALU.mult))
                    settle()
                    step(v.tensor_tensor(m[:, :, 1], m[:, :, 1], q, ALU.add))
                    assert count[0] == steps_mean(n)

                def to_var(sums):
                    dve.wait_ge(sum_sem, sums)
                    step(v.tensor_copy(gs_[:, 2 * lo:2 * (lo + n)], psum[:, bank, 2 * lo:2 * (lo + n)]))
                    settle()
                    step(v.tensor_tensor(q, g[:, :, 0], g[:, :, 0], ALU.mult))
                    settle()
                    step(v.tensor_tensor(var_[:, cols], g[:, :, 1], q, ALU.subtract))
                    assert count[0] == steps_var(n)

                def to_scale(devs):
                    dve.wait_ge(dev_sem, devs)
                    step(v.reciprocal(scale[:, cols], dev_in[:, cols]))
                    settle()
                    step(v.scalar_tensor_tensor(out=shifted[:, cols], in0=g[:, :, 0], scalar=-1.0, in1=scale[:, cols],
                                                op0=ALU.mult, op1=ALU.mult))
                    settle()
                    assert count[0] == steps_all(n)

                return to_mean, to_var, to_scale

            norm0 = (half0, stat0, sum0, dev0, bn0, mv0, gs0, sq0, var0, rstd_in0, 7, sc0, sh0)
            norm1 = (half1, stat1, sum1, dev1, bn1, mv1, gs1, sq1, var1, rstd_in1, 6, sc1, sh1)

            def half_stats(bnv, half_sem, j, u, halves=(0, 1)):
                for k in [2 * u + half for half in halves]:
                    at_ = 6 * (k % 8)
                    v.bn_stats(bnv[:, at_:at_ + 6],
                               image[:, ds(j * (GB * ROWS) + 512 * k, 512)]).then_inc(half_sem, 1)

            def normalise(j, u, first):
                if not (first and u < 2):
                    dve.wait_ge(conv_done, j * 8 + 2 * (u - 1))
                xn = padded[u % 2].rearrange("p (h w) -> p h w", w=PADW)
                v.tensor_scalar(xn[:, :, 1:1 + W],
                                image[:, ds(j * (GB * ROWS) + u * ROWS, ROWS)].rearrange("p (h w) -> p h w", w=W),
                                sc0[:, u:u + 1], sh0[:, u:u + 1], ALU.mult, ALU.add).then_inc(padded_ready, 1)

            def add_conv(j, u, halves=(0, 1)):
                for half in halves:
                    dve.wait_ge(conv_done, j * 8 + (2 * u + half + 1))
                    part = image[:, ds(j * (GB * ROWS) + (2 * u + half) * 512, 512)]
                    v.scalar_tensor_tensor(out=part, in0=psum[:, (2 * u + half) % 4, :], scalar=bias_c[:, 0:1],
                                           in1=part, op0=ALU.add, op1=ALU.add).then_inc(conv_added, 1)

            def conv_group(j, first, last):
                before1 = chain(norm1, 0, GB, (j - 1) * KGN) if not first else None
                next0 = chain(norm0, 0, GB, (j + 1) * KGN + EXTRA0) if not last else None
                for u in range(GB):
                    if u < GB - 1:
                        normalise(j, u + 1, first)
                    elif not last:
                        next0[1](j + 3)
                    if u == 1 and not first:
                        before1[1](j)
                    if first and u == 1:
                        dve.wait_ge(conv_b_in, 16 * HM)
                    if not (first and u == 0):
                        add_conv(j, u - 1)
                        if not (first and u == 1):
                            dve.wait_ge(carried, j * GB + (u - 1))
                        dve.wait_ge(conv_added, j * 8 + 2 * u)
                        v.memset(carrier, 0.0).then_inc(carried, 1)
                        half_stats(bn1, half1, *((j - 1, GB - 1) if u == 0 else (j, u - 1)))
                    if u < GB - 1 and not last:
                        for i in ((0,), (1, 2), (3,))[u]:
                            half_stats(bn0, half0, j + 1, i)
                    if u == 0 and not first:
                        before1[0](j * 8)
                    if u == 1 and not first:
                        before1[2](j)
                    if u == 2 and not last:
                        next0[0](j * 8 + 16)
                    if u == GB - 1 and not last:
                        next0[2](j + 3)
                        normalise(j + 1, 0, False)

            v.memset(conv_m[:, :], 0.0).then_inc(conv_zeroed, 1)
            v.memset(eps_c, EPS).then_inc(eps_set, 1)
            for i in range(2):
                xn = padded[i].rearrange("p (h w) -> p h w", w=PADW)
                v.memset(xn[:, :, 0:1], 0.0).then_inc(pads_zeroed, 1)
                v.memset(xn[:, :, PADW - 1:PADW], 0.0).then_inc(pads_zeroed, 1)
                v.memset(edges[i], 0.0).then_inc(pads_zeroed, 1)
                v.memset(sedge[i], 0.0).then_inc(pads_zeroed, 1)
            dve.wait_ge(x_first[0], 16)
            half_stats(bn0, half0, 0, 0)
            one, rest = chain(norm0, 0, 1, 0), chain(norm0, 1, GB - 1, steps_all(1))
            one[0](2)
            dve.wait_ge(x_first[1], 16)
            half_stats(bn0, half0, 0, 1)
            one[1](1)
            dve.wait_ge(pads_zeroed, 8)
            one[2](1)
            normalise(0, 0, True)
            for u in range(2, GB):
                dve.wait_ge(x_first[u], 16)
                half_stats(bn0, half0, 0, u)
            rest[0](8)
            rest[1](2)
            rest[2](2)
            dve.wait_ge(x_in[1], 16)
            conv_group(0, True, False)
            for j in range(2, NG):
                dve.wait_ge(x_in[j], 16)
            with dve.Fori(1, NG - 1) as j:
                conv_group(j, False, False)
            conv_group(NG - 1, False, True)
            three, one = chain(norm1, 0, GB - 1, (NG - 1) * KGN), chain(norm1, GB - 1, 1, (NG - 1) * KGN + steps_all(GB - 1))
            three[0](8 * NG - 2)
            for half in range(2):
                add_conv(NG - 1, GB - 1, (half,))
                dve.wait_ge(conv_added, 2 * B - 1 + half)
                half_stats(bn1, half1, NG - 1, GB - 1, (half,))
            three[1](NG)
            dve.wait_ge(columns_ready, B - GB)
            three[2](NG)
            one[0](8 * NG)
            one[1](NG + 1)
            one[2](NG + 1)
            to_cols(v.tensor_scalar, NG - 1, GB - 1, slice(W // 2, W), sc1[:, GB - 1:GB], sh1[:, GB - 1:GB],
                    ALU.mult, ALU.add).then_inc(last_columns, 1)

            dve.wait_ge(small_in, 16 * 8)
            v.tensor_tensor(bias_rz, bias_s[:, 0:2], bias_s[:, 3:5], ALU.add).then_inc(bias_ready, 1)
            for h in range(2):
                if h == 1:
                    dve.wait_ge(columns_ready, B)
                v.tensor_copy(state[h], columns[:, h * HB:h * HB + HB]).then_inc(state_ready[h], 1)

            def new_state(h, w):
                dve.wait_ge(r_gate[h], w)
                v.scalar_tensor_tensor(out=pre1[h], in0=psum[:, 4 * h + 3, 0:HB], scalar=bias_s[:, 5:6], in1=gr[h],
                                       op0=ALU.add, op1=ALU.mult).then_inc(reset_done[h], 1)
                dve.wait_ge(n_sum[h], w)
                dve.wait_ge(reset_done[h], w)
                v.tensor_tensor(pre2[h], pre1[h], psum[:, 4 * h + 2, 0:HB], ALU.add).then_inc(pre_ready[h], 1)
                dve.wait_ge(z_gate[h], w)
                v.scalar_tensor_tensor(out=keep[h], in0=gz[h], scalar=1.0, in1=columns[:, ds(w * (2 * HB) + h * HB, HB)],
                                       op0=ALU.subtract, op1=ALU.mult).then_inc(keep_ready[h], 1)
                dve.wait_ge(n_gate[h], w)
                v.tensor_tensor(mix[h], gn[h], gz[h], ALU.mult).then_inc(mix_ready[h], 1)
                dve.wait_ge(mix_ready[h], w)
                dve.wait_ge(keep_ready[h], w)
                dve.wait_ge(added[h], w)
                dve.wait_ge(sedge_ready[h], w * 2)
                v.tensor_tensor(state[h], mix[h], keep[h], ALU.subtract).then_inc(state_ready[h], 1)

            with dve.Fori(0, (W - 1) // 3) as i:
                for k in range(3):
                    for h in range(2):
                        new_state(h, i * 3 + (k + 1))

            dve.wait_ge(added[0], W)
            to_stage(v.tensor_copy, 0, 1).then_inc(staged[1], 1)
            dve.wait_ge(added[1], W)

            n2 = [0]

            def step2(ins):
                n2[0] += 1
                ins.then_inc(stat2, 1)

            def settle2():
                dve.wait_ge(stat2, n2[0])

            m16 = mv.rearrange("p (b k) -> p b k", k=2)
            g16 = gs.rearrange("p (b k) -> p b k", k=2)

            def mean_of_all():
                dve.wait_ge(half2, 32)
                for b in range(B):
                    step2(v.bn_aggr(mv[:, 2 * b:2 * b + 2], bn[:, 12 * b:12 * b + 12]))
                settle2()
                step2(v.tensor_tensor(sq, m16[:, :, 0], m16[:, :, 0], ALU.mult))
                settle2()
                step2(v.tensor_tensor(m16[:, :, 1], m16[:, :, 1], sq, ALU.add))
                assert n2[0] == B + 2

            def variance_of_all():
                dve.wait_ge(sum2, 1)
                step2(v.tensor_copy(gs, psum[:, 1, 0:2 * B]))
                settle2()
                step2(v.tensor_tensor(sq, g16[:, :, 0], g16[:, :, 0], ALU.mult))
                settle2()
                step2(v.tensor_tensor(var, g16[:, :, 1], sq, ALU.subtract))
                assert n2[0] == B + 5

            def move_by_w(j):
                for n in BY_DVE:
                    dve.wait_ge(t_done, j * 8 + (n + 1))
                    v.tensor_copy(by_w[:, 512 * n:512 * n + 512], psum[:, n, :]).then_inc(t_dve, 1)

            def forward(j, last_group=False):
                for k in range(6):
                    dve.wait_ge(w_done, j * 6 + (k + 1))
                    for ri in range(2):
                        to_by_h(v.tensor_copy, k, 1, ri).then_inc(w_dve, 1)
                if not last_group:
                    move_by_w(j + 1)
                for k in range(8):
                    v.bn_stats(bn[:, ds(j * 48 + 6 * k, 6)],
                               image[:, ds(j * (GB * ROWS) + 512 * k, 512)]).then_inc(half2, 1)
                    if not last_group and k in (3, 5, 7):
                        dve.wait_ge(h_done, j * 9 + (k + 1))
                        to_spectrum(v.tensor_copy, j, k).then_inc(h_dve, 1)
                if last_group:
                    mean_of_all()
                    for n in (3, 5, 7):
                        dve.wait_ge(h_done, j * 9 + (n + 1))
                        to_spectrum(v.tensor_copy, j, n).then_inc(h_dve, 1)
                    variance_of_all()

            move_by_w(0)
            with dve.Fori(0, NG - 1) as j:
                forward(j)
            forward(NG - 1, True)

            dve.wait_ge(dev2, 1)
            step2(v.reciprocal(rstd, rstd_in))
            step2(v.tensor_scalar(shift, g16[:, :, 0], float(H * W), None, ALU.mult))
            dve.wait_ge(h_act, 6 * NG)
            dve.wait_ge(h_dve, 3 * NG)
            settle2()
            dc = spec[0:C, 0:B]
            step2(v.tensor_tensor(dc, dc, shift[0:C, :], ALU.subtract))
            settle2()
            assert n2[0] == B + 8
            dve.wait_ge(diag_zeroed, 2)
            for c in range(4):
                if c >= 2:
                    dve.wait_ge(l2_done, c - 1)
                for m in range(3):
                    positive(v.tensor_tensor, c % 2, m, chunk(c)).then_inc(l2_pos, 1)
            v.memset(delta, 0.0).then_inc(l2_added, 1)
            res = psum[:, 0:4, :].rearrange("p n (k r q b) -> p (n k) r q b", k=4, r=2, q=4)
            col0 = spec[0:C, 0:H * 4 * XT].rearrange("p (k t r b) -> p k t r b", t=4, r=2, b=B)[:, :, 0]
            o = res[0:C, :, :, 0, :]
            for half_ in range(2):
                dve.wait_ge(l2_done, 2 * half_ + 2)
                dve.wait_ge(sq_done, 2 * half_ + 3)
                if half_ == 0:
                    v.scalar_tensor_tensor(out=sq[0:C, :], in0=o[:, 0, 0, :], scalar=1.0, in1=shift[0:C, :],
                                           op0=ALU.mult, op1=ALU.add).then_inc(l2_added, 1)
                    dve.wait_ge(l2_added, 2)
                    v.tensor_tensor(dc, dc, sq[0:C, :], ALU.add).then_inc(l2_added, 1)
                    dve.wait_ge(l2_added, 3)
                    v.tensor_copy(delta[0:C, :], dc).then_inc(stat3, 1)
                lo, hi = (1, 8) if half_ == 0 else (8, MODES)
                for sign, ri, dst in ((0.5, 0, col0[:, lo:hi, 0, :]), (0.5, 1, col0[:, lo:hi, 1, :]),
                                      (0.5, 0, col0[:, H - lo:H - hi:-1, 0, :]),
                                      (-0.5, 1, col0[:, H - lo:H - hi:-1, 1, :])):
                    v.scalar_tensor_tensor(out=dst, in0=o[:, lo:hi, ri, :], scalar=sign, in1=dst,
                                           op0=ALU.mult, op1=ALU.add).then_inc(l2_added, 1)
                for t in range(3):
                    for m in range(HM):
                        if (t, m) != (0, 0):
                            add_low(v.tensor_tensor, t, m, half_).then_inc(l2_added, 1)
            n3 = [1]

            def step3(ins):
                n3[0] += 1
                ins.then_inc(stat3, 1)

            def settle3():
                dve.wait_ge(stat3, n3[0])

            dve.wait_ge(sq_summed, 4)
            step3(v.tensor_reduce(energy, psum[:, 6, :].rearrange("p (n b) -> p b n", b=B),
                                  mybir.AxisListType.X, ALU.add))
            dve.wait_ge(sum3, 1)
            step3(v.tensor_scalar(mean, psum[:, 5, 0:B], 8.0 / (2 * H * W), None, ALU.mult))
            settle3()
            step3(v.scalar_tensor_tensor(out=energy, in0=energy, scalar=-ENERGY, in1=var, op0=ALU.mult, op1=ALU.add))
            step3(v.tensor_tensor(sq, mean, mean, ALU.mult))
            settle3()
            step3(v.tensor_tensor(energy, energy, sq, ALU.subtract))
            settle3()
            dve.wait_ge(sq_summed, 8)
            step3(v.tensor_reduce(sq, psum[:, 7, :].rearrange("p (n b) -> p b n", b=B),
                                  mybir.AxisListType.X, ALU.add))
            settle3()
            step3(v.scalar_tensor_tensor(out=var, in0=sq, scalar=ENERGY, in1=energy, op0=ALU.mult, op1=ALU.add))
            assert n3[0] == STAT3 - 2
            step3(v.scalar_tensor_tensor(out=dc, in0=mean[0:C, :], scalar=-float(H * W), in1=dc,
                                         op0=ALU.mult, op1=ALU.add))
            dve.wait_ge(dev3, 1)
            step3(v.reciprocal(rstd, rstd_in))
            settle3()

            def positives(s_, slot, columns_, need):
                if need is not None:
                    dve.wait_ge(mix_done, need)
                for m in range(3):
                    positive(v.tensor_tensor, slot, m, columns_).then_inc(pos_ready, 1)

            def full(q):
                for i in range(4):
                    positives(None, (i + 1) % 4, chunk(q * 4 + i), q * 4 + (i - 2))

            def symmetrise(ri, half_b, before):
                part = slice(half_b * (B // 2), (half_b + 1) * (B // 2))
                y0 = spec[0:C, 0:H * 4 * XT].rearrange("p (k r q b) -> p k r q b", r=2, q=4, b=B)[:, :, ri, 0, part]
                n32 = nyq[0:C, :].rearrange("p (r k b) -> p r k b", r=2, b=B)[:, 1 - ri, :, part]
                ts = t_sum[0:C, :].rearrange("p (k b) -> p k b", b=B // 2)
                back_ = slice(H - 1, 0, -1)
                mirror = ALU.add if ri == 0 else ALU.subtract
                v.tensor_tensor(ts[:, 1:H], y0[:, 1:H], y0[:, back_], mirror).then_inc(sym, 1)
                v.tensor_tensor(ts[:, 0:1], y0[:, 0:1], y0[:, 0:1], mirror).then_inc(sym, 1)
                dve.wait_ge(sym, before + 2)
                v.tensor_tensor(ts, ts, n32, ALU.subtract if ri == 0 else ALU.add).then_inc(sym, 1)
                dve.wait_ge(sym, before + 3)
                v.tensor_tensor(y0[:, 1:H], ts[:, 1:H], n32[:, back_], ALU.add).then_inc(sym, 1)
                v.tensor_tensor(y0[:, 0:1], ts[:, 0:1], n32[:, 0:1], ALU.add).then_inc(sym, 1)
                dve.wait_ge(sym, before + 5)

            dve.wait_ge(diag_zeroed, 4)
            for i in range(4):
                positives(i, i, chunk(i), None)
            positives(4, 0, spec9, 1)
            with dve.Fori(1, NCHUNK // 8 + 1) as q:
                full(q)
            dve.wait_ge(nyq_moved, 8)
            dve.wait_ge(y_moved, NCHUNK // 2)
            for i in range(4):
                symmetrise(i // 2, i % 2, 5 * i)
                if i < 3:
                    full(NCHUNK // 8 + 1 + i)
            def move_transposes(j, order):
                for i, n in enumerate(order):
                    if i in BY_DVE:
                        dve.wait_ge(a_done, j * 8 + (i + 1))
                        v.tensor_copy(by_kh[:, 512 * n:512 * n + 512], psum[:, n, :]).then_inc(a_dve, 1)

            def move_kh(j):
                for k in range(4):
                    dve.wait_ge(b_done, j * 8 + (2 * k + 2))
                    for ri in range(2):
                        to_kw(v.tensor_copy, k, 1, ri).then_inc(b_dve, 1)

            def add_result(j):
                for n in range(8):
                    dve.wait_ge(c_done, j * 8 + (n + 1))
                    for i in range(2):
                        part = images(j).rearrange("p (b h w) -> p h b w", b=GB, w=W)[:, 2 * n + i]
                        res = psum[:, n, 256 * i:256 * i + 256].rearrange("p (b w) -> p b w", b=GB)
                        v.scalar_tensor_tensor(out=part, in0=res, scalar=bias_o[:, 0:1], in1=part,
                                               op0=ALU.add, op1=ALU.add).then_inc(image_done, 1)

            yv = ystage.rearrange("p (n b) -> p n b", b=GB)
            sv_ = spec[:, :].rearrange("p (n b) -> p n b", b=B)
            move_transposes(0, T_ORDER)
            dve.wait_ge(y_moved, NCHUNK)
            v.tensor_copy(yv[:, 512:1024], sv_[:, 512:1024, GB:2 * GB]).then_inc(ystaged, 1)
            with dve.Fori(0, NG - 1) as j:
                move_kh(j)
                move_transposes(j + 1, range(8))
                add_result(j)
            move_kh(NG - 1)
            add_result(NG - 1)



def kernel(x, L0_conv_weight, L0_conv_bias, L1_conv_weight_ih, L1_conv_bias_ih, L1_conv_weight_hh,
           L1_conv_bias_hh, L2_conv_w_real, L2_conv_w_imag, L3_conv_kernel_re, L3_conv_kernel_im, L3_conv_bias):
    import concourse.bacc as bacc
    from concourse.bass_utils import run_bass_kernel_spmd

    def rows(a, n=P):
        return np.ascontiguousarray(a).reshape(n, -1)

    x_l = rows(np.asarray(x).reshape(B, C, H4, HM, W).transpose(3, 1, 0, 2, 4))
    conv_w = np.ascontiguousarray(np.asarray(L0_conv_weight)[:, :, ::-1].transpose(1, 3, 2, 0)).reshape(C, 3, 3 * C)
    wi = np.ascontiguousarray(np.asarray(L1_conv_weight_ih).reshape(3, C, 3, C)[:, :, ::-1].transpose(3, 0, 2, 1)).reshape(C, 3, 3 * C)
    wh = np.ascontiguousarray(np.asarray(L1_conv_weight_hh).reshape(3, C, C).transpose(2, 0, 1))
    sb_ = np.ascontiguousarray(np.concatenate([np.asarray(L1_conv_bias_ih).reshape(3, C),
                                               np.asarray(L1_conv_bias_hh).reshape(3, C)]).T)
    w2 = np.stack([np.asarray(L2_conv_w_real), np.asarray(L2_conv_w_imag)])
    w2 = rows(w2.reshape(2, C, C, MODES, 4, 4).transpose(5, 1, 3, 4, 0, 2))
    k = np.stack([np.asarray(L3_conv_kernel_re), np.asarray(L3_conv_kernel_im)])
    w3 = rows(k[..., :KW].reshape(2, C, C, H, 2, 4, 4).transpose(6, 2, 4, 3, 5, 0, 1))
    w9 = rows(k[..., KW].reshape(2, C, C, 4, 16).transpose(3, 2, 4, 0, 1))
    group, parts = constants()
    const = np.ascontiguousarray(np.concatenate([parts[n] for n in (*KEPT_COLS, *FORWARD_COLS)], 1))
    arrays = dict(x=x_l, conv_w=conv_w, conv_b=np.asarray(L0_conv_bias).reshape(C, 1), scan_wi=wi, scan_wh=wh,
                  scan_b=sb_, w2=w2, w3=w3, w9=w9, out_b=np.asarray(L3_conv_bias).reshape(C, 1),
                  group=group, const=const)
    nc = bacc.Bacc("TRN2", target_bir_lowering=False, num_devices=1)
    args = [nc.dram_tensor(f"{n}_dram", a.shape, F32, kind="ExternalInput").ap() for n, a in arrays.items()]
    args.append(nc.dram_tensor("out_dram", [P, B * ROWS], F32, kind="ExternalOutput").ap())
    program(nc, *args)
    r = run_bass_kernel_spmd(nc, [{f"{n}_dram": a for n, a in arrays.items()}], core_ids=[0])
    y = r.results[0]["out_dram"].reshape(HM, C, B, H4, W)
    return np.ascontiguousarray(y.transpose(2, 1, 3, 0, 4)).reshape(B, C, H, W)
```
